# Optimizing a Trainium2 kernel written in Bass

```python
import numpy as np
import jax
import jax.numpy as jnp

def _softmax(x, axis=-1):
    return jax.nn.softmax(x, axis=axis)

def _gelu(x):
    return jax.nn.gelu(x, approximate=True)

def _silu(x):
    return jax.nn.silu(x)

def _sigmoid(x):
    return jax.nn.sigmoid(x)

def _layernorm(x, axis=-1, eps=1e-05):
    m = jnp.mean(x, axis=axis, keepdims=True)
    v = jnp.var(x, axis=axis, keepdims=True)
    return (x - m) / jnp.sqrt(v + eps)

def _scatter_add(tgt, idx, src, axis=0):
    return tgt.at[idx].add(src)

def _segment_sum(src, seg, n):
    return jax.ops.segment_sum(src, seg, n)
kernel_name = 'mk_macaron_d1_jaxref_r4_be4fd2'

def setup_inputs(seed: int=0):
    np.random.seed(seed)
    _w = jnp.asarray

    def _L0_attn_setup():
        import jax, jax.numpy as jnp
        import numpy as np
        from jax.scipy.linalg import solve_triangular
        HID = 256
        H = 4
        D = HID // H
        P = H * D
        KW = 4
        C = 64
        EPS = 1e-05

        def _dwconv_silu(x, w):
            y = jax.lax.conv_general_dilated(x.transpose(0, 2, 1), w, window_strides=(1,), padding=[(KW - 1, 0)], feature_group_count=P, dimension_numbers=('NCH', 'OIH', 'NCH'))
            return jax.nn.silu(y).transpose(0, 2, 1)

        def _forward(x, Wq, Wk, Wv, Wb, conv_q_w, conv_k_w, conv_v_w, rms_w, Wo):
            B, L, _ = x.shape
            nc = L // C
            dt = x.dtype
            q = _dwconv_silu(x @ Wq, conv_q_w).reshape(B, L, H, D)
            k = _dwconv_silu(x @ Wk, conv_k_w).reshape(B, L, H, D)
            v = _dwconv_silu(x @ Wv, conv_v_w).reshape(B, L, H, D)
            q = q / jnp.linalg.norm(q, axis=-1, keepdims=True)
            k = k / jnp.linalg.norm(k, axis=-1, keepdims=True)
            beta = jax.nn.sigmoid(x @ Wb)

            def to_chunks(t):
                return t.transpose(0, 2, 1, 3).reshape(B, H, nc, C, D).transpose(2, 0, 1, 3, 4)
            Qc = to_chunks(q) * D ** (-0.5)
            Kc = to_chunks(k)
            Vc = to_chunks(v)
            Bc = beta.transpose(0, 2, 1).reshape(B, H, nc, C, 1).transpose(2, 0, 1, 3, 4)
            I32 = jnp.eye(C, dtype=jnp.float32)
            M = jnp.tril(jnp.ones((C, C), dt))

            def step(S, ch):
                Q, K, V, bt = ch
                Kb = K * bt
                Vb = V * bt
                A = jnp.eye(C, dtype=dt) + jnp.tril(jnp.einsum('bhcd,bhed->bhce', Kb, K), -1)
                T = solve_triangular(A.astype(jnp.float32), jnp.broadcast_to(I32, A.shape), lower=True).astype(dt)
                W = T @ Kb
                U = T @ Vb
                St = S.swapaxes(-1, -2)
                mid = U - W @ St
                O = Q @ St + jnp.einsum('bhcd,bhed->bhce', Q, K) * M @ mid
                S_new = S + mid.swapaxes(-1, -2) @ K
                return (S_new, O)
            S0 = jnp.zeros((B, H, D, D), dt)
            S, Os = jax.lax.scan(step, S0, (Qc, Kc, Vc, Bc))
            o = Os.transpose(1, 0, 3, 2, 4).reshape(B, L, H, D)
            o = o * jax.lax.rsqrt(jnp.mean(o * o, axis=-1, keepdims=True) + EPS) * rms_w
            o = o.reshape(B, L, P) @ Wo
            return (o, S)

        def _reference_tuple_inner(x, Wq, Wk, Wv, Wb, conv_q_w, conv_k_w, conv_v_w, rms_w, Wo):
            return _forward(x, Wq, Wk, Wv, Wb, conv_q_w, conv_k_w, conv_v_w, rms_w, Wo)
        key = jax.random.key(seed)
        ks = jax.random.split(key, 10)
        B, L = (4, 1024)
        f32 = jnp.float32
        return {'x': jax.random.normal(ks[0], (B, L, HID), f32), 'Wq': jax.random.normal(ks[1], (HID, P), f32) * 0.02, 'Wk': jax.random.normal(ks[2], (HID, P), f32) * 0.02, 'Wv': jax.random.normal(ks[3], (HID, P), f32) * 0.02, 'Wb': jax.random.normal(ks[4], (HID, H), f32) * 0.02, 'conv_q_w': jax.random.normal(ks[5], (P, 1, KW), f32) * 0.2, 'conv_k_w': jax.random.normal(ks[6], (P, 1, KW), f32) * 0.2, 'conv_v_w': jax.random.normal(ks[7], (P, 1, KW), f32) * 0.2, 'rms_w': jnp.ones((D,), f32), 'Wo': jax.random.normal(ks[8], (P, HID), f32) * 0.02}
    _L0_attn_in = _L0_attn_setup()

    def _L0_ffn_setup():
        import jax, jax.numpy as jnp
        import numpy as np
        TOP_K = 2
        key = jax.random.key(seed)
        k_x, k_g, k_w1, k_w2, k_w3 = jax.random.split(key, 5)
        B, S, D, H, E = (2, 128, 256, 128, 8)
        x = jax.random.normal(k_x, (B, S, D), dtype=jnp.float32)
        gate_w = jax.random.normal(k_g, (D, E), dtype=jnp.float32) * D ** (-0.5)
        w1 = jax.random.normal(k_w1, (E, D, H), dtype=jnp.float32) * 0.02
        w2 = jax.random.normal(k_w2, (E, H, D), dtype=jnp.float32) * 0.02
        w3 = jax.random.normal(k_w3, (E, D, H), dtype=jnp.float32) * 0.02
        return {'x': x, 'gate_w': gate_w, 'w1': w1, 'w2': w2, 'w3': w3}
    _L0_ffn_in = _L0_ffn_setup()
    _d = {'L0_attn_x': _L0_attn_in['x'], 'L0_attn_Wq': _L0_attn_in['Wq'], 'L0_attn_Wk': _L0_attn_in['Wk'], 'L0_attn_Wv': _L0_attn_in['Wv'], 'L0_attn_Wb': _L0_attn_in['Wb'], 'L0_attn_conv_q_w': _L0_attn_in['conv_q_w'], 'L0_attn_conv_k_w': _L0_attn_in['conv_k_w'], 'L0_attn_conv_v_w': _L0_attn_in['conv_v_w'], 'L0_attn_rms_w': _L0_attn_in['rms_w'], 'L0_attn_Wo': _L0_attn_in['Wo'], 'L0_ffn_gate_w': _L0_ffn_in['gate_w'], 'L0_ffn_w1': _L0_ffn_in['w1'], 'L0_ffn_w2': _L0_ffn_in['w2'], 'L0_ffn_w3': _L0_ffn_in['w3']}
    _x0 = _d['L0_attn_x']
    _d['L0_attn_x'] = jax.random.normal(jax.random.fold_in(jax.random.key(seed), 1), (2, 4096, 256), dtype=_x0.dtype)
    del _x0
    return _d

def reference(L0_attn_x, L0_attn_Wq, L0_attn_Wk, L0_attn_Wv, L0_attn_Wb, L0_attn_conv_q_w, L0_attn_conv_k_w, L0_attn_conv_v_w, L0_attn_rms_w, L0_attn_Wo, L0_ffn_gate_w, L0_ffn_w1, L0_ffn_w2, L0_ffn_w3):

    def _L0_attn_ref(x, Wq, Wk, Wv, Wb, conv_q_w, conv_k_w, conv_v_w, rms_w, Wo):
        import jax, jax.numpy as jnp
        import numpy as np
        from jax.scipy.linalg import solve_triangular
        HID = 256
        H = 4
        D = HID // H
        P = H * D
        KW = 4
        C = 64
        EPS = 1e-05

        def _dwconv_silu(x, w):
            y = jax.lax.conv_general_dilated(x.transpose(0, 2, 1), w, window_strides=(1,), padding=[(KW - 1, 0)], feature_group_count=P, dimension_numbers=('NCH', 'OIH', 'NCH'))
            return jax.nn.silu(y).transpose(0, 2, 1)

        def _forward(x, Wq, Wk, Wv, Wb, conv_q_w, conv_k_w, conv_v_w, rms_w, Wo):
            B, L, _ = x.shape
            nc = L // C
            dt = x.dtype
            q = _dwconv_silu(x @ Wq, conv_q_w).reshape(B, L, H, D)
            k = _dwconv_silu(x @ Wk, conv_k_w).reshape(B, L, H, D)
            v = _dwconv_silu(x @ Wv, conv_v_w).reshape(B, L, H, D)
            q = q / jnp.linalg.norm(q, axis=-1, keepdims=True)
            k = k / jnp.linalg.norm(k, axis=-1, keepdims=True)
            beta = jax.nn.sigmoid(x @ Wb)

            def to_chunks(t):
                return t.transpose(0, 2, 1, 3).reshape(B, H, nc, C, D).transpose(2, 0, 1, 3, 4)
            Qc = to_chunks(q) * D ** (-0.5)
            Kc = to_chunks(k)
            Vc = to_chunks(v)
            Bc = beta.transpose(0, 2, 1).reshape(B, H, nc, C, 1).transpose(2, 0, 1, 3, 4)
            I32 = jnp.eye(C, dtype=jnp.float32)
            M = jnp.tril(jnp.ones((C, C), dt))

            def step(S, ch):
                Q, K, V, bt = ch
                Kb = K * bt
                Vb = V * bt
                A = jnp.eye(C, dtype=dt) + jnp.tril(jnp.einsum('bhcd,bhed->bhce', Kb, K), -1)
                T = solve_triangular(A.astype(jnp.float32), jnp.broadcast_to(I32, A.shape), lower=True).astype(dt)
                W = T @ Kb
                U = T @ Vb
                St = S.swapaxes(-1, -2)
                mid = U - W @ St
                O = Q @ St + jnp.einsum('bhcd,bhed->bhce', Q, K) * M @ mid
                S_new = S + mid.swapaxes(-1, -2) @ K
                return (S_new, O)
            S0 = jnp.zeros((B, H, D, D), dt)
            S, Os = jax.lax.scan(step, S0, (Qc, Kc, Vc, Bc))
            o = Os.transpose(1, 0, 3, 2, 4).reshape(B, L, H, D)
            o = o * jax.lax.rsqrt(jnp.mean(o * o, axis=-1, keepdims=True) + EPS) * rms_w
            o = o.reshape(B, L, P) @ Wo
            return (o, S)

        def _reference_tuple_inner(x, Wq, Wk, Wv, Wb, conv_q_w, conv_k_w, conv_v_w, rms_w, Wo):
            return _forward(x, Wq, Wk, Wv, Wb, conv_q_w, conv_k_w, conv_v_w, rms_w, Wo)
        return _reference_tuple_inner(x, Wq, Wk, Wv, Wb, conv_q_w, conv_k_w, conv_v_w, rms_w, Wo)[0]

    def _L0_ffn_ref(x, gate_w, w1, w2, w3):
        import jax, jax.numpy as jnp
        import numpy as np
        TOP_K = 2
        B, S, D = x.shape
        E = gate_w.shape[1]
        xf = x.reshape(B * S, D)
        T = B * S
        logits = xf @ gate_w
        scores = jax.nn.softmax(logits, axis=-1)
        top_scores, top_idx = jax.lax.top_k(scores, TOP_K)
        scale = jnp.zeros((T, E), dtype=x.dtype).at[jnp.arange(T)[:, None], top_idx].set(top_scores)
        xs = scale.T[:, :, None] * xf[None, :, :]
        h = jax.nn.silu(jnp.einsum('etd,edh->eth', xs, w1)) * jnp.einsum('etd,edh->eth', xs, w3)
        y = jnp.einsum('eth,ehd->etd', h, w2)
        out = y.sum(axis=0)
        return out.reshape(B, S, D)
    x = L0_attn_x
    x = x + 0.5 * _L0_ffn_ref(_layernorm(x, axis=-1), L0_ffn_gate_w, L0_ffn_w1, L0_ffn_w2, L0_ffn_w3)
    x = x + _L0_attn_ref(_layernorm(x, axis=-1), L0_attn_Wq, L0_attn_Wk, L0_attn_Wv, L0_attn_Wb, L0_attn_conv_q_w, L0_attn_conv_k_w, L0_attn_conv_v_w, L0_attn_rms_w, L0_attn_Wo)
    x = x + 0.5 * _L0_ffn_ref(_layernorm(x, axis=-1), L0_ffn_gate_w, L0_ffn_w1, L0_ffn_w2, L0_ffn_w3)
    return x

_drawn_inputs = setup_inputs


def setup_inputs(seed=0):
    import zlib

    import numpy as np

    out = dict(_drawn_inputs(seed))
    spreads = {'L0_attn_rms_w': (1.0, 0.2)}
    factors = {'L0_ffn_gate_w': 8.0, 'L0_ffn_w1': 8.0, 'L0_ffn_w2': 8.0, 'L0_ffn_w3': 8.0}
    for name, (base, spread) in spreads.items():
        noise = np.random.default_rng([zlib.crc32(name.encode()), seed]).standard_normal(out[name].shape)
        drawn = base * np.exp(spread * noise) if base else spread * noise
        out[name] = jnp.asarray(drawn.astype(out[name].dtype))
    for name, factor in factors.items():
        out[name] = (out[name] * factor).astype(out[name].dtype)
    return out
```

```python
from contextlib import ExitStack

import concourse.bass as bass
from concourse import mybir

P = 128
B, L, DM = 2, 4096, 256
NT = B * L // P
KC = DM // P
E, HF = 8, 128
TPB = 4
TB = TPB * P
NB = NT // TPB
EPS = 1e-5
F32 = mybir.dt.float32
F32R = mybir.dt.float32r
ALU = mybir.AluOpType
ACT = mybir.ActivationFunctionType
AX = mybir.AxisListType


def wait(eng, sem, value):
    if not (isinstance(value, int) and value <= 0):
        eng.wait_ge(sem, value)


def pass_by(eng, passed):
    eng.sem_inc(passed, 1)


def blocks_of(eng, body, count):
    body(0, 0, 0)
    body(0, 1, 1)
    with eng.Fori(1, count // 2 - 1) as i:
        body(i, 0, None)
        body(i, 1, None)
    body(count // 2 - 1, 0, count - 2)
    body(count // 2 - 1, 1, count - 1)


def ffn(nc, name, src, dst, s_dram, gate_w, w1, w2, w3):
    ctx = ExitStack()
    with ctx:
        def sb(n, shape, dt=F32):
            return ctx.enter_context(nc.sbuf_tensor(f"{name}_{n}", shape, dt))

        def sem(n):
            return ctx.enter_context(nc.semaphore(f"{name}_{n}"))

        w1s = sb("w1s", [P, 2, KC, E, HF], F32R)
        w3s = sb("w3s", [P, 2, KC, E, HF], F32R)
        w2s = sb("w2s", [P, 2, E, DM], F32R)
        gws = sb("gws", [P, 2, KC, E], F32R)
        stage = sb("stage", [P, 2, E * DM])
        gstage = sb("gstage", [P, KC, E])
        ident = sb("ident", [P, P])
        eps_t = sb("eps_t", [P, 1])
        mhalf = sb("mhalf", [P, TPB])
        xin = sb("xin", [P, 2, TPB, DM])
        stats = sb("stats", [P, TPB, 6])
        mv = sb("mv", [P, TPB, 2])
        var_eps = sb("var_eps", [P, TPB])
        rstd = sb("rstd", [P, TPB])
        xn = sb("xn", [P, TPB, DM])
        xhi = sb("xhi", [P, 2, KC, TB], F32R)
        xlo = sb("xlo", [P, 2, KC, TB], F32R)
        lgT = sb("lgT", [E, TB])
        lmax = sb("lmax", [P, TPB])
        lsub = sb("lsub", [P, TPB, E])
        lexp = sb("lexp", [P, TPB, E])
        lsum = sb("lsum", [P, TPB])
        linv = sb("linv", [P, TPB])
        score = sb("score", [P, TPB, 2 * E])
        top = sb("top", [P, TPB, 8])
        rest = sb("rest", [P, TPB, 2 * E])
        scale = sb("scale", [P, TPB, E])
        scT = sb("scT", [E, TB])
        scB = sb("scB", [P, 2, E, TB])
        ts = sb("ts", [P, 2, 2, TB])
        sil = sb("sil", [P, 2, TB])
        hid = sb("hid", [P, 2, TB])
        hhi = sb("hhi", [P, 4, TB], F32R)
        hlo = sb("hlo", [P, 4, TB], F32R)
        xres = sb("xres", [P, TPB, DM])

        def pt(n, shape):
            return ctx.enter_context(nc.psum_tensor(f"{name}_{n}", shape, F32))

        up = pt("up", [P, 2, 2, TB])
        yb = pt("yb", [P, TPB, DM])
        tr = pt("tr", [P, KC, TB])

        s_w = [sem(f"w_loaded{j}") for j in range(2)]
        w_hi = sem("w_hi")
        w_lo = sem("w_lo")
        consts = sem("consts")
        passed = sem("passed")
        id_set = sem("id_set")
        x_loaded = [sem(f"x_loaded{j}") for j in range(2)]
        res_loaded = sem("res_loaded")
        stats_ready = sem("stats_ready")
        stats_part = sem("stats_part")
        rstd_part = sem("rstd_part")
        rstd_ready = sem("rstd_ready")
        xn_ready = sem("xn_ready")
        xT_done = sem("xT_done")
        xhi_ready = sem("xhi_ready")
        xlo_ready = sem("xlo_ready")
        lgT_done = sem("lgT_done")
        lgT_copied = sem("lgT_copied")
        lg_done = sem("lg_done")
        lsub_ready = sem("lsub_ready")
        lexp_ready = sem("lexp_ready")
        chain = sem("route_chain")
        scale_ready = sem("scale_ready")
        scT_done = sem("scT_done")
        scT_copied = sem("scT_copied")
        sc_stored = sem("sc_stored")
        scB_loaded = [sem(f"scB_loaded{j}") for j in range(2)]
        up_done = sem("up_done")
        ts_ready = sem("ts_ready")
        sil_ready = sem("sil_ready")
        hid_ready = sem("hid_ready")
        hhi_ready = sem("hhi_ready")
        hlo_ready = sem("hlo_ready")
        down_done = sem("down_done")
        y_read = sem("y_read")
        stored = sem("stored")
        CH = 7

        block = ctx.enter_context(nc.Block())
        x_v = src.rearrange("(n j p) d -> n p j d", j=TPB, p=P)
        o_v = dst.rearrange("(n j p) d -> n p j d", j=TPB, p=P)
        sets = [(w1.rearrange("e (c p) h -> p c e h", p=P), w1s),
                (w3.rearrange("e (c p) h -> p c e h", p=P), w3s),
                (w2.rearrange("e h d -> h e d"), w2s)]

        def flat(w, part):
            a = w[:, part]
            return a.rearrange("p c e h -> p (c e h)") if len(a.shape) == 4 else a.rearrange("p e d -> p (e d)")

        @block.sync
        def _(sp):
            def load_x(m, i, c):
                wait(sp, xn_ready, m - 1)
                sp.dma_start(xin[:, c % 2], x_v[m]).then_inc(x_loaded[c % 2], 16)

            def load_res(n):
                wait(sp, stored, 16 * n)
                sp.dma_start(xres[:], x_v[n]).then_inc(res_loaded, 16)

            def store(n):
                sp.wait_ge(y_read, n + 1)
                sp.dma_start(o_v[n], xres[:]).then_inc(stored, 16)

            def spread(m, c):
                sp.wait_ge(scT_copied, m + 1)
                sp.dma_start(s_dram, scT[:]).then_inc(sc_stored, 16)
                sp.wait_ge(sc_stored, 16 * (m + 1))
                pass_by(sp, passed)
                wait(sp, ts_ready, E * (m - 1))
                for h in range(2):
                    sp.dma_start(scB[:, c % 2, 4 * h:4 * h + 4], s_dram[4 * h:4 * h + 4].partition_broadcast(P))\
                      .then_inc(scB_loaded[h], 16)

            sp.dma_start(gstage[:], gate_w.rearrange("(c p) e -> p c e", p=P)).then_inc(s_w[0], 16)
            load_x(0, 0, 0)
            load_x(1, 0, 1)
            for k, (w, _) in enumerate(sets):
                if k == 2:
                    sp.wait_ge(w_lo, 2)
                o = stage[:, k % 2].rearrange("p (c e h) -> p c e h", c=KC, e=E) if k < 2 else \
                    stage[:, 0].rearrange("p (e d) -> p e d", e=E)
                if k < 2:
                    for q in range(KC):
                        sp.dma_start(o[:, q], w[:, q]).then_inc(s_w[1], 16)
                        sp.wait_ge(s_w[1], 16 * (2 * k + q + 1))
                else:
                    sp.dma_start(o, w).then_inc(s_w[1], 16)
            load_res(0)
            spread(0, 0)

            def body(i, c, n):
                n = 2 * i + c if n is None else n
                if not (isinstance(n, int) and n == 0):
                    store(n - 1)
                    load_res(n)
                if not (isinstance(n, int) and n + 2 >= NB):
                    load_x(n + 2, i, c + 2)
                if not (isinstance(n, int) and n + 1 >= NB):
                    spread(n + 1, c + 1)

            blocks_of(sp, body, NB)
            store(NB - 1)
            sp.wait_ge(stored, 16 * NB)

        @block.tensor
        def _(pe):
            TERMS = [(0, 0), (0, 1), (1, 0)]

            def transposes(m):
                pe.wait_ge(xn_ready, m + 1)
                wait(pe, scT_copied, m)
                for j in range(TPB):
                    for q in range(KC):
                        last = pe.transpose(tr[:, q, j * P:(j + 1) * P], xn[:, j, q * P:(q + 1) * P], ident[:])
                last.then_inc(xT_done, 1)

            def logits(m, c):
                pe.wait_ge(xhi_ready, m + 1)
                pe.wait_ge(xlo_ready, m + 1)
                for k, (a, b) in enumerate(TERMS):
                    for q in range(KC):
                        last = pe.matmul(tr[0:E, 0, :], gws[:, a, q, :], (xhi, xlo)[b][:, c % 2, q, :],
                                         start=(k == 0 and q == 0), stop=(k == 2 and q == KC - 1))
                last.then_inc(lgT_done, 1)

            def logits_back(m):
                pe.wait_ge(lgT_copied, m + 1)
                pass_by(pe, passed)
                for j in range(TPB):
                    last = pe.transpose(tr[:, 1, j * E:(j + 1) * E], lgT[:, j * P:(j + 1) * P], ident[0:E, 0:E])
                last.then_inc(lg_done, 1)

            def scales_up(m):
                pe.wait_ge(scale_ready, m + 1)
                for j in range(TPB):
                    last = pe.transpose(tr[0:E, 0, j * P:(j + 1) * P], scale[:, j, :], ident[:])
                last.then_inc(scT_done, 1)

            def expert_up(n, c, k):
                g = E * n + k
                if k == 0:
                    pe.wait_ge(xhi_ready, n + 1)
                    pe.wait_ge(xlo_ready, n + 1)
                wait(pe, ts_ready, g - 1)
                for o, w in enumerate((w1s, w3s)):
                    for t, (a, b) in enumerate(TERMS):
                        for q in range(KC):
                            last = pe.matmul(up[:, k % 2, o, :], w[:, a, q, k, :], (xhi, xlo)[b][:, c % 2, q, :],
                                             start=(t == 0 and q == 0), stop=(t == 2 and q == KC - 1))
                last.then_inc(up_done, 1)

            def expert_down(n, k):
                g = E * n + k
                pe.wait_ge(hhi_ready, g + 1)
                pe.wait_ge(hlo_ready, g + 1)
                if k == 0:
                    wait(pe, y_read, n)
                for j in range(TPB):
                    for t, (a, b) in enumerate(TERMS):
                        last = pe.matmul(yb[:, j, :], (hhi, hlo)[b][:, k % 4, j * P:(j + 1) * P], w2s[:, a, k, :],
                                         start=(k == 0 and t == 0 and j % 2 == 0),
                                         stop=(k == E - 1 and t == 2), skip_group_check=True)
                last.then_inc(down_done, 1)

            pe.wait_ge(consts, 1)
            pe.wait_ge(id_set, 2)
            transposes(0)
            pe.wait_ge(w_hi, 1)
            pe.wait_ge(w_lo, 1)
            logits(0, 0)
            logits_back(0)
            scales_up(0)
            pe.wait_ge(w_hi, 4)
            pe.wait_ge(w_lo, 4)

            def body(i, c, n):
                n = 2 * i + c if n is None else n
                first, last = isinstance(n, int) and n == 0, isinstance(n, int) and n + 1 >= NB
                for k in range(E):
                    expert_up(n, c, k)
                    if k >= 2:
                        expert_down(n, k - 2)
                    elif not first:
                        expert_down(n - 1, E + k - 2)
                    if not last:
                        if k == 0:
                            transposes(n + 1)
                        if k == 1:
                            logits(n + 1, c + 1)
                        if k == 2:
                            logits_back(n + 1)
                        if k == 4:
                            scales_up(n + 1)

            blocks_of(pe, body, NB)
            expert_down(NB - 1, E - 2)
            expert_down(NB - 1, E - 1)

        @block.vector
        def _(dve):
            def ln_stats(m, c, i):
                dve.wait_ge(x_loaded[c % 2], 16 * (i + c // 2 + 1))
                wait(dve, rstd_ready, m)
                wait(dve, xn_ready, m)
                for j in range(TPB):
                    dve.bn_stats(stats[:, j, :], xin[:, c % 2, j, :]).then_inc(stats_part, 1)
                dve.wait_ge(stats_part, TPB * (m + 1))
                pass_by(dve, passed)
                for j in range(TPB):
                    last = dve.bn_aggr(mv[:, j, :], stats[:, j, :])
                last.then_inc(stats_ready, 1)

            def normalize(m, c):
                dve.wait_ge(rstd_ready, m + 1)
                wait(dve, xT_done, m)
                for j in range(TPB):
                    last = dve.tensor_scalar(xn[:, j, :], xin[:, c % 2, j, :], mv[:, j, 0:1], rstd[:, j:j + 1],
                                             ALU.subtract, ALU.mult)
                last.then_inc(xn_ready, 1)

            def low_part(m, c):
                dve.wait_ge(xhi_ready, m + 1)
                wait(dve, up_done, E * (m - 1))
                dve.tensor_tensor(xlo[:, c % 2], tr[:], xhi[:, c % 2].bitcast(F32), ALU.subtract).then_inc(xlo_ready, 1)

            def logits_copy(m):
                dve.wait_ge(lgT_done, m + 1)
                wait(dve, lg_done, m)
                dve.tensor_copy(lgT[:], tr[0:E, 0, :]).then_inc(lgT_copied, 1)

            def minus_max(m):
                dve.wait_ge(lg_done, m + 1)
                lg = tr[:, 1, 0:TPB * E].rearrange("p (j e) -> p j e", e=E)
                dve.tensor_reduce(lmax[:], lg, AX.X, ALU.max).then_inc(chain, 1)
                dve.wait_ge(chain, CH * m + 1)
                wait(dve, lexp_ready, m)
                dve.tensor_tensor(lsub[:], lg, lmax[:].unsqueeze(2).broadcast_to([P, TPB, E]), ALU.subtract)\
                   .then_inc(lsub_ready, 1)

            def top_two(m):
                dve.wait_ge(lexp_ready, m + 1)
                dve.tensor_reduce(lsum[:], lexp[:], AX.X, ALU.add).then_inc(chain, 1)
                dve.wait_ge(chain, CH * m + 2)
                dve.reciprocal(linv[:], lsum[:]).then_inc(chain, 1)
                dve.wait_ge(chain, CH * m + 3)
                dve.tensor_tensor(score[:, :, 0:E], lexp[:], linv[:].unsqueeze(2).broadcast_to([P, TPB, E]),
                                  ALU.mult).then_inc(chain, 1)
                dve.wait_ge(chain, CH * m + 4)
                pass_by(dve, passed)
                for j in range(TPB):
                    last = dve.max(top[:, j, :], score[:, j, 0:E])
                last.then_inc(chain, 1)
                dve.wait_ge(chain, CH * m + 5)
                dve.memset(top[:, :, 2:8], -1.0).then_inc(chain, 1)
                dve.wait_ge(chain, CH * m + 6)
                pass_by(dve, passed)
                for j in range(TPB):
                    last = dve.match_replace(rest[:, j, :], top[:, j, :], score[:, j, :], 0.0)
                last.then_inc(chain, 1)
                dve.wait_ge(chain, CH * m + 7)
                wait(dve, scT_done, m)
                dve.tensor_tensor(scale[:], score[:, :, 0:E], rest[:, :, 0:E], ALU.subtract).then_inc(scale_ready, 1)

            def scales_copy(m):
                dve.wait_ge(scT_done, m + 1)
                wait(dve, sc_stored, 16 * m)
                dve.tensor_copy(scT[:], tr[0:E, 0, :]).then_inc(scT_copied, 1)

            def scaled(n, c, k):
                g = E * n + k
                dve.wait_ge(up_done, g + 1)
                if k % 4 == 0:
                    dve.wait_ge(scB_loaded[k // 4], 16 * (n + 1))
                wait(dve, hid_ready, g - 1)
                s = scB[:, c % 2, k, :].unsqueeze(1).broadcast_to([P, 2, TB])
                dve.tensor_tensor(ts[:, k % 2], up[:, k % 2], s, ALU.mult).then_inc(ts_ready, 1)

            def hidden(n, k):
                g = E * n + k
                dve.wait_ge(sil_ready, g + 1)
                dve.wait_ge(ts_ready, g + 1)
                wait(dve, hlo_ready, g - 1)
                dve.tensor_tensor(hid[:, k % 2], ts[:, k % 2, 1], sil[:, k % 2], ALU.mult).then_inc(hid_ready, 1)

            def residual(n):
                dve.wait_ge(down_done, E * (n + 1))
                dve.wait_ge(res_loaded, 16 * (n + 1))
                dve.scalar_tensor_tensor(xres[:], yb[:], 0.5, xres[:], ALU.mult, ALU.add).then_inc(y_read, 1)

            def split_weights(k, n):
                dve.wait_ge(w_hi, k + 1)
                hi, lo = (gws[:, 0], gws[:, 1]) if k == 0 else (flat(sets[k - 1][1], 0), flat(sets[k - 1][1], 1))
                raw = gstage[:] if k == 0 else stage[:, (k - 1) % 2]
                dve.tensor_tensor(lo, raw, hi.bitcast(F32), ALU.subtract).then_inc(w_lo, 1)

            dve.memset(score[:], -1.0).then_inc(consts, 1)
            split_weights(0, 0)
            ln_stats(0, 0, 0)
            normalize(0, 0)
            low_part(0, 0)
            split_weights(1, 0)
            logits_copy(0)
            minus_max(0)
            split_weights(2, 0)
            dve.wait_ge(consts, 1)
            top_two(0)
            scales_copy(0)
            split_weights(3, 0)
            ln_stats(1, 1, 0)
            normalize(1, 1)

            def body(i, c, n):
                n = 2 * i + c if n is None else n
                first, last = isinstance(n, int) and n == 0, isinstance(n, int) and n + 1 >= NB
                for k in range(E):
                    scaled(n, c, k)
                    if k > 0:
                        hidden(n, k - 1)
                    elif not first:
                        hidden(n - 1, E - 1)
                    if k == 2 and not first:
                        residual(n - 1)
                    if not last:
                        if k == 0:
                            low_part(n + 1, c + 1)
                        if k == 2:
                            logits_copy(n + 1)
                            minus_max(n + 1)
                        if k == 3:
                            top_two(n + 1)
                        if k == 5:
                            scales_copy(n + 1)
                    if k == 6 and not (isinstance(n, int) and n + 2 >= NB):
                        ln_stats(n + 2, c + 2, i)
                        normalize(n + 2, c + 2)

            blocks_of(dve, body, NB)
            hidden(NB - 1, E - 1)
            residual(NB - 1)

        @block.scalar
        def _(act):
            def high_part(m, c):
                act.wait_ge(xT_done, m + 1)
                wait(act, up_done, E * (m - 1))
                act.activation(xhi[:, c % 2], tr[:], ACT.Copy).then_inc(xhi_ready, 1)

            def exps(m):
                act.wait_ge(lsub_ready, m + 1)
                act.activation(lexp[:], lsub[:], ACT.Exp).then_inc(lexp_ready, 1)

            def silu(n, k):
                g = E * n + k
                act.wait_ge(ts_ready, g + 1)
                wait(act, hid_ready, g - 1)
                act.activation(sil[:, k % 2], ts[:, k % 2, 0], ACT.Silu).then_inc(sil_ready, 1)

            def high_hidden(n, k):
                g = E * n + k
                act.wait_ge(hid_ready, g + 1)
                wait(act, down_done, g - 3)
                act.activation(hhi[:, k % 4], hid[:, k % 2], ACT.Copy).then_inc(hhi_ready, 1)

            def round_weights(k):
                if k == 0:
                    act.wait_ge(s_w[0], 16)
                    act.activation(gws[:, 0], gstage[:], ACT.Copy).then_inc(w_hi, 1)
                    return
                act.wait_ge(s_w[1], (32, 64, 80)[k - 1])
                act.activation(flat(sets[k - 1][1], 0), stage[:, (k - 1) % 2], ACT.Copy).then_inc(w_hi, 1)

            round_weights(0)
            high_part(0, 0)
            round_weights(1)
            exps(0)
            round_weights(2)
            round_weights(3)

            def body(i, c, n):
                n = 2 * i + c if n is None else n
                first, last = isinstance(n, int) and n == 0, isinstance(n, int) and n + 1 >= NB
                for k in range(E):
                    silu(n, k)
                    if k > 0:
                        high_hidden(n, k - 1)
                    elif not first:
                        high_hidden(n - 1, E - 1)
                    if not last:
                        if k == 0:
                            high_part(n + 1, c + 1)
                        if k == 2:
                            exps(n + 1)

            blocks_of(act, body, NB)
            high_hidden(NB - 1, E - 1)

        @block.gpsimd
        def _(pool):
            pool.memset(ident[:], 0.0).then_inc(id_set, 1)
            pool.memset(mhalf[:], -0.5).then_inc(rstd_part, 1)
            pool.wait_ge(id_set, 1)
            pool.affine_select(out=ident[:], in_=ident[:], compare_op=ALU.not_equal, fill=1.0, base=0,
                               pattern=[[-1, P]], channel_multiplier=1).then_inc(id_set, 1)

            def inverse_std(m):
                pool.wait_ge(stats_ready, m + 1)
                wait(pool, xn_ready, m)
                pass_by(pool, passed)
                pool.tensor_scalar(var_eps[:], mv[:, :, 1], EPS, None, ALU.add).then_inc(rstd_part, 1)
                pool.wait_ge(rstd_part, m + 2)
                pool.tensor_tensor(rstd[:], var_eps[:], mhalf[:], ALU.pow).then_inc(rstd_ready, 1)

            def low_hidden(n, k):
                g = E * n + k
                pool.wait_ge(hhi_ready, g + 1)
                wait(pool, down_done, g - 3)
                pool.tensor_tensor(hlo[:, k % 4], hid[:, k % 2], hhi[:, k % 4].bitcast(F32), ALU.subtract)\
                    .then_inc(hlo_ready, 1)

            inverse_std(0)
            inverse_std(1)

            def body(i, c, n):
                n = 2 * i + c if n is None else n
                first, last = isinstance(n, int) and n == 0, isinstance(n, int) and n + 1 >= NB
                if not first:
                    low_hidden(n - 1, E - 1)
                for k in range(1, E):
                    low_hidden(n, k - 1)
                    if k == 6 and not (isinstance(n, int) and n + 2 >= NB):
                        inverse_std(n + 2)

            blocks_of(pool, body, NB)
            low_hidden(NB - 1, E - 1)


def attention(nc, name, src, dst, wq, wk, wv, wb, cq, ck, cv, rms_w, wo):
    ctx = ExitStack()
    H, D, KW = 4, 64, 4
    NS = L // P
    PR = H // 2
    LEVELS = P.bit_length() - 1
    PRODUCTS = [(0, "X")] + [(l, k) for l in range(1, LEVELS - 1) for k in "XTU"] + \
        [(LEVELS - 1, "X"), (LEVELS - 1, "U")]
    NP = PR + len(PRODUCTS)
    with ctx:
        def sb(n, shape, dt=F32):
            return ctx.enter_context(nc.sbuf_tensor(f"{name}_{n}", shape, dt))

        def sem(n):
            return ctx.enter_context(nc.semaphore(f"{name}_{n}"))

        def sems(n, k):
            return [sem(f"{n}{j}") for j in range(k)]

        wqkv = sb("wqkv", [P, 2, KC, 3, DM], F32R)
        wbs = sb("wbs", [P, 2, KC, H], F32R)
        wos = sb("wos", [P, 2, PR, DM], F32R)
        wstage = sb("wstage", [P, 4, KC, DM])
        bstage = sb("bstage", [P, KC, H])
        rms2 = sb("rms2", [P, 1])
        taps = sb("taps", [P, 3, PR, KW])
        ident = sb("ident", [P, P])
        below = sb("below", [P, P])
        upto = sb("upto", [P, P])
        pair0 = sb("pair0", [P, P])
        halves = sb("halves", [P, LEVELS, P])
        powers = sb("powers", [P, 2, 2 * H])
        xin = sb("xin", [P, 2, 2, DM])
        stats = sb("stats", [P, 2, 6])
        mv = sb("mv", [P, 2, 2])
        var_eps = sb("var_eps", [P, 2])
        rstd = sb("rstd", [P, 2])
        xn = sb("xn", [P, 2, DM])
        xhi = sb("xhi", [P, KC, 2 * P], F32R)
        xlo = sb("xlo", [P, KC, 2 * P], F32R)
        raw = sb("raw", [P, 3, PR, 2, KW - 1 + P])
        acc = sb("acc", [P, 3, PR, 2, P])
        bth = sb("bth", [H, 2 * P])
        beta = sb("beta", [P, 2, H])
        kq = sb("kq", [P, 2, PR, 2, 2, P])
        kx = sb("kx", [P, PR, 2, 2, P])
        vch = sb("vch", [P, PR, 2, P])
        sq = sb("sq", [P, 2, 2, DM])
        ss = sb("ss", [P, 2, 2, 2, H])
        kn = sb("kn", [P, 2, H])
        rk = sb("rk", [P, 2, H])
        cc = sb("cc", [P, 2, 2, H])
        ktok = sb("ktok", [P, 2, 2, DM])
        vn = sb("vn", [P, 2, 2, DM])
        nn = sb("nn", [P, 2, H, P])
        at = sb("at", [P, 2, 2, H, P])
        xt = sb("xt", [P, 2, H, P])
        tt = sb("tt", [P, 2, 2, H, P])
        tu = sb("tu", [P, 2, H, P])
        tc = sb("tc", [P, 2, H, P])
        state = sb("state", [P, 2, PR, P])
        rr = sb("rr", [P, 2, DM])
        mid = sb("mid", [P, 2, H, P])
        osq = sb("osq", [P, 2, DM])
        oms = sb("oms", [P, 2, H])
        ovar = sb("ovar", [P, 2, H])
        oeps = sb("oeps", [P, 2, H])
        osum = sb("osum", [P, 2, H])
        og = sb("og", [P, 2, H])
        on = sb("on", [P, 2, DM])
        othi = sb("othi", [P, PR, 2, P], F32R)
        otlo = sb("otlo", [P, PR, 2, P], F32R)
        xres = sb("xres", [P, 2, DM])

        def pt(n, shape):
            return ctx.enter_context(nc.psum_tensor(f"{name}_{n}", shape, F32))

        fr = pt("fr", [P, 3, 512])
        tp = pt("tp", [P, 2, 512])
        sc = pt("sc", [P, 2, 512])
        ob = pt("ob", [P, 512])

        w_loaded, w_scaled, w_hi, w_lo, masks, zeroed = (sem(n) for n in (
            "w_loaded", "w_scaled", "w_hi", "w_lo", "masks", "zeroed"))
        x_loaded = sems("x_loaded", 2)
        (stats_part, stats_ready, rstd_part, rstd_ready, xn_ready, xT_done, xhi_ready, xlo_ready, qkv_done,
         beta_done, hist_ready, raw_ready, tap0_ready, conv_step, bth_ready, bT_done, beta_ready, silu_ready,
         kx_ready, turned, sq_ready, ss_ready, ktok_ready, kn_ready, rk_ready, cc_ready, vn_ready) = (sem(n) for n in (
             "stats_part", "stats_ready", "rstd_part", "rstd_ready", "xn_ready", "xT_done", "xhi_ready", "xlo_ready",
             "qkv_done", "beta_done", "hist_ready", "raw_ready", "tap0_ready", "conv_step", "bth_ready", "bT_done",
             "beta_ready", "silu_ready", "kx_ready", "turned", "sq_ready", "ss_ready", "ktok_ready", "kn_ready",
             "rk_ready", "cc_ready", "vn_ready"))
        prod_done, evac_done = sems("prod_done", 2), sems("evac_done", 2)
        tstep = sem("tstep")
        passed = sem("passed")
        ks_done, r_ready, mid_done, mid_ready, ds_done, s_ready = (
            sems(n, 2) for n in ("ks_done", "r_ready", "mid_done", "mid_ready", "ds_done", "s_ready"))
        osum_ready = sem("osum_ready")
        (o_done, osq_ready, oms_ready, ovar_part, og_ready, on_ready, oT_done, othi_ready, otlo_ready, y_done,
         y_read, res_loaded, stored) = (sem(n) for n in (
             "o_done", "osq_ready", "oms_ready", "ovar_part", "og_ready", "on_ready", "oT_done", "othi_ready",
             "otlo_ready", "y_done", "y_read", "res_loaded", "stored"))

        block = ctx.enter_context(nc.Block())
        x_v = src.rearrange("(s n p) d -> n p s d", s=2, p=P)
        o_v = dst.rearrange("(s n p) d -> n p s d", s=2, p=P)
        TERMS = [(0, 0), (0, 1), (1, 0)]
        WSETS = [wk, wv, wq]

        def steps_of(eng, body):
            def go(i, c, f, t, s):
                body(*((((2 * i + c + d), (c + d) % 2, i + (c + d) // 2) if on else None)
                       for d, on in ((2, f), (1, t), (0, s))))
            go(-1, 0, True, False, False)
            go(-1, 1, True, True, False)
            go(0, 0, True, True, True)
            go(0, 1, True, True, True)
            with eng.Fori(1, NS // 2 - 2) as i:
                go(i, 0, True, True, True)
                go(i, 1, True, True, True)
            go(NS // 2 - 2, 0, True, True, True)
            go(NS // 2 - 2, 1, True, True, True)
            go(NS // 2 - 1, 0, False, True, True)
            go(NS // 2 - 1, 1, False, False, True)

        @block.sync
        def _(sp):
            sp.dma_start(wstage[:, 3], wo.rearrange("(c p) n -> p c n", p=P)).then_inc(w_loaded, 16)
            for j, w in enumerate(WSETS):
                sp.dma_start(wstage[:, j], w.rearrange("(c p) n -> p c n", p=P)).then_inc(w_loaded, 16)
            sp.dma_start(bstage[:], wb.rearrange("(c p) n -> p c n", p=P)).then_inc(w_loaded, 16)
            for j, w in enumerate((ck, cv, cq)):
                sp.dma_start(taps[:, j], w.rearrange("(r p) o k -> p r (o k)", p=P)).then_inc(w_loaded, 16)
            for h in range(2):
                sp.dma_start(rms2[h * D:(h + 1) * D, :], rms_w.rearrange("(d o) -> d o", o=1)).then_inc(w_loaded, 16)

            def load_x(f):
                m, par, turn = f
                wait(sp, xn_ready, m - 1)
                sp.dma_start(xin[:, par], x_v[m]).then_inc(x_loaded[par], 16)

            def body(f, t, s):
                if f:
                    load_x(f)
                if s:
                    m = s[0]
                    wait(sp, stored, 16 * m)
                    sp.dma_start(xres[:], x_v[m]).then_inc(res_loaded, 16)
                    sp.wait_ge(y_read, m + 1)
                    sp.dma_start(o_v[m], xres[:]).then_inc(stored, 16)

            steps_of(sp, body)
            sp.wait_ge(stored, 16 * NS)

        @block.tensor
        def _(pe):
            def x_turn(f):
                m = f[0]
                pe.wait_ge(xn_ready, m + 1)
                wait(pe, vn_ready, m)
                for q in range(KC):
                    for s in range(2):
                        last = pe.transpose(fr[:, 0, (2 * q + s) * P:(2 * q + s + 1) * P],
                                            xn[:, s, q * P:(q + 1) * P], ident[:])
                last.then_inc(xT_done, 1)

            def project(out, w, col, start):
                for k, (a, b) in enumerate(TERMS):
                    for q in range(KC):
                        last = pe.matmul(out, w[:, a, q, col], (xhi, xlo)[b][:, q, :], skip_group_check=True,
                                         start=(start and k == 0 and q == 0), stop=(k == 2 and q == KC - 1))
                return last

            def qkv(f, j):
                m = f[0]
                if j == 0:
                    pe.wait_ge(xhi_ready, m + 1)
                    pe.wait_ge(xlo_ready, m + 1)
                    wait(pe, sq_ready, m)
                    wait(pe, ktok_ready, m)
                if j == 2:
                    pe.wait_ge(bth_ready, m + 1)
                for r in range(PR):
                    last = project(fr[:, (2, 0, 1)[j], r * 2 * P:(r + 1) * 2 * P],
                                   wqkv[:, :, :, j, :], slice(r * P, (r + 1) * P), r == 0)
                last.then_inc(qkv_done, 1)

            def beta_rows(f):
                m = f[0]
                project(fr[0:H, 1, 0:2 * P], wbs, slice(0, H), True).then_inc(beta_done, 1)

            def beta_turn(f):
                m = f[0]
                pe.wait_ge(bth_ready, m + 1)
                pe.wait_ge(raw_ready, 3 * m + 2)
                pass_by(pe, passed)
                for s in range(2):
                    last = pe.transpose(fr[:, 0, s * H:(s + 1) * H], bth[:, s * P:(s + 1) * P], ident[0:H, 0:H])
                last.then_inc(bT_done, 1)

            def turn_back(f):
                m, par, _ = f
                pe.wait_ge(silu_ready, 3 * (m + 1))
                pe.wait_ge(raw_ready, 3 * (m + 1))
                for s in range(2):
                    for j in range(2):
                        for r in range(PR):
                            last = pe.transpose(fr[:, 1 + s, (2 * j + r) * P:(2 * j + r + 1) * P],
                                                kq[:, par, r, s, j, :], ident[:])
                last.then_inc(turned, 1)
                pe.wait_ge(beta_ready, m + 1)
                for s in range(2):
                    for r in range(PR):
                        last = pe.transpose(fr[:, 0, (2 * s + r) * P:(2 * s + r + 1) * P], vch[:, r, s, :], ident[:])
                last.then_inc(turned, 1)

            def product(t, q):
                m, par, _ = t
                for s in range(2):
                    wait(pe, evac_done[s], NP * m + q)
                    if q == 0 and s == 0:
                        pe.wait_ge(kx_ready, 2 * (m + 1))
                    if q < PR:
                        for h in range(2):
                            last = pe.matmul(tp[:, s, h * 2 * P:(h + 1) * 2 * P], kx[:, q, s, h, :],
                                             kq[:, par, q, s], start=(h == 0), stop=True, skip_group_check=True)
                    else:
                        l, kind = PRODUCTS[q - PR]
                        for h in range(H):
                            a, b = {"X": (nn[:, s, h, :], tu[:, s, h, :] if l else ident[:]),
                                    "T": (xt[:, s, h, :], tt[:, l % 2, s, h, :]),
                                    "U": (tt[:, l % 2, s, h, :], xt[:, s, h, :])}[kind]
                            last = pe.matmul(tp[:, s, h * P:(h + 1) * P], a, b, start=(h == 0), stop=True,
                                             skip_group_check=True)
                    last.then_inc(prod_done[s], 1)

            def state_in(st):
                m, par, _ = st
                for s in range(2):
                    pe.wait_ge(s_ready[s], m + 1)
                    for r in range(PR):
                        last = pe.matmul(sc[:, s, r * P:(r + 1) * P], kq[:, par, r, s, 0, :], state[:, s, r, :],
                                         start=(r == 0), stop=True, skip_group_check=True)
                    last.then_inc(ks_done[s], 1)
                wait(pe, y_read, m)
                for s in range(2):
                    for r in range(PR):
                        pe.matmul(ob[:, s * DM + r * P:s * DM + (r + 1) * P], kq[:, par, r, s, 1, :],
                                  state[:, s, r, :], start=(s == 0 and r == 0), stop=False, skip_group_check=True)

            def mids(st):
                m = st[0]
                for s in range(2):
                    pe.wait_ge(r_ready[s], m + 1)
                    pe.wait_ge(evac_done[s], NP * (m + 1))
                    for h in range(H):
                        r = h // 2
                        last = pe.matmul(sc[:, s, h * P:(h + 1) * P], tc[:, s, h, :], rr[:, s, r * P:(r + 1) * P],
                                         start=(h == 0), stop=True, skip_group_check=True)
                    last.then_inc(mid_done[s], 1)

            def state_out(st):
                m, par, _ = st
                for s in range(2):
                    pe.wait_ge(mid_ready[s], m + 1)
                    mm = mid[:, s].rearrange("p h (g d) -> p (h g) d", d=D)
                    for r in range(PR):
                        last = pe.matmul(sc[:, s, r * P:(r + 1) * P], ktok[:, par, s, r * P:(r + 1) * P],
                                         mm[:, 4 * r:4 * r + 4:3, :], start=(r == 0), stop=True,
                                         skip_group_check=True)
                    last.then_inc(ds_done[s], 1)

            def outputs(st):
                m, par, _ = st
                for s in range(2):
                    for h in range(H):
                        r = h // 2
                        last = pe.matmul(ob[:, s * DM + r * P:s * DM + (r + 1) * P], at[:, par, s, h, :],
                                         mid[:, s, h, :], start=False, stop=(h % 2 == 1), skip_group_check=True)
                last.then_inc(o_done, 1)

            def out_turn(st):
                m = st[0]
                pe.wait_ge(on_ready, m + 1)
                for r in range(PR):
                    for s in range(2):
                        last = pe.transpose(ob[:, (2 * r + s) * P:(2 * r + s + 1) * P],
                                            on[:, s, r * P:(r + 1) * P], ident[:])
                last.then_inc(oT_done, 1)

            def out_project(st):
                m = st[0]
                pe.wait_ge(othi_ready, m + 1)
                pe.wait_ge(otlo_ready, m + 1)
                for s in range(2):
                    for k, (a, b) in enumerate(TERMS):
                        for r in range(PR):
                            last = pe.matmul(ob[:, s * DM:(s + 1) * DM], (othi, otlo)[b][:, r, s, :], wos[:, a, r, :],
                                             start=(s == 0 and k == 0 and r == 0), stop=(k == 2 and r == PR - 1),
                                             skip_group_check=True)
                last.then_inc(y_done, 1)

            pe.wait_ge(masks, 1)
            pe.wait_ge(w_hi, 3)
            pe.wait_ge(w_lo, 3)
            pe.wait_ge(zeroed, 2)

            def body(f, t, s):
                for q in range(NP):
                    if t:
                        product(t, q)
                    if s:
                        if q == 0:
                            state_in(s)
                        if q == 2:
                            mids(s)
                        if q == 4:
                            state_out(s)
                        if q == 6:
                            outputs(s)
                        if q == 9:
                            out_turn(s)
                        if q == 11:
                            out_project(s)
                    if f:
                        if q == 1:
                            x_turn(f)
                        if q == 3:
                            qkv(f, 0)
                            beta_rows(f)
                        if q == 4:
                            qkv(f, 1)
                        if q == 5:
                            qkv(f, 2)
                        if q == 8:
                            beta_turn(f)
                        if q == 15:
                            turn_back(f)

            steps_of(pe, body)

        @block.vector
        def _(dve):
            def split(k, hi, lo, rawp):
                dve.wait_ge(w_hi, k + 1)
                dve.tensor_tensor(lo, rawp, hi.bitcast(F32), ALU.subtract).then_inc(w_lo, 1)

            def norm_in(f):
                m, par, turn = f
                dve.wait_ge(x_loaded[par], 16 * (turn + 1))
                wait(dve, xn_ready, m)
                for s in range(2):
                    dve.bn_stats(stats[:, s, :], xin[:, par, s, :]).then_inc(stats_part, 1)
                dve.wait_ge(stats_part, 2 * (m + 1))
                pass_by(dve, passed)
                for s in range(2):
                    last = dve.bn_aggr(mv[:, s, :], stats[:, s, :])
                last.then_inc(stats_ready, 1)
                dve.wait_ge(rstd_ready, m + 1)
                wait(dve, xT_done, m)
                for s in range(2):
                    last = dve.tensor_scalar(xn[:, s, :], xin[:, par, s, :], mv[:, s, 0:1], rstd[:, s:s + 1],
                                             ALU.subtract, ALU.mult)
                last.then_inc(xn_ready, 1)

            def x_low(f):
                m = f[0]
                dve.wait_ge(xhi_ready, m + 1)
                dve.tensor_tensor(xlo[:].rearrange("p c t -> p (c t)"), fr[:, 0, :],
                                  xhi[:].rearrange("p c t -> p (c t)").bitcast(F32), ALU.subtract).then_inc(xlo_ready, 1)

            def history(f):
                m = f[0]
                wait(dve, conv_step, 18 * m)
                rv = raw[:].rearrange("p j r s t -> p (j r s) t")
                dve.tensor_copy(rv[:, :, 0:KW - 1], rv[:, :, P:P + KW - 1]).then_inc(hist_ready, 1)

            def conv(f, tap):
                m = f[0]
                for j in range(3):
                    for r in range(PR):
                        n = 6 * (tap - 1) + 2 * j + r
                        if tap == 1:
                            dve.wait_ge(tap0_ready, 6 * m + 2 * j + r + 1)
                        else:
                            dve.wait_ge(conv_step, 18 * m + n - 5)
                        dve.scalar_tensor_tensor(acc[:, j, r], raw[:, j, r, :, tap:tap + P],
                                                 taps[:, j, r, tap:tap + 1], acc[:, j, r], ALU.mult, ALU.add)\
                           .then_inc(conv_step, 1)

            def betas(f):
                m = f[0]
                dve.wait_ge(bT_done, m + 1)
                wait(dve, cc_ready, m)
                dve.tensor_scalar(beta[:].rearrange("p s h -> p (s h)"), fr[:, 0, 0:2 * H], 0.5, 0.5, ALU.mult,
                                  ALU.add).then_inc(beta_ready, 1)

            def norms(f):
                m, par, _ = f
                dve.wait_ge(sq_ready, m + 1)
                wait(dve, og_ready, m - 1)
                wait(dve, evac_done[1], NP * (m - 1))
                wait(dve, cc_ready, m)
                dve.tensor_reduce(ss[:, par].rearrange("p s j h -> p (s j h)"),
                                  sq[:].rearrange("p s j (h d) -> p (s j h) d", d=D), AX.X, ALU.add).then_inc(ss_ready, 1)
                dve.wait_ge(ss_ready, m + 1)
                dve.reciprocal(rk[:], ss[:, par, :, 0, :]).then_inc(rk_ready, 1)
                dve.wait_ge(rk_ready, m + 1)
                dve.wait_ge(beta_ready, m + 1)
                dve.tensor_tensor(cc[:, par], beta[:], rk[:], ALU.mult).then_inc(cc_ready, 1)

            def values(f):
                m, par, _ = f
                dve.wait_ge(kn_ready, m + 1)
                dve.wait_ge(turned, 2 * (m + 1))
                for s in range(2):
                    wait(dve, r_ready[s], m - 1)
                dve.tensor_tensor(vn[:, par].rearrange("p s (h d) -> p (s h) d", d=D),
                                  fr[:, 0, :].rearrange("p (g d) -> p g d", d=D),
                                  kn[:].rearrange("p s h -> p (s h)").unsqueeze(2).broadcast_to([P, 2 * H, D]),
                                  ALU.mult).then_inc(vn_ready, 1)

            TS = 6

            def evacuate(t, q):
                m, par, _ = t
                for s in range(2):
                    dve.wait_ge(prod_done[s], NP * m + q + 1)
                    if q < PR:
                        if q == 0:
                            dve.wait_ge(cc_ready, m + 1)
                        g = tp[:, s, :].rearrange("p (h j t) -> p h j t", h=2, j=2)
                        for h in range(2):
                            dve.scalar_tensor_tensor(nn[:, s, 2 * q + h, :], g[:, h, 0, :],
                                                     cc[:, par, s, 2 * q + h:2 * q + h + 1], below[:],
                                                     ALU.mult, ALU.mult)
                        dve.tensor_tensor(at[:, par, s, 2 * q:2 * q + 2, :], g[:, :, 1, :],
                                          upto[:].unsqueeze(1).broadcast_to([P, 2, P]), ALU.mult)\
                           .then_inc(evac_done[s], 1)
                        continue
                    l, kind = PRODUCTS[q - PR]
                    prod = tp[:, s, :].rearrange("p (h t) -> p h t", t=P)
                    up = halves[:, l, :].unsqueeze(1).broadcast_to([P, H, P])
                    idb = ident[:].unsqueeze(1).broadcast_to([P, H, P])
                    if l == 0:
                        dve.tensor_tensor(xt[:, s], prod, up, ALU.mult).then_inc(tstep, 1)
                        dve.tensor_tensor(tt[:, 0, s], nn[:, s], pair0[:].unsqueeze(1).broadcast_to([P, H, P]),
                                          ALU.mult).then_inc(tstep, 1)
                        dve.wait_ge(tstep, TS * m + 2 * s + 1)
                        dve.tensor_tensor(tu[:, s], idb, xt[:, s], ALU.subtract)
                        dve.wait_ge(tstep, TS * m + 2 * s + 2)
                        dve.tensor_tensor(tt[:, 1, s], idb, tt[:, 0, s], ALU.subtract).then_inc(evac_done[s], 1)
                    elif kind == "X":
                        dve.tensor_tensor(xt[:, s], prod, up, ALU.mult).then_inc(evac_done[s], 1)
                    elif kind == "T":
                        dve.tensor_tensor(tt[:, (l + 1) % 2, s], tt[:, l % 2, s], prod, ALU.subtract)\
                           .then_inc(evac_done[s], 1)
                    elif l < LEVELS - 1:
                        dve.tensor_tensor(tu[:, s], tu[:, s], prod, ALU.subtract).then_inc(evac_done[s], 1)
                    else:
                        dve.tensor_tensor(xt[:, s], tu[:, s], prod, ALU.subtract).then_inc(tstep, 1)
                        dve.wait_ge(tstep, TS * m + 5 + s)
                        dve.tensor_tensor(tc[:, s], xt[:, s], cc[:, par, s, :].unsqueeze(2).broadcast_to([P, H, P]),
                                          ALU.mult).then_inc(evac_done[s], 1)

            def remainder(st):
                m, par, _ = st
                for s in range(2):
                    dve.wait_ge(ks_done[s], m + 1)
                    dve.wait_ge(vn_ready, m + 1)
                    dve.tensor_tensor(rr[:, s, :], vn[:, par, s, :], sc[:, s, 0:DM], ALU.subtract)\
                       .then_inc(r_ready[s], 1)

            def state_add(st):
                m = st[0]
                for s in range(2):
                    dve.wait_ge(ds_done[s], m + 1)
                    d = sc[:, s, 0:DM].rearrange("p (r c) -> p r c", c=P)
                    for h in range(2):
                        a = slice(h * D, (h + 1) * D)
                        last = dve.tensor_tensor(state[a, s, :, a], state[a, s, :, a], d[a, :, a], ALU.add)
                    last.then_inc(s_ready[s], 1)

            def out_norm(st):
                m, par, _ = st
                dve.wait_ge(osq_ready, m + 1)
                wait(dve, ovar_part, 2 * m)
                dve.tensor_reduce(oms[:].rearrange("p s h -> p (s h)"),
                                  osq[:].rearrange("p s (h d) -> p (s h) d", d=D), AX.X, ALU.add).then_inc(oms_ready, 1)

            def out_scale(st):
                m = st[0]
                dve.wait_ge(og_ready, m + 1)
                wait(dve, oT_done, m)
                dve.tensor_tensor(on[:].rearrange("p s (h d) -> p (s h) d", d=D),
                                  ob[:].rearrange("p (g d) -> p g d", d=D),
                                  og[:].rearrange("p s h -> p (s h)").unsqueeze(2).broadcast_to([P, 2 * H, D]),
                                  ALU.mult).then_inc(on_ready, 1)

            def out_low(st):
                m = st[0]
                dve.wait_ge(othi_ready, m + 1)
                dve.tensor_tensor(otlo[:].rearrange("p r s t -> p (r s t)"), ob[:],
                                  othi[:].rearrange("p r s t -> p (r s t)").bitcast(F32), ALU.subtract)\
                   .then_inc(otlo_ready, 1)

            def residual(st):
                m = st[0]
                dve.wait_ge(y_done, m + 1)
                dve.wait_ge(res_loaded, 16 * (m + 1))
                dve.tensor_tensor(xres[:].rearrange("p s d -> p (s d)"), ob[:], xres[:].rearrange("p s d -> p (s d)"),
                                  ALU.add).then_inc(y_read, 1)

            dve.memset(raw[:], 0.0).then_inc(zeroed, 1)
            for s in range(2):
                dve.memset(state[:, s], 0.0).then_inc(s_ready[s], 1)
            dve.memset(mid[:], 0.0).then_inc(zeroed, 1)
            dve.wait_ge(w_loaded, 16 * 10)
            dve.tensor_scalar(wstage[:, 3], wstage[:, 3], rms2[:, 0:1], None, ALU.mult).then_inc(w_scaled, 1)
            dve.wait_ge(w_scaled, 1)
            split(0, wqkv[:, 0].rearrange("p c j d -> p j c d"), wqkv[:, 1].rearrange("p c j d -> p j c d"), wstage[:, 0:3])
            split(1, wbs[:, 0], wbs[:, 1], bstage[:])
            split(2, wos[:, 0], wos[:, 1], wstage[:, 3])
            dve.wait_ge(zeroed, 2)
            dve.wait_ge(masks, 1)
            norm_in((0, 0, 0))

            def body(f, t, s):
                for q in range(NP):
                    if t:
                        evacuate(t, q)
                    if s:
                        if q == 0:
                            remainder(s)
                        if q == 4:
                            state_add(s)
                        if q == 7:
                            out_norm(s)
                        if q == 8:
                            out_scale(s)
                        if q == 10:
                            out_low(s)
                        if q == 12:
                            residual(s)
                    if f:
                        if q == 1:
                            x_low(f)
                            history(f)
                        if q in (7, 9, 11):
                            conv(f, (q - 5) // 2)
                        if q == 8:
                            betas(f)
                        if q == 16:
                            norms(f)
                        if q == 17:
                            values(f)
                        if q == 18 and not (isinstance(f[0], int) and f[0] + 1 >= NS):
                            m, par, turn = f
                            nxt = (m + 1, 1 - par, turn + par)
                            norm_in(nxt)

            steps_of(dve, body)

        @block.scalar
        def _(act):
            def x_high(f):
                m = f[0]
                act.wait_ge(xT_done, m + 1)
                wait(act, qkv_done, 3 * m)
                act.activation(xhi[:].rearrange("p c t -> p (c t)"), fr[:, 0, :], ACT.Copy).then_inc(xhi_ready, 1)

            def raw_out(f, j):
                m = f[0]
                act.wait_ge(qkv_done, 3 * m + j + 1)
                act.wait_ge(hist_ready, m + 1)
                act.activation(raw[:, j].rearrange("p r s t -> p (r s) t")[:, :, KW - 1:],
                               fr[:, (2, 0, 1)[j], :].rearrange("p (g t) -> p g t", t=P), ACT.Copy).then_inc(raw_ready, 1)

            def tap0(f, j):
                m = f[0]
                act.wait_ge(raw_ready, 3 * m + j + 1)
                wait(act, silu_ready, 3 * m)
                for r in range(PR):
                    act.activation(acc[:, j, r], raw[:, j, r, :, 0:P], ACT.Copy, scale=taps[:, j, r, 0:1])\
                       .then_inc(tap0_ready, 1)

            def beta_tanh(f):
                m = f[0]
                act.wait_ge(beta_done, m + 1)
                wait(act, bT_done, m)
                act.activation(bth[:], fr[0:H, 1, 0:2 * P], ACT.Tanh, scale=0.5).then_inc(bth_ready, 1)

            def silus(f):
                m, par, _ = f
                for j in range(3):
                    act.wait_ge(conv_step, 18 * m + 14 + 2 * j)
                    if j == 0:
                        wait(act, o_done, m - 1)
                        wait(act, turned, 2 * m)
                    out = (kq[:, par, :, :, 0, :], vch[:], kq[:, par, :, :, 1, :])[j]
                    act.activation(out, acc[:, j], ACT.Silu).then_inc(silu_ready, 1)

            def squares(f):
                m, par, _ = f
                act.wait_ge(turned, 2 * m + 1)
                wait(act, ss_ready, m)
                act.activation(sq[:].rearrange("p s j d -> p s (j d)"), fr[:, 1:3, :], ACT.Square).then_inc(sq_ready, 1)
                wait(act, ds_done[1], m - 1)
                act.activation(ktok[:, par], fr[:, 1:3, 0:DM], ACT.Copy).then_inc(ktok_ready, 1)

            def mid_out(st):
                m = st[0]
                for s in range(2):
                    act.wait_ge(mid_done[s], m + 1)
                    mm = mid[:, s].rearrange("p h (g d) -> p (h g) d", d=D).rearrange("p (r g) d -> p r g d", r=PR)
                    pp = sc[:, s, :].rearrange("p (r g d) -> p r g d", r=PR, d=D)
                    act.activation(mm[:, :, 0:4:3, :], pp[:, :, 0:4:3, :], ACT.Copy).then_inc(mid_ready[s], 1)

            def out_squares(st):
                m = st[0]
                act.wait_ge(o_done, m + 1)
                wait(act, oms_ready, m)
                act.activation(osq[:].rearrange("p s d -> p (s d)"), ob[:], ACT.Square).then_inc(osq_ready, 1)

            def out_high(st):
                m = st[0]
                act.wait_ge(oT_done, m + 1)
                wait(act, y_done, m)
                act.activation(othi[:].rearrange("p r s t -> p (r s t)"), ob[:], ACT.Copy).then_inc(othi_ready, 1)

            act.wait_ge(w_loaded, 16 * 10)
            act.activation(wqkv[:, 0].rearrange("p c j d -> p j c d"), wstage[:, 0:3], ACT.Copy).then_inc(w_hi, 1)
            act.activation(wbs[:, 0], bstage[:], ACT.Copy).then_inc(w_hi, 1)
            act.wait_ge(w_scaled, 1)
            act.activation(wos[:, 0], wstage[:, 3], ACT.Copy).then_inc(w_hi, 1)

            def body(f, t, s):
                for q in range(NP):
                    if s:
                        if q == 2:
                            mid_out(s)
                        if q == 6:
                            out_squares(s)
                        if q == 9:
                            out_high(s)
                    if f:
                        if q == 1:
                            x_high(f)
                        if q == 3:
                            raw_out(f, 0)
                            beta_tanh(f)
                            tap0(f, 0)
                        if q == 4:
                            raw_out(f, 1)
                            tap0(f, 1)
                        if q == 5:
                            raw_out(f, 2)
                            tap0(f, 2)
                        if q == 12:
                            silus(f)
                        if q == 15:
                            squares(f)

            steps_of(act, body)

        @block.gpsimd
        def _(pool):
            count = [0]

            def link(ins):
                count[0] += 1
                ins.then_inc(rstd_part, 1)
                pool.wait_ge(rstd_part, count[0])

            def select(view, pattern, base, mult, op=ALU.is_ge, fill=0.0):
                link(pool.affine_select(out=view, in_=view, compare_op=op, fill=fill, base=base, pattern=pattern,
                                        channel_multiplier=mult))

            link(pool.memset(ident[:], 0.0))
            select(ident[:], [[-1, P]], 0, 1, ALU.not_equal, 1.0)
            link(pool.memset(below[:], 1.0))
            select(below[:], [[-1, P]], -1, 1)
            link(pool.memset(upto[:], 1.0))
            select(upto[:], [[1, P]], 0, -1)
            link(pool.memset(pair0[:], 0.0))
            select(pair0[:], [[-1, P]], -1, 1, ALU.not_equal, 1.0)
            v = pair0[:].rearrange("p (b t) -> p b t", t=2)
            link(pool.memset(v[:, :, 1:2], 0.0))
            for l in range(LEVELS):
                w = 2 ** l
                v = halves[:, l, :].rearrange("p (b h t) -> p b h t", h=2, t=w)
                link(pool.memset(v[:, :, 0:1, :], 0.0))
                link(pool.memset(v[:, :, 1:2, :], 1.0))
                v = v.rearrange("p b h t -> p b (h t)")
                pat = [[-2 * w, P // (2 * w)], [0, 2 * w]]
                select(v, pat, 0, 1)
                select(v, [[2 * w, P // (2 * w)], [0, 2 * w]], w - 1, -1)
            link(pool.memset(powers[:, 0, :], 0.5))
            link(pool.memset(powers[:, 1, :], -0.5))
            pool.memset(kx[:], 0.0).then_inc(masks, 1)
            pool.wait_ge(masks, 1)
            base = count[0]

            def inverse_std(m):
                pool.wait_ge(stats_ready, m + 1)
                wait(pool, xn_ready, m)
                pass_by(pool, passed)
                pool.tensor_scalar(var_eps[:], mv[:, :, 1], EPS, None, ALU.add).then_inc(rstd_part, 1)
                pool.wait_ge(rstd_part, base + m + 1)
                pool.tensor_tensor(rstd[:], var_eps[:], powers[:, 1, 0:2], ALU.pow).then_inc(rstd_ready, 1)

            def expand(f):
                m, par, _ = f
                pool.wait_ge(silu_ready, 3 * m + 1)
                for s in range(2):
                    wait(pool, prod_done[s], NP * (m - 1) + PR)
                for h in range(2):
                    a = slice(h * D, (h + 1) * D)
                    pass_by(pool, passed)
                    pool.tensor_copy(kx[a, :, :, h, :], kq[a, par, :, :, 0, :]).then_inc(kx_ready, 1)
                    pool.wait_ge(kx_ready, 2 * m + h + 1)

            def key_norms(f):
                m, par, _ = f
                pool.wait_ge(ss_ready, m + 1)
                wait(pool, vn_ready, m)
                pool.tensor_tensor(kn[:], ss[:, par, :, 0, :], powers[:, 0, :].rearrange("p (s h) -> p s h", s=2),
                                   ALU.pow).then_inc(kn_ready, 1)

            def out_factor(st):
                m, par, _ = st
                pool.wait_ge(oms_ready, m + 1)
                wait(pool, og_ready, m)
                pass_by(pool, passed)
                pool.tensor_scalar(ovar[:], oms[:], 1.0 / D, None, ALU.mult).then_inc(ovar_part, 1)
                pool.tensor_scalar(oeps[:], ss[:, par, :, 1, :], D * EPS, None, ALU.mult).then_inc(ovar_part, 1)
                pool.wait_ge(ovar_part, 2 * m + 2)
                pool.tensor_tensor(osum[:], ovar[:], oeps[:], ALU.add).then_inc(osum_ready, 1)
                pool.wait_ge(osum_ready, m + 1)
                wait(pool, on_ready, m)
                pool.tensor_tensor(og[:], osum[:], powers[:, 1, :].rearrange("p (s h) -> p s h", s=2),
                                   ALU.pow).then_inc(og_ready, 1)

            inverse_std(0)

            def body(f, t, s):
                for q in range(NP):
                    if s and q == 7:
                        out_factor(s)
                    if f:
                        if q == 13:
                            expand(f)
                        if q == 16:
                            key_norms(f)
                        if q == 18 and not (isinstance(f[0], int) and f[0] + 1 >= NS):
                            inverse_std(f[0] + 1)

            steps_of(pool, body)


def build(nc, x, wq, wk, wv, wb, cq, ck, cv, rms_w, wo, gate_w, w1, w2, w3, out):
    def dram(n, shape):
        return nc.dram_tensor(n, shape, F32, kind="Internal").ap()

    x1, x2 = dram("x_after_first", [B * L, DM]), dram("x_after_attention", [B * L, DM])
    s1, s2 = dram("scales_first", [E, TB]), dram("scales_second", [E, TB])
    ffn(nc, "ffn1", x.rearrange("b l d -> (b l) d"), x1, s1, gate_w, w1, w2, w3)
    attention(nc, "attn", x1, x2, wq, wk, wv, wb, cq, ck, cv, rms_w, wo)
    ffn(nc, "ffn2", x2, out.rearrange("b l d -> (b l) d"), s2, gate_w, w1, w2, w3)


_INS = ["L0_attn_x", "L0_attn_Wq", "L0_attn_Wk", "L0_attn_Wv", "L0_attn_Wb", "L0_attn_conv_q_w", "L0_attn_conv_k_w",
        "L0_attn_conv_v_w", "L0_attn_rms_w", "L0_attn_Wo", "L0_ffn_gate_w", "L0_ffn_w1", "L0_ffn_w2", "L0_ffn_w3"]
_OUTS = [((B, L, DM), "float32")]


def kernel(**inputs):
    import numpy as _np
    import concourse.bacc as _bacc
    from concourse import mybir as _mybir
    from concourse.bass_utils import run_bass_kernel_spmd as _run

    nc = _bacc.Bacc("TRN2", target_bir_lowering=False, num_devices=1)
    arrays, args = {}, []
    for name in _INS:
        a = _np.ascontiguousarray(inputs[name])
        arrays[f"in_{name}_dram"] = a
        args.append(nc.dram_tensor(f"in_{name}_dram", a.shape, _mybir.dt.from_np(a.dtype), kind="ExternalInput").ap())
    for i, (shape, dtype) in enumerate(_OUTS):
        dt = _mybir.dt.from_np(_np.dtype(dtype))
        args.append(nc.dram_tensor(f"out_{i}_dram", shape, dt, kind="ExternalOutput").ap())
    build(nc, *args)
    r = _run(nc, [arrays], core_ids=[0])
    return r.results[0]["out_0_dram"]
```

```python
from contextlib import ExitStack

import concourse.bass as bass
from concourse import mybir

P = 128
B, L, DM = 2, 4096, 256
NT = B * L // P
KC = DM // P
E, HF = 8, 128
TPB = 4
TB = TPB * P
NB = NT // TPB
EPS = 1e-5
F32 = mybir.dt.float32
F32R = mybir.dt.float32r
ALU = mybir.AluOpType
ACT = mybir.ActivationFunctionType
AX = mybir.AxisListType


def wait(eng, sem, value):
    if not (isinstance(value, int) and value <= 0):
        eng.wait_ge(sem, value)


def pass_by(eng, passed):
    eng.sem_inc(passed, 1)


def blocks_of(eng, body, count):
    body(0, 0, 0)
    body(0, 1, 1)
    with eng.Fori(1, count // 2 - 1) as i:
        body(i, 0, None)
        body(i, 1, None)
    body(count // 2 - 1, 0, count - 2)
    body(count // 2 - 1, 1, count - 1)


def ffn(nc, name, src, dst, s_dram, gate_w, w1, w2, w3):
    ctx = ExitStack()
    with ctx:
        def sb(n, shape, dt=F32):
            return ctx.enter_context(nc.sbuf_tensor(f"{name}_{n}", shape, dt))

        def sem(n):
            return ctx.enter_context(nc.semaphore(f"{name}_{n}"))

        w1s = sb("w1s", [P, 2, KC, E, HF], F32R)
        w3s = sb("w3s", [P, 2, KC, E, HF], F32R)
        w2s = sb("w2s", [P, 2, E, DM], F32R)
        gws = sb("gws", [P, 2, KC, E], F32R)
        stage = sb("stage", [P, 2, E * DM])
        gstage = sb("gstage", [P, KC, E])
        ident = sb("ident", [P, P])
        eps_t = sb("eps_t", [P, 1])
        mhalf = sb("mhalf", [P, TPB])
        xin = sb("xin", [P, 2, TPB, DM])
        stats = sb("stats", [P, TPB, 6])
        mv = sb("mv", [P, TPB, 2])
        var_eps = sb("var_eps", [P, TPB])
        rstd = sb("rstd", [P, TPB])
        xn = sb("xn", [P, TPB, DM])
        xhi = sb("xhi", [P, 2, KC, TB], F32R)
        xlo = sb("xlo", [P, 2, KC, TB], F32R)
        lgT = sb("lgT", [E, TB])
        lmax = sb("lmax", [P, TPB])
        lsub = sb("lsub", [P, TPB, E])
        lexp = sb("lexp", [P, TPB, E])
        lsum = sb("lsum", [P, TPB])
        linv = sb("linv", [P, TPB])
        score = sb("score", [P, TPB, 2 * E])
        top = sb("top", [P, TPB, 8])
        rest = sb("rest", [P, TPB, 2 * E])
        scale = sb("scale", [P, TPB, E])
        scT = sb("scT", [E, TB])
        scB = sb("scB", [P, 2, E, TB])
        ts = sb("ts", [P, 2, 2, TB])
        sil = sb("sil", [P, 2, TB])
        hid = sb("hid", [P, 2, TB])
        hhi = sb("hhi", [P, 4, TB], F32R)
        hlo = sb("hlo", [P, 4, TB], F32R)
        xres = sb("xres", [P, TPB, DM])

        def pt(n, shape):
            return ctx.enter_context(nc.psum_tensor(f"{name}_{n}", shape, F32))

        up = pt("up", [P, 2, 2, TB])
        yb = pt("yb", [P, TPB, DM])
        tr = pt("tr", [P, KC, TB])

        s_w = [sem(f"w_loaded{j}") for j in range(2)]
        w_hi = sem("w_hi")
        w_lo = sem("w_lo")
        consts = sem("consts")
        passed = sem("passed")
        id_set = sem("id_set")
        x_loaded = [sem(f"x_loaded{j}") for j in range(2)]
        res_loaded = sem("res_loaded")
        stats_ready = sem("stats_ready")
        stats_part = sem("stats_part")
        rstd_part = sem("rstd_part")
        rstd_ready = sem("rstd_ready")
        xn_ready = sem("xn_ready")
        xT_done = sem("xT_done")
        xhi_ready = sem("xhi_ready")
        xlo_ready = sem("xlo_ready")
        lgT_done = sem("lgT_done")
        lgT_copied = sem("lgT_copied")
        lg_done = sem("lg_done")
        lsub_ready = sem("lsub_ready")
        lexp_ready = sem("lexp_ready")
        chain = sem("route_chain")
        scale_ready = sem("scale_ready")
        scT_done = sem("scT_done")
        scT_copied = sem("scT_copied")
        sc_stored = sem("sc_stored")
        scB_loaded = [sem(f"scB_loaded{j}") for j in range(2)]
        up_done = sem("up_done")
        ts_ready = sem("ts_ready")
        sil_ready = sem("sil_ready")
        hid_ready = sem("hid_ready")
        hhi_ready = sem("hhi_ready")
        hlo_ready = sem("hlo_ready")
        down_done = sem("down_done")
        y_read = sem("y_read")
        stored = sem("stored")
        CH = 7

        block = ctx.enter_context(nc.Block())
        x_v = src.rearrange("(n j p) d -> n p j d", j=TPB, p=P)
        o_v = dst.rearrange("(n j p) d -> n p j d", j=TPB, p=P)
        sets = [(w1.rearrange("e (c p) h -> p c e h", p=P), w1s),
                (w3.rearrange("e (c p) h -> p c e h", p=P), w3s),
                (w2.rearrange("e h d -> h e d"), w2s)]

        def flat(w, part):
            a = w[:, part]
            return a.rearrange("p c e h -> p (c e h)") if len(a.shape) == 4 else a.rearrange("p e d -> p (e d)")

        @block.sync
        def _(sp):
            def load_x(m, i, c):
                wait(sp, xn_ready, m - 1)
                sp.dma_start(xin[:, c % 2], x_v[m]).then_inc(x_loaded[c % 2], 16)

            def load_res(n):
                wait(sp, stored, 16 * n)
                sp.dma_start(xres[:], x_v[n]).then_inc(res_loaded, 16)

            def store(n):
                sp.wait_ge(y_read, n + 1)
                sp.dma_start(o_v[n], xres[:]).then_inc(stored, 16)

            def spread(m, c):
                sp.wait_ge(scT_copied, m + 1)
                sp.dma_start(s_dram, scT[:]).then_inc(sc_stored, 16)
                sp.wait_ge(sc_stored, 16 * (m + 1))
                pass_by(sp, passed)
                wait(sp, ts_ready, E * (m - 1))
                for h in range(2):
                    sp.dma_start(scB[:, c % 2, 4 * h:4 * h + 4], s_dram[4 * h:4 * h + 4].partition_broadcast(P))\
                      .then_inc(scB_loaded[h], 16)

            sp.dma_start(gstage[:], gate_w.rearrange("(c p) e -> p c e", p=P)).then_inc(s_w[0], 16)
            load_x(0, 0, 0)
            load_x(1, 0, 1)
            for k, (w, _) in enumerate(sets):
                if k == 2:
                    sp.wait_ge(w_lo, 2)
                o = stage[:, k % 2].rearrange("p (c e h) -> p c e h", c=KC, e=E) if k < 2 else \
                    stage[:, 0].rearrange("p (e d) -> p e d", e=E)
                if k < 2:
                    for q in range(KC):
                        sp.dma_start(o[:, q], w[:, q]).then_inc(s_w[1], 16)
                        sp.wait_ge(s_w[1], 16 * (2 * k + q + 1))
                else:
                    sp.dma_start(o, w).then_inc(s_w[1], 16)
            load_res(0)
            spread(0, 0)

            def body(i, c, n):
                n = 2 * i + c if n is None else n
                if not (isinstance(n, int) and n == 0):
                    store(n - 1)
                    load_res(n)
                if not (isinstance(n, int) and n + 2 >= NB):
                    load_x(n + 2, i, c + 2)
                if not (isinstance(n, int) and n + 1 >= NB):
                    spread(n + 1, c + 1)

            blocks_of(sp, body, NB)
            store(NB - 1)
            sp.wait_ge(stored, 16 * NB)

        @block.tensor
        def _(pe):
            TERMS = [(0, 0), (0, 1), (1, 0)]

            def transposes(m):
                pe.wait_ge(xn_ready, m + 1)
                wait(pe, scT_copied, m)
                for j in range(TPB):
                    for q in range(KC):
                        last = pe.transpose(tr[:, q, j * P:(j + 1) * P], xn[:, j, q * P:(q + 1) * P], ident[:])
                last.then_inc(xT_done, 1)

            def logits(m, c):
                pe.wait_ge(xhi_ready, m + 1)
                pe.wait_ge(xlo_ready, m + 1)
                for k, (a, b) in enumerate(TERMS):
                    for q in range(KC):
                        last = pe.matmul(tr[0:E, 0, :], gws[:, a, q, :], (xhi, xlo)[b][:, c % 2, q, :],
                                         start=(k == 0 and q == 0), stop=(k == 2 and q == KC - 1))
                last.then_inc(lgT_done, 1)

            def logits_back(m):
                pe.wait_ge(lgT_copied, m + 1)
                pass_by(pe, passed)
                for j in range(TPB):
                    last = pe.transpose(tr[:, 1, j * E:(j + 1) * E], lgT[:, j * P:(j + 1) * P], ident[0:E, 0:E])
                last.then_inc(lg_done, 1)

            def scales_up(m):
                pe.wait_ge(scale_ready, m + 1)
                for j in range(TPB):
                    last = pe.transpose(tr[0:E, 0, j * P:(j + 1) * P], scale[:, j, :], ident[:])
                last.then_inc(scT_done, 1)

            def expert_up(n, c, k):
                g = E * n + k
                if k == 0:
                    pe.wait_ge(xhi_ready, n + 1)
                    pe.wait_ge(xlo_ready, n + 1)
                wait(pe, ts_ready, g - 1)
                for o, w in enumerate((w1s, w3s)):
                    for t, (a, b) in enumerate(TERMS):
                        for q in range(KC):
                            last = pe.matmul(up[:, k % 2, o, :], w[:, a, q, k, :], (xhi, xlo)[b][:, c % 2, q, :],
                                             start=(t == 0 and q == 0), stop=(t == 2 and q == KC - 1))
                last.then_inc(up_done, 1)

            def expert_down(n, k):
                g = E * n + k
                pe.wait_ge(hhi_ready, g + 1)
                pe.wait_ge(hlo_ready, g + 1)
                if k == 0:
                    wait(pe, y_read, n)
                for j in range(TPB):
                    for t, (a, b) in enumerate(TERMS):
                        last = pe.matmul(yb[:, j, :], (hhi, hlo)[b][:, k % 4, j * P:(j + 1) * P], w2s[:, a, k, :],
                                         start=(k == 0 and t == 0 and j % 2 == 0),
                                         stop=(k == E - 1 and t == 2), skip_group_check=True)
                last.then_inc(down_done, 1)

            pe.wait_ge(consts, 1)
            pe.wait_ge(id_set, 2)
            transposes(0)
            pe.wait_ge(w_hi, 1)
            pe.wait_ge(w_lo, 1)
            logits(0, 0)
            logits_back(0)
            scales_up(0)
            pe.wait_ge(w_hi, 4)
            pe.wait_ge(w_lo, 4)

            def body(i, c, n):
                n = 2 * i + c if n is None else n
                first, last = isinstance(n, int) and n == 0, isinstance(n, int) and n + 1 >= NB
                for k in range(E):
                    if k == 3 and not last:
                        logits_back(n + 1)
                    expert_up(n, c, k)
                    if k >= 2:
                        expert_down(n, k - 2)
                    elif not first:
                        expert_down(n - 1, E + k - 2)
                    if not last:
                        if k == 0:
                            transposes(n + 1)
                        if k == 1:
                            logits(n + 1, c + 1)
                        if k == 5:
                            scales_up(n + 1)

            blocks_of(pe, body, NB)
            expert_down(NB - 1, E - 2)
            expert_down(NB - 1, E - 1)

        @block.vector
        def _(dve):
            def ln_stats(m, c, i):
                dve.wait_ge(x_loaded[c % 2], 16 * (i + c // 2 + 1))
                wait(dve, rstd_ready, m)
                wait(dve, xn_ready, m)
                for j in range(TPB):
                    dve.bn_stats(stats[:, j, :], xin[:, c % 2, j, :]).then_inc(stats_part, 1)
                dve.wait_ge(stats_part, TPB * (m + 1))
                pass_by(dve, passed)
                for j in range(TPB):
                    last = dve.bn_aggr(mv[:, j, :], stats[:, j, :])
                last.then_inc(stats_ready, 1)

            def normalize(m, c):
                dve.wait_ge(rstd_ready, m + 1)
                wait(dve, xT_done, m)
                for j in range(TPB):
                    last = dve.tensor_scalar(xn[:, j, :], xin[:, c % 2, j, :], mv[:, j, 0:1], rstd[:, j:j + 1],
                                             ALU.subtract, ALU.mult)
                last.then_inc(xn_ready, 1)

            def low_part(m, c):
                dve.wait_ge(xhi_ready, m + 1)
                wait(dve, up_done, E * (m - 1))
                dve.tensor_tensor(xlo[:, c % 2], tr[:], xhi[:, c % 2].bitcast(F32), ALU.subtract).then_inc(xlo_ready, 1)

            def logits_copy(m):
                dve.wait_ge(lgT_done, m + 1)
                wait(dve, lg_done, m)
                dve.tensor_copy(lgT[:], tr[0:E, 0, :]).then_inc(lgT_copied, 1)

            def minus_max(m):
                dve.wait_ge(lg_done, m + 1)
                lg = tr[:, 1, 0:TPB * E].rearrange("p (j e) -> p j e", e=E)
                dve.tensor_reduce(lmax[:], lg, AX.X, ALU.max).then_inc(chain, 1)
                dve.wait_ge(chain, CH * m + 1)
                wait(dve, lexp_ready, m)
                dve.tensor_tensor(lsub[:], lg, lmax[:].unsqueeze(2).broadcast_to([P, TPB, E]), ALU.subtract)\
                   .then_inc(lsub_ready, 1)

            def top_two(m):
                dve.wait_ge(lexp_ready, m + 1)
                dve.tensor_reduce(lsum[:], lexp[:], AX.X, ALU.add).then_inc(chain, 1)
                dve.wait_ge(chain, CH * m + 2)
                dve.reciprocal(linv[:], lsum[:]).then_inc(chain, 1)
                dve.wait_ge(chain, CH * m + 3)
                dve.tensor_tensor(score[:, :, 0:E], lexp[:], linv[:].unsqueeze(2).broadcast_to([P, TPB, E]),
                                  ALU.mult).then_inc(chain, 1)
                dve.wait_ge(chain, CH * m + 4)
                pass_by(dve, passed)
                for j in range(TPB):
                    last = dve.max(top[:, j, :], score[:, j, 0:E])
                last.then_inc(chain, 1)
                dve.wait_ge(chain, CH * m + 5)
                dve.memset(top[:, :, 2:8], -1.0).then_inc(chain, 1)
                dve.wait_ge(chain, CH * m + 6)
                pass_by(dve, passed)
                for j in range(TPB):
                    last = dve.match_replace(rest[:, j, :], top[:, j, :], score[:, j, :], 0.0)
                last.then_inc(chain, 1)
                dve.wait_ge(chain, CH * m + 7)
                wait(dve, scT_done, m)
                dve.tensor_tensor(scale[:], score[:, :, 0:E], rest[:, :, 0:E], ALU.subtract).then_inc(scale_ready, 1)

            def scales_copy(m):
                dve.wait_ge(scT_done, m + 1)
                wait(dve, sc_stored, 16 * m)
                dve.tensor_copy(scT[:], tr[0:E, 0, :]).then_inc(scT_copied, 1)

            def scaled(n, c, k):
                g = E * n + k
                dve.wait_ge(up_done, g + 1)
                if k % 4 == 0:
                    dve.wait_ge(scB_loaded[k // 4], 16 * (n + 1))
                wait(dve, hid_ready, g - 1)
                s = scB[:, c % 2, k, :].unsqueeze(1).broadcast_to([P, 2, TB])
                dve.tensor_tensor(ts[:, k % 2], up[:, k % 2], s, ALU.mult).then_inc(ts_ready, 1)

            def hidden(n, k):
                g = E * n + k
                dve.wait_ge(sil_ready, g + 1)
                dve.wait_ge(ts_ready, g + 1)
                wait(dve, hlo_ready, g - 1)
                dve.tensor_tensor(hid[:, k % 2], ts[:, k % 2, 1], sil[:, k % 2], ALU.mult).then_inc(hid_ready, 1)

            def residual(n):
                dve.wait_ge(down_done, E * (n + 1))
                dve.wait_ge(res_loaded, 16 * (n + 1))
                dve.scalar_tensor_tensor(xres[:], yb[:], 0.5, xres[:], ALU.mult, ALU.add).then_inc(y_read, 1)

            def split_weights(k, n):
                dve.wait_ge(w_hi, k + 1)
                hi, lo = (gws[:, 0], gws[:, 1]) if k == 0 else (flat(sets[k - 1][1], 0), flat(sets[k - 1][1], 1))
                raw = gstage[:] if k == 0 else stage[:, (k - 1) % 2]
                dve.tensor_tensor(lo, raw, hi.bitcast(F32), ALU.subtract).then_inc(w_lo, 1)

            dve.memset(score[:], -1.0).then_inc(consts, 1)
            split_weights(0, 0)
            ln_stats(0, 0, 0)
            normalize(0, 0)
            low_part(0, 0)
            split_weights(1, 0)
            logits_copy(0)
            minus_max(0)
            split_weights(2, 0)
            dve.wait_ge(consts, 1)
            top_two(0)
            scales_copy(0)
            split_weights(3, 0)
            ln_stats(1, 1, 0)
            normalize(1, 1)

            def body(i, c, n):
                n = 2 * i + c if n is None else n
                first, last = isinstance(n, int) and n == 0, isinstance(n, int) and n + 1 >= NB
                for k in range(E):
                    if k > 0:
                        hidden(n, k - 1)
                    elif not first:
                        hidden(n - 1, E - 1)
                    scaled(n, c, k)
                    if k == 1 and not first:
                        residual(n - 1)
                    if not last:
                        if k == 0:
                            low_part(n + 1, c + 1)
                        if k == 1:
                            logits_copy(n + 1)
                        if k == 3:
                            minus_max(n + 1)
                        if k == 4:
                            top_two(n + 1)
                        if k == 6:
                            scales_copy(n + 1)
                    if not (isinstance(n, int) and n + 2 >= NB):
                        if k == 5:
                            ln_stats(n + 2, c + 2, i)
                        if k == 7:
                            normalize(n + 2, c + 2)

            blocks_of(dve, body, NB)
            hidden(NB - 1, E - 1)
            residual(NB - 1)

        @block.scalar
        def _(act):
            def high_part(m, c):
                act.wait_ge(xT_done, m + 1)
                wait(act, up_done, E * (m - 1))
                act.activation(xhi[:, c % 2], tr[:], ACT.Copy).then_inc(xhi_ready, 1)

            def exps(m):
                act.wait_ge(lsub_ready, m + 1)
                act.activation(lexp[:], lsub[:], ACT.Exp).then_inc(lexp_ready, 1)

            def silu(n, k):
                g = E * n + k
                act.wait_ge(ts_ready, g + 1)
                wait(act, hid_ready, g - 1)
                act.activation(sil[:, k % 2], ts[:, k % 2, 0], ACT.Silu).then_inc(sil_ready, 1)

            def high_hidden(n, k):
                g = E * n + k
                act.wait_ge(hid_ready, g + 1)
                wait(act, down_done, g - 3)
                act.activation(hhi[:, k % 4], hid[:, k % 2], ACT.Copy).then_inc(hhi_ready, 1)

            def round_weights(k):
                if k == 0:
                    act.wait_ge(s_w[0], 16)
                    act.activation(gws[:, 0], gstage[:], ACT.Copy).then_inc(w_hi, 1)
                    return
                act.wait_ge(s_w[1], (32, 64, 80)[k - 1])
                act.activation(flat(sets[k - 1][1], 0), stage[:, (k - 1) % 2], ACT.Copy).then_inc(w_hi, 1)

            round_weights(0)
            high_part(0, 0)
            round_weights(1)
            exps(0)
            round_weights(2)
            round_weights(3)

            def body(i, c, n):
                n = 2 * i + c if n is None else n
                first, last = isinstance(n, int) and n == 0, isinstance(n, int) and n + 1 >= NB
                for k in range(E):
                    if k > 0:
                        high_hidden(n, k - 1)
                    elif not first:
                        high_hidden(n - 1, E - 1)
                    silu(n, k)
                    if not last:
                        if k == 0:
                            high_part(n + 1, c + 1)
                        if k == 3:
                            exps(n + 1)

            blocks_of(act, body, NB)
            high_hidden(NB - 1, E - 1)

        @block.gpsimd
        def _(pool):
            pool.memset(ident[:], 0.0).then_inc(id_set, 1)
            pool.memset(mhalf[:], -0.5).then_inc(rstd_part, 1)
            pool.wait_ge(id_set, 1)
            pool.affine_select(out=ident[:], in_=ident[:], compare_op=ALU.not_equal, fill=1.0, base=0,
                               pattern=[[-1, P]], channel_multiplier=1).then_inc(id_set, 1)

            def inverse_std(m):
                pool.wait_ge(stats_ready, m + 1)
                wait(pool, xn_ready, m)
                pass_by(pool, passed)
                pool.tensor_scalar(var_eps[:], mv[:, :, 1], EPS, None, ALU.add).then_inc(rstd_part, 1)
                pool.wait_ge(rstd_part, m + 2)
                pool.tensor_tensor(rstd[:], var_eps[:], mhalf[:], ALU.pow).then_inc(rstd_ready, 1)

            def low_hidden(n, k):
                g = E * n + k
                pool.wait_ge(hhi_ready, g + 1)
                wait(pool, down_done, g - 3)
                pool.tensor_tensor(hlo[:, k % 4], hid[:, k % 2], hhi[:, k % 4].bitcast(F32), ALU.subtract)\
                    .then_inc(hlo_ready, 1)

            inverse_std(0)
            inverse_std(1)

            def body(i, c, n):
                n = 2 * i + c if n is None else n
                first, last = isinstance(n, int) and n == 0, isinstance(n, int) and n + 1 >= NB
                if not first:
                    low_hidden(n - 1, E - 1)
                for k in range(1, E):
                    low_hidden(n, k - 1)
                    if k == 6 and not (isinstance(n, int) and n + 2 >= NB):
                        inverse_std(n + 2)

            blocks_of(pool, body, NB)
            low_hidden(NB - 1, E - 1)


def attention(nc, name, src, dst, n_dram, t_dram, wq, wk, wv, wb, cq, ck, cv, rms_w, wo):
    ctx = ExitStack()
    H, D, KW = 4, 64, 4
    NS = L // P
    PR = H // 2
    SB = 16
    NBK = P // SB
    BP = NBK * 2 * H
    PRODUCTS = [(16, "X"), (16, "T"), (16, "U"), (32, "X"), (32, "U"), (32, "T"), (64, "X"), (64, "U")]
    NP = len(PRODUCTS)
    NQ = 10
    T0 = NQ - NP
    with ctx:
        def sb(n, shape, dt=F32):
            return ctx.enter_context(nc.sbuf_tensor(f"{name}_{n}", shape, dt))

        def sem(n):
            return ctx.enter_context(nc.semaphore(f"{name}_{n}"))

        def sems(n, k):
            return [sem(f"{n}{j}") for j in range(k)]

        wqkv = sb("wqkv", [P, 2, KC, 3, DM], F32R)
        wbs = sb("wbs", [P, 2, KC, H], F32R)
        wos = sb("wos", [P, 2, PR, DM], F32R)
        wstage = sb("wstage", [P, 4, KC, DM])
        bstage = sb("bstage", [P, KC, H])
        rms2 = sb("rms2", [P, 1])
        taps = sb("taps", [P, 3, PR, KW])
        ident = sb("ident", [P, P])
        below = sb("below", [P, P])
        upto = sb("upto", [P, P])
        quarter = sb("quarter", [P, P])
        eye = sb("eye", [BP, SB, SB])
        powers = sb("powers", [P, 2, 2 * H])
        xin = sb("xin", [P, 2, 2, DM])
        stats = sb("stats", [P, 2, 6])
        mv = sb("mv", [P, 2, 2])
        var_eps = sb("var_eps", [P, 2])
        rstd = sb("rstd", [P, 2])
        xn = sb("xn", [P, 2, DM])
        xhi = sb("xhi", [P, KC, 2 * P], F32R)
        xlo = sb("xlo", [P, KC, 2 * P], F32R)
        raw = sb("raw", [P, 3, PR, 2, KW - 1 + P])
        acc = sb("acc", [P, 3, PR, 2, P])
        bth = sb("bth", [H, 2 * P])
        beta = sb("beta", [P, 2, H])
        kq = sb("kq", [P, 4, PR, 2, 2, P])
        kx = sb("kx", [P, PR, 2, 2, P])
        vch = sb("vch", [P, PR, 2, P])
        sq = sb("sq", [P, 2, 2, DM])
        ss = sb("ss", [P, 4, 2, 2, H])
        kn = sb("kn", [P, 2, H])
        rk = sb("rk", [P, 2, H])
        cc = sb("cc", [P, 4, 2, H])
        ktok = sb("ktok", [P, 4, 2, DM])
        vtok = sb("vtok", [P, 2 * DM])
        vn = sb("vn", [P, 4, 2, DM])
        nn = sb("nn", [P, 2, 2, H, P])
        at = sb("at", [P, 4, 2, H, P])
        small = sb("small", [BP, SB, SB])
        term = sb("term", [BP, SB, SB])
        inv = sb("inv", [BP, 2, SB, SB])
        tb = sb("tb", [P, 2, 2, H, P])
        tt = sb("tt", [P, 2, H, P])
        tu = sb("tu", [P, 2, H, P])
        xt = sb("xt", [P, 2, H, P])
        x32 = sb("x32", [P, 2, H, P])
        x64 = sb("x64", [P, 2, H, P // 2])
        tc = sb("tc", [P, 2, H, P])
        state = sb("state", [P, 2, PR, P])
        rr = sb("rr", [P, 2, DM])
        mid = sb("mid", [P, 2, H, P])
        osq = sb("osq", [P, 2, DM])
        oms = sb("oms", [P, 2, H])
        ovar = sb("ovar", [P, 2, H])
        oeps = sb("oeps", [P, 2, H])
        osum = sb("osum", [P, 2, H])
        og = sb("og", [P, 2, H])
        on = sb("on", [P, 2, DM])
        othi = sb("othi", [P, PR, 2, P], F32R)
        otlo = sb("otlo", [P, PR, 2, P], F32R)
        xres = sb("xres", [P, 2, DM])

        def pt(n, shape):
            return ctx.enter_context(nc.psum_tensor(f"{name}_{n}", shape, F32))

        fr = pt("fr", [P, 3, 512])
        tp = pt("tp", [P, 2, 512])
        sc = pt("sc", [P, 2, 512])
        ob = pt("ob", [P, 512])

        w_loaded, w_scaled, w_hi, w_lo, masks, zeroed = (sem(n) for n in (
            "w_loaded", "w_scaled", "w_hi", "w_lo", "masks", "zeroed"))
        x_loaded = sems("x_loaded", 2)
        (stats_part, stats_ready, rstd_part, rstd_ready, xn_ready, xT_done, xhi_ready, xlo_ready, qkv_done,
         beta_done, hist_ready, raw_ready, tap0_ready, conv_step, bth_ready, bT_done, beta_ready, silu_ready,
         kx_ready, turned, sq_ready, ss_ready, ktok_ready, kn_ready, rk_ready, cc_ready, vtok_ready, vn_ready) = (sem(n) for n in (
             "stats_part", "stats_ready", "rstd_part", "rstd_ready", "xn_ready", "xT_done", "xhi_ready", "xlo_ready",
             "qkv_done", "beta_done", "hist_ready", "raw_ready", "tap0_ready", "conv_step", "bth_ready", "bT_done",
             "beta_ready", "silu_ready", "kx_ready", "turned", "sq_ready", "ss_ready", "ktok_ready", "kn_ready",
             "rk_ready", "cc_ready", "vtok_ready", "vn_ready"))
        gram_done, gram_read, prod_done, prod_read = (
            sems(n, 2) for n in ("gram_done", "gram_read", "prod_done", "prod_read"))
        blocks_out, blocks_in, solve_step, inv_out, tb_ready, tc_part = (sem(n) for n in (
            "blocks_out", "blocks_in", "solve_step", "inv_out", "tb_ready", "tc_part"))
        passed = sem("passed")
        ks_done, r_ready, mid_done, mid_ready, ds_done, s_ready = (
            sems(n, 2) for n in ("ks_done", "r_ready", "mid_done", "mid_ready", "ds_done", "s_ready"))
        osum_ready = sem("osum_ready")
        (o_done, osq_ready, oms_ready, ovar_part, og_ready, on_ready, oT_done, othi_ready, otlo_ready, y_done,
         y_read, res_loaded, stored) = (sem(n) for n in (
             "o_done", "osq_ready", "oms_ready", "ovar_part", "og_ready", "on_ready", "oT_done", "othi_ready",
             "otlo_ready", "y_done", "y_read", "res_loaded", "stored"))

        block = ctx.enter_context(nc.Block())
        x_v = src.rearrange("(s n p) d -> n p s d", s=2, p=P)
        o_v = dst.rearrange("(s n p) d -> n p s d", s=2, p=P)
        TERMS = [(0, 0), (0, 1), (1, 0)]
        WSETS = [wk, wv, wq]
        SOLVE = 2 * SB - 2

        def after(f):
            m, par, turn = f
            return m + 1, (par + 1) % 4, turn + par % 2

        def steps_of(eng, body):
            def go(i, c, f, g, t, s):
                body(*(((4 * i + c + d), (c + d) % 4, 2 * i + (c + d) // 2) if on else None
                       for d, on in ((3, f), (2, g), (1, t), (0, s))))
            for c in range(1, 4):
                go(-1, c, True, c > 1, c > 2, False)
            for c in range(4):
                go(0, c, True, True, True, True)
            with eng.Fori(1, NS // 4 - 1) as i:
                for c in range(4):
                    go(i, c, True, True, True, True)
            for c in range(4):
                go(NS // 4 - 1, c, c < 1, c < 2, c < 3, True)

        @block.sync
        def _(sp):
            def hold(sem, value):
                wait(sp, sem, value)
                pass_by(sp, passed)

            sp.dma_start(wstage[:, 3], wo.rearrange("(c p) n -> p c n", p=P)).then_inc(w_loaded, 16)
            for j, w in enumerate(WSETS):
                sp.dma_start(wstage[:, j], w.rearrange("(c p) n -> p c n", p=P)).then_inc(w_loaded, 16)
            sp.dma_start(bstage[:], wb.rearrange("(c p) n -> p c n", p=P)).then_inc(w_loaded, 16)
            for j, w in enumerate((ck, cv, cq)):
                sp.dma_start(taps[:, j], w.rearrange("(r p) o k -> p r (o k)", p=P)).then_inc(w_loaded, 16)
            for h in range(2):
                sp.dma_start(rms2[h * D:(h + 1) * D, :], rms_w.rearrange("(d o) -> d o", o=1)).then_inc(w_loaded, 16)

            def load_x(f):
                m, par, _ = f
                hold(xn_ready, m - 1)
                sp.dma_start(xin[:, par % 2], x_v[m]).then_inc(x_loaded[par % 2], 16)

            def spread_blocks(g):
                m, par, _ = g
                for s in range(2):
                    hold(gram_read[s], PR * (m + 1))
                for b in range(NBK):
                    a = slice(b * SB, (b + 1) * SB)
                    sp.dma_start(n_dram[b].rearrange("g r c -> r g c"),
                                 nn[a, par % 2].rearrange("p s h t -> p (s h) t")[:, :, a]).then_inc(blocks_out, 16)

            def take_blocks(g):
                m = g[0]
                hold(blocks_out, 16 * NBK * (m + 1))
                hold(solve_step, SOLVE * m)
                sp.dma_start(small[:], n_dram.rearrange("b g r c -> (b g) r c")).then_inc(blocks_in, 16)

            def collect_inverses(g):
                m = g[0]
                hold(solve_step, SOLVE * (m + 1))
                hold(tb_ready, 16 * NBK * m)
                for u in range(2):
                    sp.dma_start(t_dram[:, u].rearrange("b g r c -> b g (r c)"), inv[:, u].rearrange("p r c -> p (r c)"))\
                      .then_inc(inv_out, 16)
                for s in range(2):
                    hold(prod_read[s], NP * (m - 1) + 3)
                hold(inv_out, 32 * (m + 1))
                for b in range(NBK):
                    a = slice(b * SB, (b + 1) * SB)
                    sp.dma_start(tb[a].rearrange("p u s h t -> p (u s h) t")[:, :, a],
                                 t_dram[b].rearrange("u g r c -> r (u g) c")).then_inc(tb_ready, 16)

            def body(f, g, t, s):
                if g:
                    spread_blocks(g)
                if f and not (isinstance(f[0], int) and f[0] + 1 >= NS):
                    load_x(after(f))
                if s:
                    m = s[0]
                    hold(stored, 16 * m)
                    sp.dma_start(xres[:], x_v[m]).then_inc(res_loaded, 16)
                if g:
                    take_blocks(g)
                if s:
                    hold(y_read, m + 1)
                    sp.dma_start(o_v[m], xres[:]).then_inc(stored, 16)
                if g:
                    collect_inverses(g)

            load_x((0, 0, 0))
            steps_of(sp, body)
            hold(stored, 16 * NS)

        @block.tensor
        def _(pe):
            def x_turn(f):
                m = f[0]
                pe.wait_ge(xn_ready, m + 1)
                wait(pe, vtok_ready, m)
                for q in range(KC):
                    for s in range(2):
                        last = pe.transpose(fr[:, 0, (2 * q + s) * P:(2 * q + s + 1) * P],
                                            xn[:, s, q * P:(q + 1) * P], ident[:])
                last.then_inc(xT_done, 1)

            def project(out, w, col, start):
                for k, (a, b) in enumerate(TERMS):
                    for q in range(KC):
                        last = pe.matmul(out, w[:, a, q, col], (xhi, xlo)[b][:, q, :], skip_group_check=True,
                                         start=(start and k == 0 and q == 0), stop=(k == 2 and q == KC - 1))
                return last

            def qkv(f, j):
                m = f[0]
                if j == 0:
                    pe.wait_ge(xhi_ready, m + 1)
                    pe.wait_ge(xlo_ready, m + 1)
                    wait(pe, sq_ready, m)
                    wait(pe, ktok_ready, m)
                if j == 2:
                    pe.wait_ge(bth_ready, m + 1)
                for r in range(PR):
                    last = project(fr[:, (2, 0, 1)[j], r * 2 * P:(r + 1) * 2 * P],
                                   wqkv[:, :, :, j, :], slice(r * P, (r + 1) * P), r == 0)
                last.then_inc(qkv_done, 1)

            def beta_rows(f):
                m = f[0]
                project(fr[0:H, 1, 0:2 * P], wbs, slice(0, H), True).then_inc(beta_done, 1)

            def beta_turn(f):
                m = f[0]
                pe.wait_ge(bth_ready, m + 1)
                pe.wait_ge(raw_ready, 3 * m + 2)
                pass_by(pe, passed)
                for s in range(2):
                    last = pe.transpose(fr[:, 0, s * H:(s + 1) * H], bth[:, s * P:(s + 1) * P], ident[0:H, 0:H])
                last.then_inc(bT_done, 1)

            def turn_back(f):
                m, par, _ = f
                pe.wait_ge(silu_ready, 3 * (m + 1))
                pe.wait_ge(raw_ready, 3 * (m + 1))
                for s in range(2):
                    for j in range(2):
                        for r in range(PR):
                            last = pe.transpose(fr[:, 1 + s, (2 * j + r) * P:(2 * j + r + 1) * P],
                                                kq[:, par, r, s, j, :], ident[:])
                last.then_inc(turned, 1)
                pe.wait_ge(beta_ready, m + 1)
                for s in range(2):
                    for r in range(PR):
                        last = pe.transpose(fr[:, 0, (2 * s + r) * P:(2 * s + r + 1) * P], vch[:, r, s, :], ident[:])
                last.then_inc(turned, 1)

            def gram(g, q):
                m, par, _ = g
                if q == 0:
                    pe.wait_ge(kx_ready, 2 * (m + 1))
                for s in range(2):
                    wait(pe, gram_read[s], PR * m + q)
                    if q == 0:
                        wait(pe, prod_read[s], NP * (m - 1))
                    for h in range(2):
                        last = pe.matmul(tp[:, s, h * 2 * P:(h + 1) * 2 * P], kx[:, q, s, h, :],
                                         kq[:, par, q, s], start=(h == 0), stop=True, skip_group_check=True)
                    last.then_inc(gram_done[s], 1)

            def product(t, q):
                m, par, _ = t
                if q == 0:
                    pe.wait_ge(tb_ready, 16 * NBK * (m + 1))
                edge, kind = PRODUCTS[q]
                for s in range(2):
                    wait(pe, prod_read[s], NP * m + q)
                    if q == 0:
                        pe.wait_ge(gram_read[s], min(PR * (m + 2), PR * NS) if isinstance(m, int) else PR * (m + 2))
                    for h in range(H):
                        n, half = nn[:, par % 2, s, h, :], slice(P // 2, P)
                        out = tp[:, s, h * P:(h + 1) * P]
                        if edge == 16:
                            a, b = {"X": (n, tb[:, 1, s, h, :]), "T": (xt[:, s, h, :], tb[:, 0, s, h, :]),
                                    "U": (tb[:, 0, s, h, :], xt[:, s, h, :])}[kind]
                        elif edge == 32:
                            a, b = {"X": (n, tu[:, s, h, :]), "U": (tt[:, s, h, :], x32[:, s, h, :]),
                                    "T": (x32[:, s, h, 0:64], tt[:, s, h, 0:64])}[kind]
                        else:
                            a, b = {"X": (n[:, 0:64], tu[:, s, h, half]), "U": (tt[:, s, h, 0:64], x64[:, s, h, :])}[kind]
                        if (edge, kind) == (32, "T") or edge == 64:
                            out = tp[0:64, s, h * 64:(h + 1) * 64]
                        last = pe.matmul(out, a, b, start=(h == 0), stop=True, skip_group_check=True)
                    last.then_inc(prod_done[s], 1)

            def state_in(st):
                m, par, _ = st
                for s in range(2):
                    pe.wait_ge(s_ready[s], m + 1)
                    for r in range(PR):
                        last = pe.matmul(sc[:, s, r * P:(r + 1) * P], kq[:, par, r, s, 0, :], state[:, s, r, :],
                                         start=(r == 0), stop=True, skip_group_check=True)
                    last.then_inc(ks_done[s], 1)

            def out_in(st):
                m, par, _ = st
                wait(pe, y_read, m)
                for s in range(2):
                    for r in range(PR):
                        pe.matmul(ob[:, s * DM + r * P:s * DM + (r + 1) * P], kq[:, par, r, s, 1, :],
                                  state[:, s, r, :], start=(s == 0 and r == 0), stop=False, skip_group_check=True)

            def mids(st):
                m = st[0]
                for s in range(2):
                    pe.wait_ge(r_ready[s], m + 1)
                    pe.wait_ge(prod_read[s], NP * (m + 1))
                    for h in range(H):
                        r = h // 2
                        last = pe.matmul(sc[:, s, h * P:(h + 1) * P], tc[:, s, h, :], rr[:, s, r * P:(r + 1) * P],
                                         start=(h == 0), stop=True, skip_group_check=True)
                    last.then_inc(mid_done[s], 1)

            def state_out(st):
                m, par, _ = st
                for s in range(2):
                    pe.wait_ge(mid_ready[s], m + 1)
                    mm = mid[:, s].rearrange("p h (g d) -> p (h g) d", d=D)
                    for r in range(PR):
                        last = pe.matmul(sc[:, s, r * P:(r + 1) * P], ktok[:, par, s, r * P:(r + 1) * P],
                                         mm[:, 4 * r:4 * r + 4:3, :], start=(r == 0), stop=True,
                                         skip_group_check=True)
                    last.then_inc(ds_done[s], 1)

            def outputs(st):
                m, par, _ = st
                for s in range(2):
                    pe.wait_ge(mid_ready[s], m + 1)
                    for h in range(H):
                        r = h // 2
                        last = pe.matmul(ob[:, s * DM + r * P:s * DM + (r + 1) * P], at[:, par, s, h, :],
                                         mid[:, s, h, :], start=False, stop=(h % 2 == 1), skip_group_check=True)
                last.then_inc(o_done, 1)

            def out_turn(st):
                m = st[0]
                pe.wait_ge(on_ready, m + 1)
                for r in range(PR):
                    for s in range(2):
                        last = pe.transpose(ob[:, (2 * r + s) * P:(2 * r + s + 1) * P],
                                            on[:, s, r * P:(r + 1) * P], ident[:])
                last.then_inc(oT_done, 1)

            def out_project(st):
                m = st[0]
                pe.wait_ge(othi_ready, m + 1)
                pe.wait_ge(otlo_ready, m + 1)
                for s in range(2):
                    for k, (a, b) in enumerate(TERMS):
                        for r in range(PR):
                            last = pe.matmul(ob[:, s * DM:(s + 1) * DM], (othi, otlo)[b][:, r, s, :], wos[:, a, r, :],
                                             start=(s == 0 and k == 0 and r == 0), stop=(k == 2 and r == PR - 1),
                                             skip_group_check=True)
                last.then_inc(y_done, 1)

            pe.wait_ge(masks, 1)
            pe.wait_ge(w_hi, 3)
            pe.wait_ge(w_lo, 3)
            pe.wait_ge(zeroed, 5)

            def body(f, g, t, s):
                for q in range(NQ):
                    if s and q == 0:
                        state_in(s)
                    if g and q < PR:
                        gram(g, q)
                    if f:
                        if q == 0:
                            x_turn(f)
                        if q == 2:
                            qkv(f, 1)
                        if q == 9:
                            turn_back(f)
                    if t and q >= T0:
                        product(t, q - T0)
                    if s:
                        if q == 0:
                            out_in(s)
                        if q == 1:
                            mids(s)
                        if q == 3:
                            outputs(s)
                        if q == 5:
                            state_out(s)
                        if q == 6:
                            out_turn(s)
                        if q == 8:
                            out_project(s)
                    if f:
                        if q == 1:
                            qkv(f, 0)
                            beta_rows(f)
                        if q == 4:
                            qkv(f, 2)
                        if q == 6:
                            beta_turn(f)

            steps_of(pe, body)

        @block.vector
        def _(dve):
            def split(k, hi, lo, rawp):
                dve.wait_ge(w_hi, k + 1)
                dve.tensor_tensor(lo, rawp, hi.bitcast(F32), ALU.subtract).then_inc(w_lo, 1)

            def norm_stats(f):
                m, par, turn = f
                dve.wait_ge(x_loaded[par % 2], 16 * (turn + 1))
                wait(dve, xn_ready, m)
                for s in range(2):
                    dve.bn_stats(stats[:, s, :], xin[:, par % 2, s, :]).then_inc(stats_part, 1)
                dve.wait_ge(stats_part, 2 * (m + 1))
                pass_by(dve, passed)
                for s in range(2):
                    last = dve.bn_aggr(mv[:, s, :], stats[:, s, :])
                last.then_inc(stats_ready, 1)

            def norm_in(f):
                m, par, turn = f
                dve.wait_ge(rstd_ready, m + 1)
                wait(dve, xT_done, m)
                for s in range(2):
                    last = dve.tensor_scalar(xn[:, s, :], xin[:, par % 2, s, :], mv[:, s, 0:1], rstd[:, s:s + 1],
                                             ALU.subtract, ALU.mult)
                last.then_inc(xn_ready, 1)

            def x_low(f):
                m = f[0]
                dve.wait_ge(xhi_ready, m + 1)
                dve.tensor_tensor(xlo[:].rearrange("p c t -> p (c t)"), fr[:, 0, :],
                                  xhi[:].rearrange("p c t -> p (c t)").bitcast(F32), ALU.subtract).then_inc(xlo_ready, 1)

            def history(f):
                m = f[0]
                wait(dve, conv_step, 18 * m)
                rv = raw[:].rearrange("p j r s t -> p (j r s) t")
                dve.tensor_copy(rv[:, :, 0:KW - 1], rv[:, :, P:P + KW - 1]).then_inc(hist_ready, 1)

            def conv(f, j, *at_taps):
                m = f[0]
                for tap in at_taps:
                    for r in range(PR):
                        n = 6 * j + 2 * (tap - 1) + r
                        if tap == 1:
                            dve.wait_ge(tap0_ready, 6 * m + 2 * j + r + 1)
                        else:
                            dve.wait_ge(conv_step, 18 * m + n - 1)
                        dve.scalar_tensor_tensor(acc[:, j, r], raw[:, j, r, :, tap:tap + P],
                                                 taps[:, j, r, tap:tap + 1], acc[:, j, r], ALU.mult, ALU.add)\
                           .then_inc(conv_step, 1)

            def betas(f):
                m = f[0]
                dve.wait_ge(bT_done, m + 1)
                wait(dve, cc_ready, m)
                dve.tensor_scalar(beta[:].rearrange("p s h -> p (s h)"), fr[:, 0, 0:2 * H], 0.5, 0.5, ALU.mult,
                                  ALU.add).then_inc(beta_ready, 1)

            def norms(f):
                m, par, _ = f
                dve.wait_ge(sq_ready, m + 1)
                wait(dve, og_ready, m - 3)
                wait(dve, cc_ready, m)
                dve.tensor_reduce(ss[:, par].rearrange("p s j h -> p (s j h)"),
                                  sq[:].rearrange("p s j (h d) -> p (s j h) d", d=D), AX.X, ALU.add).then_inc(ss_ready, 1)
                dve.wait_ge(ss_ready, m + 1)
                dve.reciprocal(rk[:], ss[:, par, :, 0, :]).then_inc(rk_ready, 1)
                dve.wait_ge(rk_ready, m + 1)
                dve.wait_ge(beta_ready, m + 1)
                dve.tensor_tensor(cc[:, par], beta[:], rk[:], ALU.mult).then_inc(cc_ready, 1)

            def gram_out(g, q):
                m, par, _ = g
                for s in range(2):
                    dve.wait_ge(gram_done[s], PR * m + q + 1)
                    if q == 0:
                        dve.wait_ge(cc_ready, m + 1)
                    v = tp[:, s, :].rearrange("p (h j t) -> p h j t", h=2, j=2)
                    for h in range(2):
                        dve.scalar_tensor_tensor(nn[:, par % 2, s, 2 * q + h, :], v[:, h, 0, :],
                                                 cc[:, par, s, 2 * q + h:2 * q + h + 1], below[:],
                                                 ALU.mult, ALU.mult)
                    dve.tensor_tensor(at[:, par, s, 2 * q:2 * q + 2, :], v[:, :, 1, :],
                                      upto[:].unsqueeze(1).broadcast_to([P, 2, P]), ALU.mult)\
                       .then_inc(gram_read[s], 1)

            def product_out(t, q):
                m, par, _ = t
                edge, kind = PRODUCTS[q]
                for s in range(2):
                    prod = tp[:, s, :].rearrange("p (h t) -> p h t", t=P)
                    if edge == 32:
                        continue
                    if (edge, kind) == (64, "X"):
                        continue
                    if (edge, kind) == (64, "U"):
                        dve.wait_ge(tc_part, 2 * m + s + 1)
                        dve.wait_ge(prod_done[s], NP * m + q + 1)
                        half = slice(0, P // 2)
                        dve.scalar_tensor_tensor(tc[half, s, :, P // 2:],
                                                 tp[half, s, 0:2 * P].rearrange("p (h t) -> p h t", h=H), -1.0,
                                                 cc[half, par, s, :].unsqueeze(2).broadcast_to([P // 2, H, P // 2]),
                                                 ALU.mult, ALU.mult).then_inc(prod_read[s], 1)
                        continue
                    dve.wait_ge(prod_done[s], NP * m + q + 1)
                    if kind == "X":
                        dve.tensor_tensor(xt[:, s], prod, quarter[:].unsqueeze(1).broadcast_to([P, H, P]), ALU.mult)\
                           .then_inc(prod_read[s], 1)
                    elif kind == "T":
                        dve.tensor_tensor(tt[:, s], tb[:, 0, s], prod, ALU.subtract).then_inc(prod_read[s], 1)
                    else:
                        dve.tensor_tensor(tu[:, s], tb[:, 1, s], prod, ALU.subtract).then_inc(prod_read[s], 1)

            def scale_inverse(t):
                m, par, _ = t
                for s in range(2):
                    dve.wait_ge(prod_read[s], NP * m + 5)
                    wait(dve, mid_done[s], m)
                    dve.tensor_tensor(tc[:, s], tu[:, s], cc[:, par, s, :].unsqueeze(2).broadcast_to([P, H, P]),
                                      ALU.mult).then_inc(tc_part, 1)

            def remainder(st):
                m, par, _ = st
                for s in range(2):
                    dve.wait_ge(ks_done[s], m + 1)
                    dve.wait_ge(vn_ready, m + 1)
                    dve.tensor_tensor(rr[:, s, :], vn[:, par, s, :], sc[:, s, 0:DM], ALU.subtract)\
                       .then_inc(r_ready[s], 1)

            def state_add(st):
                m = st[0]
                for s in range(2):
                    dve.wait_ge(ds_done[s], m + 1)
                    d = sc[:, s, 0:DM].rearrange("p (r c) -> p r c", c=P)
                    for h in range(2):
                        a = slice(h * D, (h + 1) * D)
                        last = dve.tensor_tensor(state[a, s, :, a], state[a, s, :, a], d[a, :, a], ALU.add)
                    last.then_inc(s_ready[s], 1)

            def out_norm(st):
                m, par, _ = st
                dve.wait_ge(osq_ready, m + 1)
                wait(dve, ovar_part, 2 * m)
                dve.tensor_reduce(oms[:].rearrange("p s h -> p (s h)"),
                                  osq[:].rearrange("p s (h d) -> p (s h) d", d=D), AX.X, ALU.add).then_inc(oms_ready, 1)

            def out_scale(st):
                m = st[0]
                dve.wait_ge(og_ready, m + 1)
                wait(dve, oT_done, m)
                dve.tensor_tensor(on[:].rearrange("p s (h d) -> p (s h) d", d=D),
                                  ob[:].rearrange("p (g d) -> p g d", d=D),
                                  og[:].rearrange("p s h -> p (s h)").unsqueeze(2).broadcast_to([P, 2 * H, D]),
                                  ALU.mult).then_inc(on_ready, 1)

            def out_low(st):
                m = st[0]
                dve.wait_ge(othi_ready, m + 1)
                dve.tensor_tensor(otlo[:].rearrange("p r s t -> p (r s t)"), ob[:],
                                  othi[:].rearrange("p r s t -> p (r s t)").bitcast(F32), ALU.subtract)\
                   .then_inc(otlo_ready, 1)

            def residual(st):
                m = st[0]
                dve.wait_ge(y_done, m + 1)
                dve.wait_ge(res_loaded, 16 * (m + 1))
                dve.tensor_tensor(xres[:].rearrange("p s d -> p (s d)"), ob[:], xres[:].rearrange("p s d -> p (s d)"),
                                  ALU.add).then_inc(y_read, 1)

            dve.memset(raw[:], 0.0).then_inc(zeroed, 1)
            for s in range(2):
                dve.memset(state[:, s], 0.0).then_inc(s_ready[s], 1)
            for buf in (mid, tb, x32, x64):
                dve.memset(buf[:], 0.0).then_inc(zeroed, 1)
            dve.wait_ge(w_loaded, 16 * 10)
            dve.tensor_scalar(wstage[:, 3], wstage[:, 3], rms2[:, 0:1], None, ALU.mult).then_inc(w_scaled, 1)
            dve.wait_ge(w_scaled, 1)
            split(0, wqkv[:, 0].rearrange("p c j d -> p j c d"), wqkv[:, 1].rearrange("p c j d -> p j c d"), wstage[:, 0:3])
            split(1, wbs[:, 0], wbs[:, 1], bstage[:])
            split(2, wos[:, 0], wos[:, 1], wstage[:, 3])
            dve.wait_ge(zeroed, 5)
            dve.wait_ge(masks, 1)
            norm_stats((0, 0, 0))
            norm_in((0, 0, 0))

            def body(f, g, t, s):
                more = f and not (isinstance(f[0], int) and f[0] + 1 >= NS)
                for q in range(NQ):
                    if s and q == 0:
                        remainder(s)
                    if g and q < PR:
                        gram_out(g, q)
                    if f and q == 0:
                        x_low(f)
                        history(f)
                    if s and q == 8:
                        residual(s)
                    if t and q >= T0:
                        product_out(t, q - T0)
                    if s:
                        if q == 4:
                            out_norm(s)
                        if q == 5:
                            state_add(s)
                            out_scale(s)
                        if q == 6:
                            out_low(s)
                    if f:
                        if q == 1:
                            conv(f, 0, 1)
                        if q == 2:
                            conv(f, 0, 2, 3)
                        if q == 3:
                            conv(f, 1, 1, 2)
                        if q == 4:
                            conv(f, 1, 3)
                        if q == 5:
                            conv(f, 2, 1, 2)
                        if q == 6:
                            conv(f, 2, 3)
                            betas(f)
                    if more and q == 4:
                        norm_stats(after(f))
                    if t and q == 7:
                        scale_inverse(t)
                    if more and q == 7:
                        norm_in(after(f))
                    if f and q == 9:
                        norms(f)

            steps_of(dve, body)

        @block.scalar
        def _(act):
            def x_high(f):
                m = f[0]
                act.wait_ge(xT_done, m + 1)
                wait(act, qkv_done, 3 * m)
                act.activation(xhi[:].rearrange("p c t -> p (c t)"), fr[:, 0, :], ACT.Copy).then_inc(xhi_ready, 1)

            def raw_out(f, j):
                m = f[0]
                act.wait_ge(qkv_done, 3 * m + j + 1)
                act.wait_ge(hist_ready, m + 1)
                act.activation(raw[:, j].rearrange("p r s t -> p (r s) t")[:, :, KW - 1:],
                               fr[:, (2, 0, 1)[j], :].rearrange("p (g t) -> p g t", t=P), ACT.Copy).then_inc(raw_ready, 1)

            def tap0(f, j):
                m = f[0]
                act.wait_ge(raw_ready, 3 * m + j + 1)
                wait(act, silu_ready, 3 * m)
                wait(act, kx_ready, 2 * m)
                for r in range(PR):
                    act.activation(acc[:, j, r], raw[:, j, r, :, 0:P], ACT.Copy, scale=taps[:, j, r, 0:1])\
                       .then_inc(tap0_ready, 1)

            def beta_tanh(f):
                m = f[0]
                act.wait_ge(beta_done, m + 1)
                wait(act, bT_done, m)
                act.activation(bth[:], fr[0:H, 1, 0:2 * P], ACT.Tanh, scale=0.5).then_inc(bth_ready, 1)

            def silus(f, j):
                m, par, _ = f
                act.wait_ge(conv_step, 18 * m + 6 * (j + 1))
                if j == 0:
                    wait(act, o_done, m - 3)
                    wait(act, turned, 2 * m)
                out = (kq[:, par, :, :, 0, :], vch[:], kq[:, par, :, :, 1, :])[j]
                act.activation(out, acc[:, j], ACT.Silu).then_inc(silu_ready, 1)
                if j == 0:
                    for s in range(2):
                        wait(act, gram_done[s], PR * m)
                    for h in range(2):
                        a = slice(h * D, (h + 1) * D)
                        act.activation(kx[a, :, :, h, :], acc[a, 0], ACT.Silu).then_inc(kx_ready, 1)

            def squares(f):
                m, par, _ = f
                act.wait_ge(turned, 2 * m + 1)
                wait(act, ss_ready, m)
                act.activation(sq[:].rearrange("p s j d -> p s (j d)"), fr[:, 1:3, :], ACT.Square).then_inc(sq_ready, 1)
                wait(act, ds_done[1], m - 3)
                act.activation(ktok[:, par], fr[:, 1:3, 0:DM], ACT.Copy).then_inc(ktok_ready, 1)
                act.wait_ge(turned, 2 * (m + 1))
                wait(act, vn_ready, m)
                act.activation(vtok[:], fr[:, 0, :], ACT.Copy).then_inc(vtok_ready, 1)

            def product_out(t, q):
                m = t[0]
                edge, kind = PRODUCTS[q]
                w = P // 4
                for s in range(2):
                    act.wait_ge(prod_done[s], NP * m + q + 1)
                    if edge == 32 and kind != "T":
                        prod = tp[:, s, :].rearrange("p (h t) -> p h t", t=P)
                        for b in range(2):
                            rows, cols = slice(2 * b * w, (2 * b + 1) * w), slice((2 * b + 1) * w, (2 * b + 2) * w)
                            last = act.activation((x32 if kind == "X" else tu)[rows, s, :, cols], prod[rows, :, cols],
                                                  ACT.Copy, scale=(1.0 if kind == "X" else -1.0))
                    else:
                        half = tp[:, s, 0:2 * P].rearrange("p (h t) -> p h t", h=H)
                        if edge == 32:
                            last = act.activation(tt[w:2 * w, s, :, 0:w], half[w:2 * w, :, 0:w], ACT.Copy, scale=-1.0)
                        else:
                            last = act.activation(x64[0:2 * w, s], half[0:2 * w], ACT.Copy)
                    last.then_inc(prod_read[s], 1)

            def mid_out(st):
                m = st[0]
                for s in range(2):
                    act.wait_ge(mid_done[s], m + 1)
                    mm = mid[:, s].rearrange("p h (g d) -> p (h g) d", d=D).rearrange("p (r g) d -> p r g d", r=PR)
                    pp = sc[:, s, :].rearrange("p (r g d) -> p r g d", r=PR, d=D)
                    act.activation(mm[:, :, 0:4:3, :], pp[:, :, 0:4:3, :], ACT.Copy).then_inc(mid_ready[s], 1)

            def out_squares(st):
                m = st[0]
                act.wait_ge(o_done, m + 1)
                wait(act, oms_ready, m)
                act.activation(osq[:].rearrange("p s d -> p (s d)"), ob[:], ACT.Square).then_inc(osq_ready, 1)

            def out_high(st):
                m = st[0]
                act.wait_ge(oT_done, m + 1)
                wait(act, y_done, m)
                act.activation(othi[:].rearrange("p r s t -> p (r s t)"), ob[:], ACT.Copy).then_inc(othi_ready, 1)

            act.wait_ge(w_loaded, 16 * 10)
            act.activation(wqkv[:, 0].rearrange("p c j d -> p j c d"), wstage[:, 0:3], ACT.Copy).then_inc(w_hi, 1)
            act.activation(wbs[:, 0], bstage[:], ACT.Copy).then_inc(w_hi, 1)
            act.wait_ge(w_scaled, 1)
            act.activation(wos[:, 0], wstage[:, 3], ACT.Copy).then_inc(w_hi, 1)

            def body(f, g, t, s):
                for q in range(NQ):
                    if f and q == 0:
                        x_high(f)
                    if s:
                        if q == 1:
                            mid_out(s)
                    if t and q - T0 in (3, 4, 5, 6):
                        product_out(t, q - T0)
                    if s:
                        if q == 3:
                            out_squares(s)
                        if q == 6:
                            out_high(s)
                    if f:
                        if q == 1:
                            raw_out(f, 0)
                            beta_tanh(f)
                            tap0(f, 0)
                        if q == 2:
                            raw_out(f, 1)
                            tap0(f, 1)
                        if q == 4:
                            raw_out(f, 2)
                            tap0(f, 2)
                        if q == 5:
                            silus(f, 0)
                        if q == 7:
                            silus(f, 1)
                        if q == 8:
                            silus(f, 2)
                        if q == 9:
                            squares(f)

            steps_of(act, body)

        @block.gpsimd
        def _(pool):
            count = [0]

            def link(ins):
                count[0] += 1
                ins.then_inc(rstd_part, 1)
                pool.wait_ge(rstd_part, count[0])

            def select(view, pattern, base, mult, op=ALU.is_ge, fill=0.0):
                link(pool.affine_select(out=view, in_=view, compare_op=op, fill=fill, base=base, pattern=pattern,
                                        channel_multiplier=mult))

            link(pool.memset(ident[:], 0.0))
            select(ident[:], [[-1, P]], 0, 1, ALU.not_equal, 1.0)
            link(pool.memset(below[:], 1.0))
            select(below[:], [[-1, P]], -1, 1)
            link(pool.memset(upto[:], 1.0))
            select(upto[:], [[1, P]], 0, -1)
            v = quarter[:].rearrange("p (b h t) -> p b h t", h=2, t=SB)
            link(pool.memset(v[:, :, 0:1, :], 0.0))
            link(pool.memset(v[:, :, 1:2, :], 1.0))
            v = quarter[:].rearrange("p (b t) -> p b t", t=2 * SB)
            select(v, [[-2 * SB, P // (2 * SB)], [0, 2 * SB]], 0, 1)
            select(v, [[2 * SB, P // (2 * SB)], [0, 2 * SB]], SB - 1, -1)
            link(pool.memset(eye[:], 0.0))
            link(pool.affine_select(out=eye[:], in_=eye[:], compare_op=ALU.not_equal, fill=1.0, base=0,
                                    pattern=[[-1, SB], [1, SB]], channel_multiplier=0))
            link(pool.memset(powers[:, 0, :], 0.5))
            link(pool.memset(powers[:, 1, :], -0.5))
            pool.memset(kx[:], 0.0).then_inc(masks, 1)
            pool.wait_ge(masks, 1)
            base = count[0]

            def inverse_std(m):
                pool.wait_ge(stats_ready, m + 1)
                wait(pool, xn_ready, m)
                pass_by(pool, passed)
                pool.tensor_scalar(var_eps[:], mv[:, :, 1], EPS, None, ALU.add).then_inc(rstd_part, 1)
                pool.wait_ge(rstd_part, base + m + 1)
                pool.tensor_tensor(rstd[:], var_eps[:], powers[:, 1, 0:2], ALU.pow).then_inc(rstd_ready, 1)

            def key_norms(f):
                m, par, _ = f
                pool.wait_ge(ss_ready, m + 1)
                wait(pool, vn_ready, m)
                pool.tensor_tensor(kn[:], ss[:, par, :, 0, :], powers[:, 0, :].rearrange("p (s h) -> p s h", s=2),
                                   ALU.pow).then_inc(kn_ready, 1)

            def invert_blocks(g, first, end):
                m = g[0]
                n, v = small, inv[:, 0]
                if first == 1:
                    pool.wait_ge(blocks_in, 16 * (m + 1))
                    wait(pool, inv_out, 32 * m)
                    pool.tensor_tensor(v, eye[:], n[:], ALU.subtract).then_inc(solve_step, 1)
                for j in range(first, end):
                    k = SB - 1 - j
                    pool.wait_ge(solve_step, SOLVE * m + 2 * j - 1)
                    pool.tensor_tensor(term[:, 0:k, 0:j], n[:, j + 1:, j:j + 1].broadcast_to([BP, k, j]),
                                       v[:, j:j + 1, 0:j].broadcast_to([BP, k, j]), ALU.mult).then_inc(solve_step, 1)
                    pool.wait_ge(solve_step, SOLVE * m + 2 * j)
                    pool.tensor_tensor(v[:, j + 1:, 0:j], v[:, j + 1:, 0:j], term[:, 0:k, 0:j], ALU.subtract)\
                        .then_inc(solve_step, 1)
                if end < SB - 1:
                    return
                pool.wait_ge(solve_step, SOLVE * (m + 1) - 1)
                pass_by(pool, passed)
                pool.tensor_copy(inv[:, 1], v.rearrange("p r c -> p c r")).then_inc(solve_step, 1)

            def values(f):
                m, par, _ = f
                pool.wait_ge(kn_ready, m + 1)
                pool.wait_ge(vtok_ready, m + 1)
                for s in range(2):
                    wait(pool, r_ready[s], m - 3)
                pool.tensor_tensor(vn[:, par].rearrange("p s (h d) -> p (s h) d", d=D),
                                   vtok[:].rearrange("p (g d) -> p g d", d=D),
                                   kn[:].rearrange("p s h -> p (s h)").unsqueeze(2).broadcast_to([P, 2 * H, D]),
                                   ALU.mult).then_inc(vn_ready, 1)

            def out_factor(st):
                m, par, _ = st
                pool.wait_ge(oms_ready, m + 1)
                wait(pool, og_ready, m)
                pass_by(pool, passed)
                pool.tensor_scalar(ovar[:], oms[:], 1.0 / D, None, ALU.mult).then_inc(ovar_part, 1)
                pool.tensor_scalar(oeps[:], ss[:, par, :, 1, :], D * EPS, None, ALU.mult).then_inc(ovar_part, 1)
                pool.wait_ge(ovar_part, 2 * m + 2)
                pool.tensor_tensor(osum[:], ovar[:], oeps[:], ALU.add).then_inc(osum_ready, 1)
                pool.wait_ge(osum_ready, m + 1)
                wait(pool, on_ready, m)
                pool.tensor_tensor(og[:], osum[:], powers[:, 1, :].rearrange("p (s h) -> p s h", s=2),
                                   ALU.pow).then_inc(og_ready, 1)

            inverse_std(0)

            def body(f, g, t, s):
                if g:
                    invert_blocks(g, 1, SB // 2 - 2)
                if s:
                    out_factor(s)
                if f and not (isinstance(f[0], int) and f[0] + 1 >= NS):
                    inverse_std(f[0] + 1)
                if g:
                    invert_blocks(g, SB // 2 - 2, SB - 1)
                if f:
                    key_norms(f)
                    values(f)

            steps_of(pool, body)


def build(nc, x, wq, wk, wv, wb, cq, ck, cv, rms_w, wo, gate_w, w1, w2, w3, out):
    def dram(n, shape):
        return nc.dram_tensor(n, shape, F32, kind="Internal").ap()

    x1, x2 = dram("x_after_first", [B * L, DM]), dram("x_after_attention", [B * L, DM])
    s1, s2 = dram("scales_first", [E, TB]), dram("scales_second", [E, TB])
    n_dram, t_dram = dram("small_blocks", [8, 8, 16, 16]), dram("small_inverses", [8, 2, 8, 16, 16])
    ffn(nc, "ffn1", x.rearrange("b l d -> (b l) d"), x1, s1, gate_w, w1, w2, w3)
    attention(nc, "attn", x1, x2, n_dram, t_dram, wq, wk, wv, wb, cq, ck, cv, rms_w, wo)
    ffn(nc, "ffn2", x2, out.rearrange("b l d -> (b l) d"), s2, gate_w, w1, w2, w3)


_INS = ["L0_attn_x", "L0_attn_Wq", "L0_attn_Wk", "L0_attn_Wv", "L0_attn_Wb", "L0_attn_conv_q_w", "L0_attn_conv_k_w",
        "L0_attn_conv_v_w", "L0_attn_rms_w", "L0_attn_Wo", "L0_ffn_gate_w", "L0_ffn_w1", "L0_ffn_w2", "L0_ffn_w3"]
_OUTS = [((B, L, DM), "float32")]


def kernel(**inputs):
    import numpy as _np
    import concourse.bacc as _bacc
    from concourse import mybir as _mybir
    from concourse.bass_utils import run_bass_kernel_spmd as _run

    nc = _bacc.Bacc("TRN2", target_bir_lowering=False, num_devices=1)
    arrays, args = {}, []
    for name in _INS:
        a = _np.ascontiguousarray(inputs[name])
        arrays[f"in_{name}_dram"] = a
        args.append(nc.dram_tensor(f"in_{name}_dram", a.shape, _mybir.dt.from_np(a.dtype), kind="ExternalInput").ap())
    for i, (shape, dtype) in enumerate(_OUTS):
        dt = _mybir.dt.from_np(_np.dtype(dtype))
        args.append(nc.dram_tensor(f"out_{i}_dram", shape, dt, kind="ExternalOutput").ap())
    build(nc, *args)
    r = _run(nc, [arrays], core_ids=[0])
    return r.results[0]["out_0_dram"]
```

```python
from contextlib import ExitStack

import concourse.bass as bass
from concourse import mybir

P = 128
B, L, DM = 2, 4096, 256
NT = B * L // P
KC = DM // P
E, HF = 8, 128
TPB = 4
TB = TPB * P
H, D, KW = 4, 64, 4
PR = H // 2
NB = NT // TPB
EPS = 1e-5
F32 = mybir.dt.float32
F32R = mybir.dt.float32r
ALU = mybir.AluOpType
ACT = mybir.ActivationFunctionType
AX = mybir.AxisListType


def wait(eng, sem, value):
    if not (isinstance(value, int) and value <= 0):
        eng.wait_ge(sem, value)


def pass_by(eng, passed):
    eng.sem_inc(passed, 1)


def blocks_of(eng, body, count):
    body(0, 0, 0)
    body(0, 1, 1)
    with eng.Fori(1, count // 2 - 1) as i:
        body(i, 0, None)
        body(i, 1, None)
    body(count // 2 - 1, 0, count - 2)
    body(count // 2 - 1, 1, count - 1)


class Kept:

    def __init__(self, ctx, nc):
        def sb(n, shape, dt=F32):
            return ctx.enter_context(nc.sbuf_tensor(n, shape, dt))

        self.w1s = sb("w1s", [P, 2, KC, E, HF], F32R)
        self.w3s = sb("w3s", [P, 2, KC, E, HF], F32R)
        self.w2s = sb("w2s", [P, 2, E, DM], F32R)
        self.gws = sb("gws", [P, KC, 2, E], F32R)
        self.wqkv = sb("wqkv", [P, 2, KC, 3, DM], F32R)
        self.wbs = sb("wbs", [P, 2, KC, H], F32R)
        self.wos = sb("wos", [P, 2, PR, DM], F32R)
        self.taps = sb("taps", [P, 3, PR, KW])
        self.ident = sb("ident", [P, P])
        self.xbuf = sb("xbuf", [P, 2, TPB, DM])
        self.attn_x = ctx.enter_context(nc.semaphore("attn_x_ahead"))
        self.ffn_x = ctx.enter_context(nc.semaphore("ffn_x_ahead"))


class Fresh:

    def __init__(self, wq, wk, wv, wb, cq, ck, cv, rms_w, wo, gate_w, w1, w2, w3):
        self.wq, self.wk, self.wv, self.wb, self.wo, self.rms_w = wq, wk, wv, wb, wo, rms_w
        self.cq, self.ck, self.cv = cq, ck, cv
        self.gate_w, self.w1, self.w2, self.w3 = gate_w, w1, w2, w3


def ffn(nc, name, src, dst, s_dram, kept, fresh=None):
    ctx = ExitStack()
    with ctx:
        def sb(n, shape, dt=F32):
            return ctx.enter_context(nc.sbuf_tensor(f"{name}_{n}", shape, dt))

        def sem(n):
            return ctx.enter_context(nc.semaphore(f"{name}_{n}"))

        w1s, w3s, w2s, gws, ident = kept.w1s, kept.w3s, kept.w2s, kept.gws, kept.ident
        if fresh:
            stage = sb("stage", [P, 2, E * DM])
            gstage = sb("gstage", [P, KC, E])
            astage = stage[:, 1].rearrange("p (j c d) -> p j c d", j=4, c=KC)
            bstage = sb("bstage", [P, KC, H])
            rms2 = sb("rms2", [P, 1])
        mhalf = sb("mhalf", [P, TPB])
        xin = kept.xbuf
        stats = sb("stats", [P, TPB, 6])
        mv = sb("mv", [P, TPB, 2])
        var_eps = sb("var_eps", [P, TPB])
        rstd = sb("rstd", [P, TPB])
        xn = sb("xn", [P, TPB, DM])
        xhi = sb("xhi", [P, 2, KC, TB], F32R)
        xlo = sb("xlo", [P, 2, KC, TB], F32R)
        lgT = sb("lgT", [2 * E, TB])
        lg = sb("lg", [P, TPB, E])
        lmax = sb("lmax", [P, TPB])
        lsub = sb("lsub", [P, TPB, E])
        lexp = sb("lexp", [P, TPB, E])
        lsum = sb("lsum", [P, TPB])
        linv = sb("linv", [P, TPB])
        score = sb("score", [P, TPB, 2 * E])
        top = sb("top", [P, TPB, 8])
        rest = sb("rest", [P, TPB, 2 * E])
        scale = sb("scale", [P, TPB, E])
        scT = sb("scT", [E, TB])
        scB = sb("scB", [P, 2, E, TB])
        ts = sb("ts", [P, 2, 2, TB])
        sil = sb("sil", [P, 2, TB])
        hid = sb("hid", [P, 2, TB])
        hhi = sb("hhi", [P, 4, TB], F32R)
        hlo = sb("hlo", [P, 4, TB], F32R)
        xres = sb("xres", [P, TPB, DM])

        def pt(n, shape):
            return ctx.enter_context(nc.psum_tensor(f"{name}_{n}", shape, F32))

        up = pt("up", [P, 2, 2, TB])
        yb = pt("yb", [P, TPB, DM])
        tr = pt("tr", [P, KC, TB])

        if fresh:
            s_w = [sem(f"w_loaded{j}") for j in range(2)]
            w_hi, w_lo, id_set, attn_loaded, attn_scaled, attn_hi, attn_lo = (sem(n) for n in (
                "w_hi", "w_lo", "id_set", "attn_loaded", "attn_scaled", "attn_hi", "attn_lo"))
        consts = sem("consts")
        passed = sem("passed")
        x_loaded = [sem(f"x_loaded{j}") for j in range(2)]
        res_loaded = sem("res_loaded")
        stats_ready = sem("stats_ready")
        stats_part = sem("stats_part")
        rstd_part = sem("rstd_part")
        rstd_ready = sem("rstd_ready")
        xn_ready = sem("xn_ready")
        xT_done = sem("xT_done")
        xhi_ready = sem("xhi_ready")
        xlo_ready = sem("xlo_ready")
        lgT_done = sem("lgT_done")
        lgT_copied = sem("lgT_copied")
        lg_done = sem("lg_done")
        lg_ready = sem("lg_ready")
        lsub_ready = sem("lsub_ready")
        lexp_ready = sem("lexp_ready")
        chain = sem("route_chain")
        scale_ready = sem("scale_ready")
        scT_done = sem("scT_done")
        scT_copied = sem("scT_copied")
        sc_stored = sem("sc_stored")
        scB_loaded = [sem(f"scB_loaded{j}") for j in range(2)]
        up_done = sem("up_done")
        ts_ready = sem("ts_ready")
        sil_ready = sem("sil_ready")
        hid_ready = sem("hid_ready")
        hhi_ready = sem("hhi_ready")
        hlo_ready = sem("hlo_ready")
        down_done = sem("down_done")
        y_read = sem("y_read")
        stored = sem("stored")
        CH = 7

        block = ctx.enter_context(nc.Block())
        x_v = src.rearrange("(n j p) d -> n p j d", j=TPB, p=P)
        o_v = dst.rearrange("(n j p) d -> n p j d", j=TPB, p=P)
        sets = [] if not fresh else [(fresh.w1.rearrange("e (c p) h -> p c e h", p=P), w1s),
                (fresh.w3.rearrange("e (c p) h -> p c e h", p=P), w3s),
                (fresh.w2.rearrange("e h d -> h e d"), w2s)]

        def flat(w, part):
            a = w[:, part]
            return a.rearrange("p c e h -> p (c e h)") if len(a.shape) == 4 else a.rearrange("p e d -> p (e d)")

        if fresh:
            attention_sets = [(kept.wqkv[:, 0, :, j], kept.wqkv[:, 1, :, j], astage[:, j]) for j in range(3)] + \
                [(kept.wbs[:, 0], kept.wbs[:, 1], bstage[:]), (kept.wos[:, 0], kept.wos[:, 1], astage[:, 3])]

        @block.sync
        def _(sp):
            def load_x(m, i, c):
                wait(sp, xn_ready, m - 1)
                sp.dma_start(xin[:, c % 2], x_v[m]).then_inc(x_loaded[c % 2], 16)

            def load_res(n):
                wait(sp, stored, 16 * n)
                sp.dma_start(xres[:], x_v[n]).then_inc(res_loaded, 16)

            def store(n):
                sp.wait_ge(y_read, n + 1)
                sp.dma_start(o_v[n], xres[:]).then_inc(stored, 16)

            def spread(m, c):
                sp.wait_ge(scT_copied, m + 1)
                sp.dma_start(s_dram, scT[:]).then_inc(sc_stored, 16)
                sp.wait_ge(sc_stored, 16 * (m + 1))
                pass_by(sp, passed)
                wait(sp, ts_ready, E * (m - 1))
                for h in range(2):
                    sp.dma_start(scB[:, c % 2, 4 * h:4 * h + 4], s_dram[4 * h:4 * h + 4].partition_broadcast(P))\
                      .then_inc(scB_loaded[h], 16)

            def load_attention_weights():
                sp.wait_ge(w_lo, 3)
                for j, w in enumerate((fresh.wk, fresh.wv, fresh.wq, fresh.wo)):
                    sp.dma_start(astage[:, j], w.rearrange("(c p) n -> p c n", p=P)).then_inc(attn_loaded, 16)
                sp.dma_start(bstage[:], fresh.wb.rearrange("(c p) n -> p c n", p=P)).then_inc(attn_loaded, 16)
                for j, w in enumerate((fresh.ck, fresh.cv, fresh.cq)):
                    sp.dma_start(kept.taps[:, j], w.rearrange("(r p) o k -> p r (o k)", p=P)).then_inc(attn_loaded, 16)
                for h in range(2):
                    sp.dma_start(rms2[h * D:(h + 1) * D, :], fresh.rms_w.rearrange("(d o) -> d o", o=1))\
                      .then_inc(attn_loaded, 16)

            if fresh:
                load_x(0, 0, 0)
                sp.dma_start(gstage[:], fresh.gate_w.rearrange("(c p) e -> p c e", p=P)).then_inc(s_w[0], 16)
                load_x(1, 0, 1)
            for k, (w, _) in enumerate(sets):
                if k == 2:
                    sp.wait_ge(w_lo, 2)
                o = stage[:, k % 2].rearrange("p (c e h) -> p c e h", c=KC, e=E) if k < 2 else \
                    stage[:, 0].rearrange("p (e d) -> p e d", e=E)
                if k < 2:
                    for q in range(KC):
                        sp.dma_start(o[:, q], w[:, q]).then_inc(s_w[1], 16)
                        sp.wait_ge(s_w[1], 16 * (2 * k + q + 1))
                else:
                    sp.dma_start(o, w).then_inc(s_w[1], 16)
            load_res(0)
            spread(0, 0)

            def body(i, c, n):
                n = 2 * i + c if n is None else n
                if not (isinstance(n, int) and n == 0):
                    store(n - 1)
                    load_res(n)
                if not (isinstance(n, int) and n + 2 >= NB):
                    load_x(n + 2, i, c + 2)
                if not (isinstance(n, int) and n + 1 >= NB):
                    spread(n + 1, c + 1)
                if fresh and isinstance(n, int) and n == 0:
                    load_attention_weights()
                if fresh and isinstance(n, int) and n == NB - 1:
                    sp.wait_ge(xn_ready, NB)
                    steps = dst.rearrange("(s n p) d -> n p s d", s=2, p=P)
                    for m in range(2):
                        sp.dma_start(xin[:, m, 0:2], steps[m]).then_inc(kept.attn_x, 16)

            blocks_of(sp, body, NB)
            store(NB - 1)
            sp.wait_ge(stored, 16 * NB)

        @block.tensor
        def _(pe):
            TERMS = [(0, 0), (0, 1), (1, 0)]

            def transposes(m):
                pe.wait_ge(xn_ready, m + 1)
                wait(pe, scT_copied, m)
                for j in range(TPB):
                    for q in range(KC):
                        last = pe.transpose(tr[:, q, j * P:(j + 1) * P], xn[:, j, q * P:(q + 1) * P], ident[:])
                last.then_inc(xT_done, 1)

            def logits(m, c):
                pe.wait_ge(xhi_ready, m + 1)
                pe.wait_ge(xlo_ready, m + 1)
                gw = gws[:].rearrange("p c a e -> p c (a e)")
                for k, (x, q, rows) in enumerate([(xhi, 0, 2 * E), (xlo, 0, E), (xlo, 1, E), (xhi, 1, 2 * E)]):
                    last = pe.matmul(tr[0:rows, 0, :], gw[:, q, 0:rows], x[:, c % 2, q, :], start=(k == 0),
                                     stop=(k == 3), skip_group_check=True)
                last.then_inc(lgT_done, 1)

            def logits_back(m):
                pe.wait_ge(lgT_copied, m + 1)
                pass_by(pe, passed)
                for j in range(TPB):
                    last = pe.transpose(tr[:, 1, 2 * j * E:2 * (j + 1) * E], lgT[:, j * P:(j + 1) * P],
                                        ident[0:2 * E, 0:2 * E])
                last.then_inc(lg_done, 1)

            def scales_up(m):
                pe.wait_ge(scale_ready, m + 1)
                for j in range(TPB):
                    last = pe.transpose(tr[0:E, 0, j * P:(j + 1) * P], scale[:, j, :], ident[:])
                last.then_inc(scT_done, 1)

            def expert_up(n, c, k):
                g = E * n + k
                if k == 0:
                    pe.wait_ge(xhi_ready, n + 1)
                    pe.wait_ge(xlo_ready, n + 1)
                wait(pe, ts_ready, g - 1)
                for o, w in enumerate((w1s, w3s)):
                    for t, (a, b) in enumerate(TERMS):
                        for q in range(KC):
                            last = pe.matmul(up[:, k % 2, o, :], w[:, a, q, k, :], (xhi, xlo)[b][:, c % 2, q, :],
                                             start=(t == 0 and q == 0), stop=(t == 2 and q == KC - 1))
                last.then_inc(up_done, 1)

            def expert_down(n, k):
                g = E * n + k
                pe.wait_ge(hhi_ready, g + 1)
                pe.wait_ge(hlo_ready, g + 1)
                if k == 0:
                    wait(pe, y_read, n)
                for j in range(TPB):
                    for t, (a, b) in enumerate(TERMS):
                        last = pe.matmul(yb[:, j, :], (hhi, hlo)[b][:, k % 4, j * P:(j + 1) * P], w2s[:, a, k, :],
                                         start=(k == 0 and t == 0 and j % 2 == 0),
                                         stop=(k == E - 1 and t == 2), skip_group_check=True)
                last.then_inc(down_done, 1)

            if fresh:
                pe.wait_ge(id_set, 2)
            transposes(0)
            if fresh:
                pe.wait_ge(w_hi, 1)
                pe.wait_ge(w_lo, 1)
            logits(0, 0)
            logits_back(0)
            if fresh:
                scales_up(0)
                pe.wait_ge(w_hi, 3)
                pe.wait_ge(w_lo, 3)
            expert_up(0, 0, 0)
            if not fresh:
                scales_up(0)
            expert_up(0, 0, 1)
            if fresh:
                pe.wait_ge(w_hi, 4)
                pe.wait_ge(w_lo, 4)

            def body(i, c, n):
                n = 2 * i + c if n is None else n
                first, last = isinstance(n, int) and n == 0, isinstance(n, int) and n + 1 >= NB
                for k in range(E):
                    if k == 3 and not last:
                        logits_back(n + 1)
                    if not (first and k < 2):
                        expert_up(n, c, k)
                    if k >= 2:
                        expert_down(n, k - 2)
                    elif not first:
                        expert_down(n - 1, E + k - 2)
                    if not last:
                        if k == 0:
                            transposes(n + 1)
                        if k == 1:
                            logits(n + 1, c + 1)
                        if k == 5:
                            scales_up(n + 1)

            blocks_of(pe, body, NB)
            expert_down(NB - 1, E - 2)
            expert_down(NB - 1, E - 1)

        @block.vector
        def _(dve):
            def ln_stats(m, c, i):
                if fresh:
                    dve.wait_ge(x_loaded[c % 2], 16 * (i + c // 2 + 1))
                elif isinstance(m, int) and m < 2:
                    dve.wait_ge(kept.ffn_x, 16 * (m + 1))
                else:
                    dve.wait_ge(x_loaded[c % 2], 16 * (i + c // 2))
                wait(dve, rstd_ready, m)
                wait(dve, xn_ready, m)
                for j in range(TPB):
                    dve.bn_stats(stats[:, j, :], xin[:, c % 2, j, :]).then_inc(stats_part, 1)
                dve.wait_ge(stats_part, TPB * (m + 1))
                pass_by(dve, passed)
                for j in range(TPB):
                    last = dve.bn_aggr(mv[:, j, :], stats[:, j, :])
                last.then_inc(stats_ready, 1)

            def normalize(m, c):
                dve.wait_ge(rstd_ready, m + 1)
                wait(dve, xT_done, m)
                for j in range(TPB):
                    last = dve.tensor_scalar(xn[:, j, :], xin[:, c % 2, j, :], mv[:, j, 0:1], rstd[:, j:j + 1],
                                             ALU.subtract, ALU.mult)
                last.then_inc(xn_ready, 1)

            def low_part(m, c):
                dve.wait_ge(xhi_ready, m + 1)
                wait(dve, up_done, E * (m - 1))
                dve.tensor_tensor(xlo[:, c % 2], tr[:], xhi[:, c % 2].bitcast(F32), ALU.subtract).then_inc(xlo_ready, 1)

            def logits_copy(m):
                dve.wait_ge(lgT_done, m + 1)
                wait(dve, lg_done, m)
                dve.tensor_copy(lgT[:], tr[0:2 * E, 0, :]).then_inc(lgT_copied, 1)

            def minus_max(m):
                dve.wait_ge(lg_done, m + 1)
                parts = tr[:, 1, 0:2 * TPB * E].rearrange("p (j a e) -> p j a e", a=2, e=E)
                dve.tensor_reduce(lg[:], parts.rearrange("p j a e -> p j e a"), AX.X, ALU.add).then_inc(lg_ready, 1)
                dve.wait_ge(lg_ready, m + 1)
                dve.tensor_reduce(lmax[:], lg[:], AX.X, ALU.max).then_inc(chain, 1)
                dve.wait_ge(chain, CH * m + 1)
                wait(dve, lexp_ready, m)
                dve.tensor_tensor(lsub[:], lg[:], lmax[:].unsqueeze(2).broadcast_to([P, TPB, E]), ALU.subtract)\
                   .then_inc(lsub_ready, 1)

            def top_two(m):
                dve.wait_ge(lexp_ready, m + 1)
                dve.tensor_reduce(lsum[:], lexp[:], AX.X, ALU.add).then_inc(chain, 1)
                dve.wait_ge(chain, CH * m + 2)
                dve.reciprocal(linv[:], lsum[:]).then_inc(chain, 1)
                dve.wait_ge(chain, CH * m + 3)
                dve.tensor_tensor(score[:, :, 0:E], lexp[:], linv[:].unsqueeze(2).broadcast_to([P, TPB, E]),
                                  ALU.mult).then_inc(chain, 1)
                dve.wait_ge(chain, CH * m + 4)
                pass_by(dve, passed)
                for j in range(TPB):
                    last = dve.max(top[:, j, :], score[:, j, 0:E])
                last.then_inc(chain, 1)
                dve.wait_ge(chain, CH * m + 5)
                dve.memset(top[:, :, 2:8], -1.0).then_inc(chain, 1)
                dve.wait_ge(chain, CH * m + 6)
                pass_by(dve, passed)
                for j in range(TPB):
                    last = dve.match_replace(rest[:, j, :], top[:, j, :], score[:, j, :], 0.0)
                last.then_inc(chain, 1)
                dve.wait_ge(chain, CH * m + 7)
                wait(dve, scT_done, m)
                dve.tensor_tensor(scale[:], score[:, :, 0:E], rest[:, :, 0:E], ALU.subtract).then_inc(scale_ready, 1)

            def scales_copy(m):
                dve.wait_ge(scT_done, m + 1)
                wait(dve, sc_stored, 16 * m)
                dve.tensor_copy(scT[:], tr[0:E, 0, :]).then_inc(scT_copied, 1)

            def scaled(n, c, k):
                g = E * n + k
                dve.wait_ge(up_done, g + 1)
                if k % 4 == 0:
                    dve.wait_ge(scB_loaded[k // 4], 16 * (n + 1))
                wait(dve, hid_ready, g - 1)
                s = scB[:, c % 2, k, :].unsqueeze(1).broadcast_to([P, 2, TB])
                dve.tensor_tensor(ts[:, k % 2], up[:, k % 2], s, ALU.mult).then_inc(ts_ready, 1)

            def hidden(n, k):
                g = E * n + k
                dve.wait_ge(sil_ready, g + 1)
                dve.wait_ge(ts_ready, g + 1)
                wait(dve, hlo_ready, g - 1)
                dve.tensor_tensor(hid[:, k % 2], ts[:, k % 2, 1], sil[:, k % 2], ALU.mult).then_inc(hid_ready, 1)

            def residual(n):
                dve.wait_ge(down_done, E * (n + 1))
                dve.wait_ge(res_loaded, 16 * (n + 1))
                dve.scalar_tensor_tensor(xres[:], yb[:], 0.5, xres[:], ALU.mult, ALU.add).then_inc(y_read, 1)

            def split_weights(k):
                if not fresh:
                    return
                dve.wait_ge(w_hi, k + 1)
                hi, lo = (gws[:, :, 0], gws[:, :, 1]) if k == 0 else (flat(sets[k - 1][1], 0), flat(sets[k - 1][1], 1))
                raw = gstage[:] if k == 0 else stage[:, (k - 1) % 2]
                dve.tensor_tensor(lo, raw, hi.bitcast(F32), ALU.subtract).then_inc(w_lo, 1)

            def split_attention_weights(k):
                if k == 2:
                    dve.wait_ge(attn_loaded, 16 * 10)
                    dve.tensor_scalar(astage[:, 3], astage[:, 3], rms2[:, 0:1], None, ALU.mult).then_inc(attn_scaled, 1)
                else:
                    dve.wait_ge(attn_hi, k - 2)
                    hi, lo, raw = attention_sets[k - 3]
                    dve.tensor_tensor(lo, raw, hi.bitcast(F32), ALU.subtract).then_inc(attn_lo, 1)

            dve.memset(score[:], -1.0).then_inc(consts, 1)
            split_weights(0)
            ln_stats(0, 0, 0)
            normalize(0, 0)
            low_part(0, 0)
            split_weights(1)
            logits_copy(0)
            minus_max(0)
            dve.wait_ge(consts, 1)
            top_two(0)
            split_weights(2)
            scales_copy(0)
            split_weights(3)
            ln_stats(1, 1, 0)
            normalize(1, 1)

            def body(i, c, n):
                n = 2 * i + c if n is None else n
                first, last = isinstance(n, int) and n == 0, isinstance(n, int) and n + 1 >= NB
                for k in range(E):
                    if k > 0:
                        hidden(n, k - 1)
                    elif not first:
                        hidden(n - 1, E - 1)
                    scaled(n, c, k)
                    if k == 1 and not first:
                        residual(n - 1)
                    if not last:
                        if k == 0:
                            low_part(n + 1, c + 1)
                        if k == 1:
                            logits_copy(n + 1)
                        if k == 3:
                            minus_max(n + 1)
                        if k == 4:
                            top_two(n + 1)
                        if k == 6:
                            scales_copy(n + 1)
                    if fresh and isinstance(n, int) and n == 1 and k >= 2:
                        split_attention_weights(k)
                    if not (isinstance(n, int) and n + 2 >= NB):
                        if k == 5:
                            ln_stats(n + 2, c + 2, i)
                        if k == 7:
                            normalize(n + 2, c + 2)

            blocks_of(dve, body, NB)
            hidden(NB - 1, E - 1)
            residual(NB - 1)

        @block.scalar
        def _(act):
            def high_part(m, c):
                act.wait_ge(xT_done, m + 1)
                wait(act, up_done, E * (m - 1))
                act.activation(xhi[:, c % 2], tr[:], ACT.Copy).then_inc(xhi_ready, 1)

            def exps(m):
                act.wait_ge(lsub_ready, m + 1)
                act.activation(lexp[:], lsub[:], ACT.Exp).then_inc(lexp_ready, 1)

            def silu(n, k):
                g = E * n + k
                act.wait_ge(ts_ready, g + 1)
                wait(act, hid_ready, g - 1)
                act.activation(sil[:, k % 2], ts[:, k % 2, 0], ACT.Silu).then_inc(sil_ready, 1)

            def high_hidden(n, k):
                g = E * n + k
                act.wait_ge(hid_ready, g + 1)
                wait(act, down_done, g - 3)
                act.activation(hhi[:, k % 4], hid[:, k % 2], ACT.Copy).then_inc(hhi_ready, 1)

            def round_weights(k):
                if not fresh:
                    return
                if k == 0:
                    act.wait_ge(s_w[0], 16)
                    act.activation(gws[:, :, 0], gstage[:], ACT.Copy).then_inc(w_hi, 1)
                    return
                act.wait_ge(s_w[1], (32, 64, 80)[k - 1])
                act.activation(flat(sets[k - 1][1], 0), stage[:, (k - 1) % 2], ACT.Copy).then_inc(w_hi, 1)

            def round_attention_weights(k):
                act.wait_ge(attn_loaded, 16 * 10)
                act.wait_ge(attn_scaled, 1)
                hi, _, raw = attention_sets[k - 3]
                act.activation(hi, raw, ACT.Copy).then_inc(attn_hi, 1)

            round_weights(0)
            high_part(0, 0)
            round_weights(1)
            exps(0)
            round_weights(2)
            round_weights(3)

            def body(i, c, n):
                n = 2 * i + c if n is None else n
                first, last = isinstance(n, int) and n == 0, isinstance(n, int) and n + 1 >= NB
                for k in range(E):
                    if k > 0:
                        high_hidden(n, k - 1)
                    elif not first:
                        high_hidden(n - 1, E - 1)
                    silu(n, k)
                    if not last:
                        if k == 0:
                            high_part(n + 1, c + 1)
                        if k == 3:
                            exps(n + 1)
                    if fresh and isinstance(n, int) and n == 1 and k >= 3:
                        round_attention_weights(k)

            blocks_of(act, body, NB)
            high_hidden(NB - 1, E - 1)

        @block.gpsimd
        def _(pool):
            pool.memset(mhalf[:], -0.5).then_inc(rstd_part, 1)
            if fresh:
                pool.memset(ident[:], 0.0).then_inc(id_set, 1)
                pool.wait_ge(id_set, 1)
                pool.affine_select(out=ident[:], in_=ident[:], compare_op=ALU.not_equal, fill=1.0, base=0,
                                   pattern=[[-1, P]], channel_multiplier=1).then_inc(id_set, 1)

            def inverse_std(m):
                pool.wait_ge(stats_ready, m + 1)
                wait(pool, xn_ready, m)
                pass_by(pool, passed)
                pool.tensor_scalar(var_eps[:], mv[:, :, 1], EPS, None, ALU.add).then_inc(rstd_part, 1)
                pool.wait_ge(rstd_part, m + 2)
                pool.tensor_tensor(rstd[:], var_eps[:], mhalf[:], ALU.pow).then_inc(rstd_ready, 1)

            def low_hidden(n, k):
                g = E * n + k
                pool.wait_ge(hhi_ready, g + 1)
                wait(pool, down_done, g - 3)
                pool.tensor_tensor(hlo[:, k % 4], hid[:, k % 2], hhi[:, k % 4].bitcast(F32), ALU.subtract)\
                    .then_inc(hlo_ready, 1)

            inverse_std(0)
            inverse_std(1)

            def body(i, c, n):
                n = 2 * i + c if n is None else n
                first, last = isinstance(n, int) and n == 0, isinstance(n, int) and n + 1 >= NB
                if not first:
                    low_hidden(n - 1, E - 1)
                for k in range(1, E):
                    low_hidden(n, k - 1)
                    if k == 6 and not (isinstance(n, int) and n + 2 >= NB):
                        inverse_std(n + 2)

            blocks_of(pool, body, NB)
            low_hidden(NB - 1, E - 1)


def attention(nc, name, src, dst, n_dram, t_dram, kept):
    ctx = ExitStack()
    NS = L // P
    SB = 16
    NBK = P // SB
    BP = NBK * 2 * H
    PRODUCTS = [(16, "X"), (16, "U"), (16, "T"), (32, "X"), (32, "U"), (64, "TX"), (64, "U")]
    NP = len(PRODUCTS)
    NQ = 9
    T0 = NQ - NP
    with ctx:
        def sb(n, shape, dt=F32):
            return ctx.enter_context(nc.sbuf_tensor(f"{name}_{n}", shape, dt))

        def sem(n):
            return ctx.enter_context(nc.semaphore(f"{name}_{n}"))

        def sems(n, k):
            return [sem(f"{n}{j}") for j in range(k)]

        wqkv, wbs, wos, taps, ident = kept.wqkv, kept.wbs, kept.wos, kept.taps, kept.ident
        below = sb("below", [P, P])
        upto = sb("upto", [P, P])
        quarter = sb("quarter", [P, P])
        eye = sb("eye", [BP, SB, SB])
        powers = sb("powers", [P, 2, 2 * H])
        xin = kept.xbuf[:, :, 0:2]
        stats = sb("stats", [P, 2, 6])
        mv = sb("mv", [P, 2, 2])
        var_eps = sb("var_eps", [P, 2])
        rstd = sb("rstd", [P, 2])
        xn = sb("xn", [P, 2, DM])
        xhi = sb("xhi", [P, KC, 2 * P], F32R)
        xlo = sb("xlo", [P, KC, 2 * P], F32R)
        raw = sb("raw", [P, 3, PR, 2, KW - 1 + P])
        acc = sb("acc", [P, 3, PR, 2, P])
        sq = acc[:].rearrange("p j r s t -> p (j r s t)")[:, 0:4 * DM].rearrange("p (s j d) -> p s j d", s=2, j=2)
        bth = sb("bth", [H, 2 * P])
        beta = sb("beta", [P, 2, H])
        kq = sb("kq", [P, 4, PR, 2, 2, P])
        kx = sb("kx", [P, PR, 2, 2, P])
        vch = sb("vch", [P, PR, 2, P])
        ss = sb("ss", [P, 4, 2, 2, H])
        kn = sb("kn", [P, 2, H])
        rk = sb("rk", [P, 2, H])
        cc = sb("cc", [P, 4, 2, H])
        ktok = sb("ktok", [P, 4, 2, DM])
        vtok = sb("vtok", [P, 2 * DM])
        vn = sb("vn", [P, 4, 2, DM])
        nn = sb("nn", [P, 2, 2, H, P])
        at = sb("at", [P, 4, 2, H, P])
        small = sb("small", [BP, SB, SB])
        term = sb("term", [BP, SB, SB])
        inv = sb("inv", [BP, 2, SB, SB])
        tb = sb("tb", [P, 2, 2, H, P])
        tt = sb("tt", [P, 2, H, P])
        tu = sb("tu", [P, 2, H, P])
        xt = sb("xt", [P, 2, H, P])
        x32 = sb("x32", [P, 2, H, P])
        x64 = sb("x64", [P, 2, H, P // 2])
        tc = sb("tc", [P, 2, H, P])
        state = sb("state", [P, 2, PR, P])
        mid = sb("mid", [P, 2, H, P])
        oms = sb("oms", [P, 2, H])
        ovar = sb("ovar", [P, 2, H])
        oeps = sb("oeps", [P, 2, H])
        osum = sb("osum", [P, 2, H])
        og = sb("og", [P, 2, H])
        on = sb("on", [P, 2, DM])
        othi = sb("othi", [P, PR, 2, P], F32R)
        otlo = sb("otlo", [P, PR, 2, P], F32R)
        xres = sb("xres", [P, 2, DM])

        def pt(n, shape):
            return ctx.enter_context(nc.psum_tensor(f"{name}_{n}", shape, F32))

        fr = pt("fr", [P, 3, 512])
        tp = pt("tp", [P, 2, 512])
        sc = pt("sc", [P, 2, 512])
        ob = pt("ob", [P, 512])

        mask_step, masks, zeroed = (sem(n) for n in ("mask_step", "masks", "zeroed"))
        x_loaded = sems("x_loaded", 2)
        (stats_part, stats_ready, rstd_part, rstd_ready, xn_ready, xT_done, xhi_ready, xlo_ready, qkv_done,
         beta_done, hist_ready, raw_ready, tap0_ready, conv_step, bth_ready, bT_done, beta_ready, silu_ready,
         kx_ready, turned, sq_ready, ss_ready, ktok_ready, kn_ready, rk_ready, cc_ready, vtok_ready, vn_ready) = (sem(n) for n in (
             "stats_part", "stats_ready", "rstd_part", "rstd_ready", "xn_ready", "xT_done", "xhi_ready", "xlo_ready",
             "qkv_done", "beta_done", "hist_ready", "raw_ready", "tap0_ready", "conv_step", "bth_ready", "bT_done",
             "beta_ready", "silu_ready", "kx_ready", "turned", "sq_ready", "ss_ready", "ktok_ready", "kn_ready",
             "rk_ready", "cc_ready", "vtok_ready", "vn_ready"))
        gram_done, gram_read, prod_done, prod_read = (
            sems(n, 2) for n in ("gram_done", "gram_read", "prod_done", "prod_read"))
        blocks_out, blocks_in, solve_step, inv_out, tb_ready, tc_part = (sem(n) for n in (
            "blocks_out", "blocks_in", "solve_step", "inv_out", "tb_ready", "tc_part"))
        passed = sem("passed")
        ks_done, r_ready, mid_done, mid_ready, ds_done, s_ready = (
            sems(n, 2) for n in ("ks_done", "r_ready", "mid_done", "mid_ready", "ds_done", "s_ready"))
        osum_ready = sem("osum_ready")
        (o_done, osq_ready, oms_ready, ovar_part, og_ready, on_ready, oT_done, othi_ready, otlo_ready, y_done,
         y_read, res_loaded, stored) = (sem(n) for n in (
             "o_done", "osq_ready", "oms_ready", "ovar_part", "og_ready", "on_ready", "oT_done", "othi_ready",
             "otlo_ready", "y_done", "y_read", "res_loaded", "stored"))

        block = ctx.enter_context(nc.Block())
        x_v = src.rearrange("(s n p) d -> n p s d", s=2, p=P)
        o_v = dst.rearrange("(s n p) d -> n p s d", s=2, p=P)
        TERMS = [(0, 0), (0, 1), (1, 0)]
        SOLVE = 2 * SB - 2

        def after(f):
            m, par, turn = f
            return m + 1, (par + 1) % 4, turn + par % 2

        def steps_of(eng, body):
            def go(i, c, f, g, t, s):
                body(*(((4 * i + c + d), (c + d) % 4, 2 * i + (c + d) // 2) if on else None
                       for d, on in ((3, f), (2, g), (1, t), (0, s))))
            for c in range(1, 4):
                go(-1, c, True, c > 1, c > 2, False)
            for c in range(4):
                go(0, c, True, True, True, True)
            with eng.Fori(1, NS // 4 - 1) as i:
                for c in range(4):
                    go(i, c, True, True, True, True)
            for c in range(4):
                go(NS // 4 - 1, c, c < 1, c < 2, c < 3, True)

        @block.sync
        def _(sp):
            def hold(sem, value):
                wait(sp, sem, value)
                pass_by(sp, passed)

            def load_x(f):
                m, par, _ = f
                hold(xn_ready, m - 1)
                sp.dma_start(xin[:, par % 2], x_v[m]).then_inc(x_loaded[par % 2], 16)

            def spread_blocks(g):
                m, par, _ = g
                for s in range(2):
                    hold(gram_read[s], PR * (m + 1))
                for b in range(NBK):
                    a = slice(b * SB, (b + 1) * SB)
                    sp.dma_start(n_dram[b].rearrange("g r c -> r g c"),
                                 nn[a, par % 2].rearrange("p s h t -> p (s h) t")[:, :, a]).then_inc(blocks_out, 16)

            def take_blocks(g):
                m = g[0]
                hold(blocks_out, 16 * NBK * (m + 1))
                hold(solve_step, SOLVE * m)
                sp.dma_start(small[:], n_dram.rearrange("b g r c -> (b g) r c")).then_inc(blocks_in, 16)

            def collect_inverses(g):
                m = g[0]
                hold(solve_step, SOLVE * (m + 1))
                hold(tb_ready, 16 * NBK * m)
                for u in range(2):
                    sp.dma_start(t_dram[:, u].rearrange("b g r c -> b g (r c)"), inv[:, u].rearrange("p r c -> p (r c)"))\
                      .then_inc(inv_out, 16)
                for s in range(2):
                    hold(prod_read[s], NP * (m - 1) + 2)
                hold(inv_out, 32 * (m + 1))
                for b in range(NBK):
                    a = slice(b * SB, (b + 1) * SB)
                    sp.dma_start(tb[a].rearrange("p u s h t -> p (u s h) t")[:, :, a],
                                 t_dram[b].rearrange("u g r c -> r (u g) c")).then_inc(tb_ready, 16)

            def body(f, g, t, s):
                if g:
                    spread_blocks(g)
                if f and not (isinstance(f[0], int) and f[0] + 1 in (1, NS)):
                    load_x(after(f))
                if s and isinstance(s[0], int) and s[0] == NS - 2:
                    hold(xn_ready, NS)
                    for n in range(2):
                        sp.dma_start(kept.xbuf[:, n], dst.rearrange("(n j p) d -> n p j d", j=TPB, p=P)[n])\
                          .then_inc(kept.ffn_x, 16)
                if s:
                    m = s[0]
                    hold(stored, 16 * m)
                    sp.dma_start(xres[:], x_v[m]).then_inc(res_loaded, 16)
                if g:
                    take_blocks(g)
                if s:
                    hold(y_read, m + 1)
                    sp.dma_start(o_v[m], xres[:]).then_inc(stored, 16)
                if g:
                    collect_inverses(g)

            steps_of(sp, body)
            hold(stored, 16 * NS)

        @block.tensor
        def _(pe):
            def x_turn(f):
                m = f[0]
                pe.wait_ge(xn_ready, m + 1)
                wait(pe, vtok_ready, m)
                for q in range(KC):
                    for s in range(2):
                        last = pe.transpose(fr[:, 0, (2 * q + s) * P:(2 * q + s + 1) * P],
                                            xn[:, s, q * P:(q + 1) * P], ident[:])
                last.then_inc(xT_done, 1)

            def project(out, w, col, start):
                for k, (a, b) in enumerate(TERMS):
                    for q in range(KC):
                        last = pe.matmul(out, w[:, a, q, col], (xhi, xlo)[b][:, q, :], skip_group_check=True,
                                         start=(start and k == 0 and q == 0), stop=(k == 2 and q == KC - 1))
                return last

            def qkv(f, j):
                m = f[0]
                if j == 0:
                    pe.wait_ge(xhi_ready, m + 1)
                    pe.wait_ge(xlo_ready, m + 1)
                    wait(pe, sq_ready, m)
                    wait(pe, ktok_ready, m)
                if j == 2:
                    pe.wait_ge(bth_ready, m + 1)
                for r in range(PR):
                    last = project(fr[:, (2, 0, 1)[j], r * 2 * P:(r + 1) * 2 * P],
                                   wqkv[:, :, :, j, :], slice(r * P, (r + 1) * P), r == 0)
                last.then_inc(qkv_done, 1)

            def beta_rows(f):
                m = f[0]
                project(fr[0:H, 1, 0:2 * P], wbs, slice(0, H), True).then_inc(beta_done, 1)

            def beta_turn(f):
                m = f[0]
                pe.wait_ge(bth_ready, m + 1)
                pe.wait_ge(raw_ready, 3 * m + 2)
                pass_by(pe, passed)
                for s in range(2):
                    last = pe.transpose(fr[:, 0, s * H:(s + 1) * H], bth[:, s * P:(s + 1) * P], ident[0:H, 0:H])
                last.then_inc(bT_done, 1)

            def turn_back(f):
                m, par, _ = f
                pe.wait_ge(silu_ready, 3 * (m + 1))
                pe.wait_ge(raw_ready, 3 * (m + 1))
                for s in range(2):
                    for j in range(2):
                        for r in range(PR):
                            last = pe.transpose(fr[:, 1 + s, (2 * j + r) * P:(2 * j + r + 1) * P],
                                                kq[:, par, r, s, j, :], ident[:])
                last.then_inc(turned, 1)
                pe.wait_ge(beta_ready, m + 1)
                for s in range(2):
                    for r in range(PR):
                        last = pe.transpose(fr[:, 0, (2 * s + r) * P:(2 * s + r + 1) * P], vch[:, r, s, :], ident[:])
                last.then_inc(turned, 1)

            def gram(g, q):
                m, par, _ = g
                if q == 0:
                    pe.wait_ge(kx_ready, 2 * (m + 1))
                for s in range(2):
                    wait(pe, gram_read[s], PR * m + q)
                    if q == 0:
                        wait(pe, prod_read[s], NP * (m - 1))
                    for h in range(2):
                        last = pe.matmul(tp[:, s, h * 2 * P:(h + 1) * 2 * P], kx[:, q, s, h, :],
                                         kq[:, par, q, s], start=(h == 0), stop=True, skip_group_check=True)
                    last.then_inc(gram_done[s], 1)

            def product(t, q):
                m, par, _ = t
                if q == 0:
                    pe.wait_ge(tb_ready, 16 * NBK * (m + 1))
                edge, kind = PRODUCTS[q]
                for s in range(2):
                    wait(pe, prod_read[s], NP * m + q)
                    if kind == "TX":
                        pass_by(pe, passed)
                        for h in range(H):
                            pe.transpose(tp[0:64, s, h * 64:(h + 1) * 64], tu[0:64, s, h, 0:64], ident[0:64, 0:64])
                    if q == 0:
                        pe.wait_ge(gram_read[s], min(PR * (m + 2), PR * NS) if isinstance(m, int) else PR * (m + 2))
                    for h in range(H):
                        n, half = nn[:, par % 2, s, h, :], slice(P // 2, P)
                        out = tp[:, s, h * P:(h + 1) * P]
                        if (edge, kind) == (16, "T"):
                            last = pe.transpose(out, tu[:, s, h, :], ident[:])
                            continue
                        if edge == 16:
                            a, b = {"X": (n, tb[:, 1, s, h, :]), "U": (tb[:, 0, s, h, :], xt[:, s, h, :])}[kind]
                        elif edge == 32:
                            a, b = {"X": (n, tu[:, s, h, :]), "U": (tt[:, s, h, :], x32[:, s, h, :])}[kind]
                        else:
                            a, b = (tt[:, s, h, 0:64], x64[:, s, h, :]) if kind == "U" else (n[:, 0:64], tu[:, s, h, half])
                        if edge == 64:
                            b0 = (2 * P if kind == "TX" else 0) + h * 64
                            out = tp[0:64, s, b0:b0 + 64]
                        last = pe.matmul(out, a, b, start=(h == 0), stop=True, skip_group_check=True)
                    last.then_inc(prod_done[s], 1)

            def state_in(st):
                m, par, _ = st
                for s in range(2):
                    pe.wait_ge(s_ready[s], m + 1)
                    for r in range(PR):
                        last = pe.matmul(sc[:, s, r * P:(r + 1) * P], kq[:, par, r, s, 0, :], state[:, s, r, :],
                                         start=(r == 0), stop=True, skip_group_check=True)
                    last.then_inc(ks_done[s], 1)

            def out_in(st):
                m, par, _ = st
                wait(pe, y_read, m)
                for s in range(2):
                    for r in range(PR):
                        pe.matmul(ob[:, s * DM + r * P:s * DM + (r + 1) * P], kq[:, par, r, s, 1, :],
                                  state[:, s, r, :], start=(s == 0 and r == 0), stop=False, skip_group_check=True)

            def mids(st):
                m, par, _ = st
                for s in range(2):
                    pe.wait_ge(r_ready[s], m + 1)
                    pe.wait_ge(prod_read[s], NP * (m + 1))
                    for h in range(H):
                        r = h // 2
                        last = pe.matmul(sc[:, s, h * P:(h + 1) * P], tc[:, s, h, :], vn[:, par, s, r * P:(r + 1) * P],
                                         start=(h == 0), stop=True, skip_group_check=True)
                    last.then_inc(mid_done[s], 1)

            def state_out(st):
                m, par, _ = st
                for s in range(2):
                    pe.wait_ge(mid_ready[s], m + 1)
                    mm = mid[:, s].rearrange("p h (g d) -> p (h g) d", d=D)
                    for r in range(PR):
                        last = pe.matmul(sc[:, s, r * P:(r + 1) * P], ktok[:, par, s, r * P:(r + 1) * P],
                                         mm[:, 4 * r:4 * r + 4:3, :], start=(r == 0), stop=True,
                                         skip_group_check=True)
                    last.then_inc(ds_done[s], 1)

            def outputs(st):
                m, par, _ = st
                for s in range(2):
                    pe.wait_ge(mid_ready[s], m + 1)
                    for h in range(H):
                        r = h // 2
                        last = pe.matmul(ob[:, s * DM + r * P:s * DM + (r + 1) * P], at[:, par, s, h, :],
                                         mid[:, s, h, :], start=False, stop=(h % 2 == 1), skip_group_check=True)
                last.then_inc(o_done, 1)

            def out_turn(st):
                m = st[0]
                pe.wait_ge(on_ready, m + 1)
                for r in range(PR):
                    for s in range(2):
                        last = pe.transpose(ob[:, (2 * r + s) * P:(2 * r + s + 1) * P],
                                            on[:, s, r * P:(r + 1) * P], ident[:])
                last.then_inc(oT_done, 1)

            def out_project(st):
                m = st[0]
                pe.wait_ge(othi_ready, m + 1)
                pe.wait_ge(otlo_ready, m + 1)
                for s in range(2):
                    for k, (a, b) in enumerate(TERMS):
                        for r in range(PR):
                            last = pe.matmul(ob[:, s * DM:(s + 1) * DM], (othi, otlo)[b][:, r, s, :], wos[:, a, r, :],
                                             start=(s == 0 and k == 0 and r == 0), stop=(k == 2 and r == PR - 1),
                                             skip_group_check=True)
                last.then_inc(y_done, 1)


            def body(f, g, t, s):
                for q in range(NQ):
                    if s and q == 0:
                        state_in(s)
                    if g and q == 0 and isinstance(g[0], int) and g[0] == 0:
                        pe.wait_ge(masks, 1)
                        pe.wait_ge(zeroed, 5)
                    if g and q < PR:
                        gram(g, q)
                    if f:
                        if q == 0:
                            x_turn(f)
                        if q == 2:
                            qkv(f, 1)
                        if q == 8:
                            turn_back(f)
                    if t and q >= T0:
                        product(t, q - T0)
                    if s:
                        if q == 0:
                            out_in(s)
                        if q == 1:
                            mids(s)
                        if q == 3:
                            outputs(s)
                        if q == 5:
                            state_out(s)
                        if q == 6:
                            out_turn(s)
                        if q == 7:
                            out_project(s)
                    if f:
                        if q == 1:
                            qkv(f, 0)
                            beta_rows(f)
                        if q == 4:
                            qkv(f, 2)
                        if q == 6:
                            beta_turn(f)

            steps_of(pe, body)

        @block.vector
        def _(dve):
            def norm_stats(f):
                m, par, turn = f
                if isinstance(m, int) and m < 2:
                    dve.wait_ge(kept.attn_x, 16 * (m + 1))
                else:
                    dve.wait_ge(x_loaded[par % 2], 16 * turn)
                wait(dve, xn_ready, m)
                for s in range(2):
                    dve.bn_stats(stats[:, s, :], xin[:, par % 2, s, :]).then_inc(stats_part, 1)
                dve.wait_ge(stats_part, 2 * (m + 1))
                pass_by(dve, passed)
                for s in range(2):
                    last = dve.bn_aggr(mv[:, s, :], stats[:, s, :])
                last.then_inc(stats_ready, 1)

            def norm_in(f):
                m, par, turn = f
                dve.wait_ge(rstd_ready, m + 1)
                wait(dve, xT_done, m)
                for s in range(2):
                    last = dve.tensor_scalar(xn[:, s, :], xin[:, par % 2, s, :], mv[:, s, 0:1], rstd[:, s:s + 1],
                                             ALU.subtract, ALU.mult)
                last.then_inc(xn_ready, 1)

            def x_low(f):
                m = f[0]
                dve.wait_ge(xhi_ready, m + 1)
                dve.tensor_tensor(xlo[:].rearrange("p c t -> p (c t)"), fr[:, 0, :],
                                  xhi[:].rearrange("p c t -> p (c t)").bitcast(F32), ALU.subtract).then_inc(xlo_ready, 1)

            def history(f):
                m = f[0]
                wait(dve, conv_step, 18 * m)
                rv = raw[:].rearrange("p j r s t -> p (j r s) t")
                dve.tensor_copy(rv[:, :, 0:KW - 1], rv[:, :, P:P + KW - 1]).then_inc(hist_ready, 1)

            def conv(f, j, *at_taps):
                m = f[0]
                for tap in at_taps:
                    for r in range(PR):
                        n = 6 * j + 2 * (tap - 1) + r
                        if tap == 1:
                            dve.wait_ge(tap0_ready, 6 * m + 2 * j + r + 1)
                        else:
                            dve.wait_ge(conv_step, 18 * m + n - 1)
                        dve.scalar_tensor_tensor(acc[:, j, r], raw[:, j, r, :, tap:tap + P],
                                                 taps[:, j, r, tap:tap + 1], acc[:, j, r], ALU.mult, ALU.add)\
                           .then_inc(conv_step, 1)

            def betas(f):
                m = f[0]
                dve.wait_ge(bT_done, m + 1)
                wait(dve, cc_ready, m)
                dve.tensor_scalar(beta[:].rearrange("p s h -> p (s h)"), fr[:, 0, 0:2 * H], 0.5, 0.5, ALU.mult,
                                  ALU.add).then_inc(beta_ready, 1)

            def norms(f):
                m, par, _ = f
                dve.wait_ge(sq_ready, m + 1)
                wait(dve, og_ready, m - 3)
                wait(dve, cc_ready, m)
                dve.tensor_reduce(ss[:, par].rearrange("p s j h -> p (s j h)"),
                                  sq.rearrange("p s j (h d) -> p (s j h) d", d=D), AX.X, ALU.add).then_inc(ss_ready, 1)
                dve.wait_ge(ss_ready, m + 1)
                dve.reciprocal(rk[:], ss[:, par, :, 0, :]).then_inc(rk_ready, 1)
                dve.wait_ge(rk_ready, m + 1)
                dve.wait_ge(beta_ready, m + 1)
                dve.tensor_tensor(cc[:, par], beta[:], rk[:], ALU.mult).then_inc(cc_ready, 1)

            def gram_out(g, q):
                m, par, _ = g
                for s in range(2):
                    dve.wait_ge(gram_done[s], PR * m + q + 1)
                    if q == 0:
                        dve.wait_ge(cc_ready, m + 1)
                    v = tp[:, s, :].rearrange("p (h j t) -> p h j t", h=2, j=2)
                    for h in range(2):
                        dve.scalar_tensor_tensor(nn[:, par % 2, s, 2 * q + h, :], v[:, h, 0, :],
                                                 cc[:, par, s, 2 * q + h:2 * q + h + 1], below[:],
                                                 ALU.mult, ALU.mult)
                    dve.tensor_tensor(at[:, par, s, 2 * q:2 * q + 2, :], v[:, :, 1, :],
                                      upto[:].unsqueeze(1).broadcast_to([P, 2, P]), ALU.mult)\
                       .then_inc(gram_read[s], 1)

            def product_out(t, q):
                m, par, _ = t
                edge, kind = PRODUCTS[q]
                for s in range(2):
                    prod = tp[:, s, :].rearrange("p (h t) -> p h t", t=P)
                    if edge == 32 or (edge, kind) in ((16, "T"), (64, "TX")):
                        continue
                    if (edge, kind) == (64, "U"):
                        dve.wait_ge(tc_part, 2 * m + s + 1)
                        dve.wait_ge(prod_done[s], NP * m + q + 1)
                        half = slice(0, P // 2)
                        dve.scalar_tensor_tensor(tc[half, s, :, P // 2:],
                                                 tp[half, s, 0:2 * P].rearrange("p (h t) -> p h t", h=H), -1.0,
                                                 cc[half, par, s, :].unsqueeze(2).broadcast_to([P // 2, H, P // 2]),
                                                 ALU.mult, ALU.mult).then_inc(prod_read[s], 1)
                        continue
                    dve.wait_ge(prod_done[s], NP * m + q + 1)
                    if kind == "X":
                        dve.tensor_tensor(xt[:, s], prod, quarter[:].unsqueeze(1).broadcast_to([P, H, P]), ALU.mult)\
                           .then_inc(prod_read[s], 1)
                    else:
                        dve.tensor_tensor(tu[:, s], tb[:, 1, s], prod, ALU.subtract).then_inc(prod_read[s], 1)

            def scale_inverse(t):
                m, par, _ = t
                for s in range(2):
                    dve.wait_ge(prod_read[s], NP * m + 5)
                    wait(dve, mid_done[s], m)
                    dve.tensor_tensor(tc[:, s], tu[:, s], cc[:, par, s, :].unsqueeze(2).broadcast_to([P, H, P]),
                                      ALU.mult).then_inc(tc_part, 1)

            def remainder(st):
                m, par, _ = st
                for s in range(2):
                    dve.wait_ge(ks_done[s], m + 1)
                    dve.wait_ge(vn_ready, m + 1)
                    dve.tensor_tensor(vn[:, par, s, :], vn[:, par, s, :], sc[:, s, 0:DM], ALU.subtract)\
                       .then_inc(r_ready[s], 1)

            def state_add(st):
                m = st[0]
                for s in range(2):
                    dve.wait_ge(ds_done[s], m + 1)
                    d = sc[:, s, 0:DM].rearrange("p (r c) -> p r c", c=P)
                    for h in range(2):
                        a = slice(h * D, (h + 1) * D)
                        last = dve.tensor_tensor(state[a, s, :, a], state[a, s, :, a], d[a, :, a], ALU.add)
                    last.then_inc(s_ready[s], 1)

            def out_norm(st):
                m, par, _ = st
                dve.wait_ge(osq_ready, m + 1)
                wait(dve, ovar_part, 2 * m)
                dve.tensor_reduce(oms[:].rearrange("p s h -> p (s h)"),
                                  on[:].rearrange("p s (h d) -> p (s h) d", d=D), AX.X, ALU.add).then_inc(oms_ready, 1)

            def out_scale(st):
                m = st[0]
                dve.wait_ge(og_ready, m + 1)
                wait(dve, oT_done, m)
                dve.tensor_tensor(on[:].rearrange("p s (h d) -> p (s h) d", d=D),
                                  ob[:].rearrange("p (g d) -> p g d", d=D),
                                  og[:].rearrange("p s h -> p (s h)").unsqueeze(2).broadcast_to([P, 2 * H, D]),
                                  ALU.mult).then_inc(on_ready, 1)

            def out_low(st):
                m = st[0]
                dve.wait_ge(othi_ready, m + 1)
                dve.tensor_tensor(otlo[:].rearrange("p r s t -> p (r s t)"), ob[:],
                                  othi[:].rearrange("p r s t -> p (r s t)").bitcast(F32), ALU.subtract)\
                   .then_inc(otlo_ready, 1)

            def residual(st):
                m = st[0]
                dve.wait_ge(y_done, m + 1)
                dve.wait_ge(res_loaded, 16 * (m + 1))
                dve.tensor_tensor(xres[:].rearrange("p s d -> p (s d)"), ob[:], xres[:].rearrange("p s d -> p (s d)"),
                                  ALU.add).then_inc(y_read, 1)

            def clear_buffers():
                for s in range(2):
                    dve.memset(state[:, s], 0.0).then_inc(s_ready[s], 1)
                for buf in (mid, tb, x32, x64):
                    dve.memset(buf[:], 0.0).then_inc(zeroed, 1)

            norm_stats((0, 0, 0))
            norm_in((0, 0, 0))
            dve.memset(raw[:], 0.0).then_inc(zeroed, 1)
            dve.wait_ge(zeroed, 1)

            def body(f, g, t, s):
                more = f and not (isinstance(f[0], int) and f[0] + 1 >= NS)
                for q in range(NQ):
                    if s and q == 0:
                        remainder(s)
                    if g and q == 0 and isinstance(g[0], int) and g[0] == 0:
                        dve.wait_ge(masks, 1)
                    if g and q < PR:
                        gram_out(g, q)
                    if f and q == 0:
                        x_low(f)
                        history(f)
                        if isinstance(f[0], int) and f[0] == 0:
                            clear_buffers()
                    if s and q == 8:
                        residual(s)
                    if t and q >= T0:
                        product_out(t, q - T0)
                    if s:
                        if q == 4:
                            out_norm(s)
                        if q == 5:
                            state_add(s)
                            out_scale(s)
                        if q == 6:
                            out_low(s)
                    if f:
                        if q == 1:
                            conv(f, 0, 1)
                        if q == 2:
                            conv(f, 0, 2, 3)
                        if q == 3:
                            conv(f, 1, 1, 2)
                        if q == 4:
                            conv(f, 1, 3)
                        if q == 5:
                            conv(f, 2, 1, 2)
                        if q == 6:
                            conv(f, 2, 3)
                            betas(f)
                    if more and q == 4:
                        norm_stats(after(f))
                    if t and q == 7:
                        scale_inverse(t)
                    if more and q == 7:
                        norm_in(after(f))
                    if f and q == 8:
                        norms(f)

            steps_of(dve, body)

        @block.scalar
        def _(act):
            def x_high(f):
                m = f[0]
                act.wait_ge(xT_done, m + 1)
                wait(act, qkv_done, 3 * m)
                act.activation(xhi[:].rearrange("p c t -> p (c t)"), fr[:, 0, :], ACT.Copy).then_inc(xhi_ready, 1)

            def raw_out(f, j):
                m = f[0]
                act.wait_ge(qkv_done, 3 * m + j + 1)
                act.wait_ge(hist_ready, m + 1)
                act.activation(raw[:, j].rearrange("p r s t -> p (r s) t")[:, :, KW - 1:],
                               fr[:, (2, 0, 1)[j], :].rearrange("p (g t) -> p g t", t=P), ACT.Copy).then_inc(raw_ready, 1)

            def tap0(f, j):
                m = f[0]
                act.wait_ge(raw_ready, 3 * m + j + 1)
                wait(act, silu_ready, 3 * m)
                wait(act, kx_ready, 2 * m)
                wait(act, ss_ready, m)
                for r in range(PR):
                    act.activation(acc[:, j, r], raw[:, j, r, :, 0:P], ACT.Copy, scale=taps[:, j, r, 0:1])\
                       .then_inc(tap0_ready, 1)

            def beta_tanh(f):
                m = f[0]
                act.wait_ge(beta_done, m + 1)
                wait(act, bT_done, m)
                act.activation(bth[:], fr[0:H, 1, 0:2 * P], ACT.Tanh, scale=0.5).then_inc(bth_ready, 1)

            def silus(f, j):
                m, par, _ = f
                act.wait_ge(conv_step, 18 * m + 6 * (j + 1))
                if j == 0:
                    wait(act, o_done, m - 3)
                    wait(act, turned, 2 * m)
                out = (kq[:, par, :, :, 0, :], vch[:], kq[:, par, :, :, 1, :])[j]
                act.activation(out, acc[:, j], ACT.Silu).then_inc(silu_ready, 1)

            def lone_keys(f):
                m = f[0]
                act.wait_ge(masks, 1)
                for s in range(2):
                    wait(act, gram_done[s], PR * m)
                for h in range(2):
                    a = slice(h * D, (h + 1) * D)
                    act.activation(kx[a, :, :, h, :], acc[a, 0], ACT.Silu).then_inc(kx_ready, 1)

            def squares(f):
                m, par, _ = f
                act.wait_ge(turned, 2 * m + 1)
                act.wait_ge(kx_ready, 2 * (m + 1))
                act.activation(sq.rearrange("p s j d -> p s (j d)"), fr[:, 1:3, :], ACT.Square).then_inc(sq_ready, 1)
                wait(act, ds_done[1], m - 3)
                act.activation(ktok[:, par], fr[:, 1:3, 0:DM], ACT.Copy).then_inc(ktok_ready, 1)
                act.wait_ge(turned, 2 * (m + 1))
                wait(act, vn_ready, m)
                act.activation(vtok[:], fr[:, 0, :], ACT.Copy).then_inc(vtok_ready, 1)

            def product_out(t, q):
                m = t[0]
                edge, kind = PRODUCTS[q]
                w = P // 4
                for s in range(2):
                    act.wait_ge(prod_done[s], NP * m + q + 1)
                    if edge == 16:
                        last = act.activation(tt[:, s].rearrange("p h t -> p (h t)"), tp[:, s, :], ACT.Copy)
                    elif edge == 32:
                        prod = tp[:, s, :].rearrange("p (h t) -> p h t", t=P)
                        for b in range(2):
                            rows, cols = slice(2 * b * w, (2 * b + 1) * w), slice((2 * b + 1) * w, (2 * b + 2) * w)
                            last = act.activation((x32 if kind == "X" else tu)[rows, s, :, cols], prod[rows, :, cols],
                                                  ACT.Copy, scale=(1.0 if kind == "X" else -1.0))
                    else:
                        both = tp[0:2 * w, s, :].rearrange("p (k h t) -> p k h t", k=2, h=H)
                        act.activation(tt[0:2 * w, s, :, 0:2 * w], both[:, 0], ACT.Copy)
                        last = act.activation(x64[0:2 * w, s], both[:, 1], ACT.Copy)
                    last.then_inc(prod_read[s], 1)

            def mid_out(st):
                m = st[0]
                for s in range(2):
                    act.wait_ge(mid_done[s], m + 1)
                    mm = mid[:, s].rearrange("p h (g d) -> p (h g) d", d=D).rearrange("p (r g) d -> p r g d", r=PR)
                    pp = sc[:, s, :].rearrange("p (r g d) -> p r g d", r=PR, d=D)
                    act.activation(mm[:, :, 0:4:3, :], pp[:, :, 0:4:3, :], ACT.Copy).then_inc(mid_ready[s], 1)

            def out_squares(st):
                m = st[0]
                act.wait_ge(o_done, m + 1)
                wait(act, oT_done, m)
                act.activation(on[:].rearrange("p s d -> p (s d)"), ob[:], ACT.Square).then_inc(osq_ready, 1)

            def out_high(st):
                m = st[0]
                act.wait_ge(oT_done, m + 1)
                wait(act, y_done, m)
                act.activation(othi[:].rearrange("p r s t -> p (r s t)"), ob[:], ACT.Copy).then_inc(othi_ready, 1)

            def body(f, g, t, s):
                for q in range(NQ):
                    if f and q == 0:
                        x_high(f)
                    if s:
                        if q == 1:
                            mid_out(s)
                    if t and q - T0 in (2, 3, 4, 5):
                        product_out(t, q - T0)
                    if s:
                        if q == 3:
                            out_squares(s)
                        if q == 6:
                            out_high(s)
                    if f:
                        if q == 1:
                            raw_out(f, 0)
                            beta_tanh(f)
                            tap0(f, 0)
                        if q == 2:
                            raw_out(f, 1)
                            tap0(f, 1)
                        if q == 4:
                            raw_out(f, 2)
                            tap0(f, 2)
                        if q == 5:
                            silus(f, 0)
                        if q == 7:
                            silus(f, 1)
                            silus(f, 2)
                            lone_keys(f)
                        if q == 8:
                            squares(f)

            steps_of(act, body)

        @block.gpsimd
        def _(pool):
            count = [0]

            def link(ins):
                count[0] += 1
                ins.then_inc(mask_step, 1)
                pool.wait_ge(mask_step, count[0])

            def select(view, pattern, base, mult, op=ALU.is_ge, fill=0.0):
                link(pool.affine_select(out=view, in_=view, compare_op=op, fill=fill, base=base, pattern=pattern,
                                        channel_multiplier=mult))

            def inverse_std(m):
                pool.wait_ge(stats_ready, m + 1)
                wait(pool, xn_ready, m)
                pass_by(pool, passed)
                pool.tensor_scalar(var_eps[:], mv[:, :, 1], EPS, None, ALU.add).then_inc(rstd_part, 1)
                pool.wait_ge(rstd_part, m + 1)
                pool.tensor_tensor(rstd[:], var_eps[:], powers[:, 1, 0:2], ALU.pow).then_inc(rstd_ready, 1)

            link(pool.memset(powers[:, 0, :], 0.5))
            link(pool.memset(powers[:, 1, :], -0.5))
            inverse_std(0)
            link(pool.memset(below[:], 1.0))
            select(below[:], [[-1, P]], -1, 1)
            link(pool.memset(upto[:], 1.0))
            select(upto[:], [[1, P]], 0, -1)
            v = quarter[:].rearrange("p (b h t) -> p b h t", h=2, t=SB)
            link(pool.memset(v[:, :, 0:1, :], 0.0))
            link(pool.memset(v[:, :, 1:2, :], 1.0))
            v = quarter[:].rearrange("p (b t) -> p b t", t=2 * SB)
            select(v, [[-2 * SB, P // (2 * SB)], [0, 2 * SB]], 0, 1)
            select(v, [[2 * SB, P // (2 * SB)], [0, 2 * SB]], SB - 1, -1)
            link(pool.memset(eye[:], 0.0))
            link(pool.affine_select(out=eye[:], in_=eye[:], compare_op=ALU.not_equal, fill=1.0, base=0,
                                    pattern=[[-1, SB], [1, SB]], channel_multiplier=0))
            pool.memset(kx[:], 0.0).then_inc(masks, 1)
            pool.wait_ge(masks, 1)

            def key_norms(f):
                m, par, _ = f
                pool.wait_ge(ss_ready, m + 1)
                wait(pool, vn_ready, m)
                pool.tensor_tensor(kn[:], ss[:, par, :, 0, :], powers[:, 0, :].rearrange("p (s h) -> p s h", s=2),
                                   ALU.pow).then_inc(kn_ready, 1)

            def invert_blocks(g, first, end):
                m = g[0]
                n, v = small, inv[:, 0]
                if first == 1:
                    pool.wait_ge(blocks_in, 16 * (m + 1))
                    wait(pool, inv_out, 32 * m)
                    pool.tensor_tensor(v, eye[:], n[:], ALU.subtract).then_inc(solve_step, 1)
                for j in range(first, end):
                    k = SB - 1 - j
                    pool.wait_ge(solve_step, SOLVE * m + 2 * j - 1)
                    pool.tensor_tensor(term[:, 0:k, 0:j], n[:, j + 1:, j:j + 1].broadcast_to([BP, k, j]),
                                       v[:, j:j + 1, 0:j].broadcast_to([BP, k, j]), ALU.mult).then_inc(solve_step, 1)
                    pool.wait_ge(solve_step, SOLVE * m + 2 * j)
                    pool.tensor_tensor(v[:, j + 1:, 0:j], v[:, j + 1:, 0:j], term[:, 0:k, 0:j], ALU.subtract)\
                        .then_inc(solve_step, 1)
                if end < SB - 1:
                    return
                pool.wait_ge(solve_step, SOLVE * (m + 1) - 1)
                pass_by(pool, passed)
                pool.tensor_copy(inv[:, 1], v.rearrange("p r c -> p c r")).then_inc(solve_step, 1)

            def values(f):
                m, par, _ = f
                pool.wait_ge(kn_ready, m + 1)
                pool.wait_ge(vtok_ready, m + 1)
                for s in range(2):
                    wait(pool, mid_done[s], m - 3)
                pool.tensor_tensor(vn[:, par].rearrange("p s (h d) -> p (s h) d", d=D),
                                   vtok[:].rearrange("p (g d) -> p g d", d=D),
                                   kn[:].rearrange("p s h -> p (s h)").unsqueeze(2).broadcast_to([P, 2 * H, D]),
                                   ALU.mult).then_inc(vn_ready, 1)

            def out_factor(st):
                m, par, _ = st
                pool.wait_ge(oms_ready, m + 1)
                wait(pool, og_ready, m)
                pass_by(pool, passed)
                pool.tensor_scalar(ovar[:], oms[:], 1.0 / D, None, ALU.mult).then_inc(ovar_part, 1)
                pool.tensor_scalar(oeps[:], ss[:, par, :, 1, :], D * EPS, None, ALU.mult).then_inc(ovar_part, 1)
                pool.wait_ge(ovar_part, 2 * m + 2)
                pool.tensor_tensor(osum[:], ovar[:], oeps[:], ALU.add).then_inc(osum_ready, 1)
                pool.wait_ge(osum_ready, m + 1)
                wait(pool, on_ready, m)
                pool.tensor_tensor(og[:], osum[:], powers[:, 1, :].rearrange("p (s h) -> p s h", s=2),
                                   ALU.pow).then_inc(og_ready, 1)

            def body(f, g, t, s):
                if g:
                    invert_blocks(g, 1, SB // 2 - 2)
                if s:
                    out_factor(s)
                if f and not (isinstance(f[0], int) and f[0] + 1 >= NS):
                    inverse_std(f[0] + 1)
                if g:
                    invert_blocks(g, SB // 2 - 2, SB - 1)
                if f:
                    key_norms(f)
                    values(f)

            steps_of(pool, body)


def build(nc, x, wq, wk, wv, wb, cq, ck, cv, rms_w, wo, gate_w, w1, w2, w3, out):
    def dram(n, shape):
        return nc.dram_tensor(n, shape, F32, kind="Internal").ap()

    x1, x2 = dram("x_after_first", [B * L, DM]), dram("x_after_attention", [B * L, DM])
    s1, s2 = dram("scales_first", [E, TB]), dram("scales_second", [E, TB])
    n_dram, t_dram = dram("small_blocks", [8, 8, 16, 16]), dram("small_inverses", [8, 2, 8, 16, 16])
    fresh = Fresh(wq, wk, wv, wb, cq, ck, cv, rms_w, wo, gate_w, w1, w2, w3)
    with ExitStack() as ctx:
        kept = Kept(ctx, nc)
        ffn(nc, "ffn1", x.rearrange("b l d -> (b l) d"), x1, s1, kept, fresh)
        attention(nc, "attn", x1, x2, n_dram, t_dram, kept)
        ffn(nc, "ffn2", x2, out.rearrange("b l d -> (b l) d"), s2, kept)


_INS = ["L0_attn_x", "L0_attn_Wq", "L0_attn_Wk", "L0_attn_Wv", "L0_attn_Wb", "L0_attn_conv_q_w", "L0_attn_conv_k_w",
        "L0_attn_conv_v_w", "L0_attn_rms_w", "L0_attn_Wo", "L0_ffn_gate_w", "L0_ffn_w1", "L0_ffn_w2", "L0_ffn_w3"]
_OUTS = [((B, L, DM), "float32")]


def kernel(**inputs):
    import numpy as _np
    import concourse.bacc as _bacc
    from concourse import mybir as _mybir
    from concourse.bass_utils import run_bass_kernel_spmd as _run

    nc = _bacc.Bacc("TRN2", target_bir_lowering=False, num_devices=1)
    arrays, args = {}, []
    for name in _INS:
        a = _np.ascontiguousarray(inputs[name])
        arrays[f"in_{name}_dram"] = a
        args.append(nc.dram_tensor(f"in_{name}_dram", a.shape, _mybir.dt.from_np(a.dtype), kind="ExternalInput").ap())
    for i, (shape, dtype) in enumerate(_OUTS):
        dt = _mybir.dt.from_np(_np.dtype(dtype))
        args.append(nc.dram_tensor(f"out_{i}_dram", shape, dt, kind="ExternalOutput").ap())
    build(nc, *args)
    r = _run(nc, [arrays], core_ids=[0])
    return r.results[0]["out_0_dram"]
```
